# Optimizing a Trainium2 kernel written in Bass

```python
import numpy as np
import jax
import jax.numpy as jnp

def _softmax(x, axis=-1):
    return jax.nn.softmax(x, axis=axis)

def _gelu(x):
    return jax.nn.gelu(x, approximate=True)

def _silu(x):
    return jax.nn.silu(x)

def _sigmoid(x):
    return jax.nn.sigmoid(x)

def _layernorm(x, axis=-1, eps=1e-05):
    m = jnp.mean(x, axis=axis, keepdims=True)
    v = jnp.var(x, axis=axis, keepdims=True)
    return (x - m) / jnp.sqrt(v + eps)

def _scatter_add(tgt, idx, src, axis=0):
    return tgt.at[idx].add(src)

def _segment_sum(src, seg, n):
    return jax.ops.segment_sum(src, seg, n)
kernel_name = 'mk_seq_postln_d2_jaxref_r8_7d7fcf'

def setup_inputs(seed: int=0):
    np.random.seed(seed)
    _w = jnp.asarray

    def _L0_attn_setup():
        import jax, jax.numpy as jnp
        import numpy as np
        D_MODEL = 128
        NHEAD = 16
        HEAD_DIM = D_MODEL // NHEAD
        MAX_POS = 256

        def _rope_tables(seq_len, dim):
            inv_freq = 1.0 / 10000.0 ** (jnp.arange(0, dim, 2, dtype=jnp.float32) / dim)
            t = jnp.arange(seq_len, dtype=jnp.float32)[:, None]
            freqs = t * inv_freq[None, :]
            emb = jnp.concatenate([freqs, freqs], axis=-1)
            return (jnp.cos(emb), jnp.sin(emb))

        def _rotate_half(x):
            x1, x2 = jnp.split(x, 2, axis=-1)
            return jnp.concatenate([-x2, x1], axis=-1)

        def _apply_rope(x, cos, sin):
            c = cos[None, :, None, :]
            s = sin[None, :, None, :]
            return x * c + _rotate_half(x) * s
        key = jax.random.key(seed)
        ks = jax.random.split(key, 9)
        B, L, D = (4, 256, D_MODEL)
        lim = 1.0 / np.sqrt(D)

        def lin(k):
            kw, kb = jax.random.split(k)
            W = jax.random.uniform(kw, (D, D), jnp.float32, -lim, lim)
            b = jax.random.uniform(kb, (D,), jnp.float32, -lim, lim)
            return (W, b)
        Wq, bq = lin(ks[0])
        Wk, bk = lin(ks[1])
        Wv, bv = lin(ks[2])
        Wo, bo = lin(ks[3])
        x = jax.random.normal(ks[4], (B, L, D), jnp.float32)
        return {'x': x, 'Wq': Wq, 'bq': bq, 'Wk': Wk, 'bk': bk, 'Wv': Wv, 'bv': bv, 'Wo': Wo, 'bo': bo}
    _L0_attn_in = _L0_attn_setup()

    def _L0_ffn_setup():
        import jax, jax.numpy as jnp
        import numpy as np
        CAPACITY_FACTOR = 1.0
        key = jax.random.key(seed)
        ks = jax.random.split(key, 5)
        B, S, D, E, F = (2, 256, 128, 8, 512)
        x = jax.random.normal(ks[0], (B, S, D), dtype=jnp.float32)
        Ws = jax.random.normal(ks[1], (D, E), dtype=jnp.float32) * (1.0 / np.sqrt(D))
        bs = jnp.zeros((E,), dtype=jnp.float32)
        W1 = jax.random.normal(ks[2], (E, D, F), dtype=jnp.float32) * (1.0 / np.sqrt(D))
        b1 = jnp.zeros((E, F), dtype=jnp.float32)
        W2 = jax.random.normal(ks[3], (E, F, D), dtype=jnp.float32) * (1.0 / np.sqrt(F))
        b2 = jnp.zeros((E, D), dtype=jnp.float32)
        return {'x': x, 'Ws': Ws, 'bs': bs, 'W1': W1, 'b1': b1, 'W2': W2, 'b2': b2}
    _L0_ffn_in = _L0_ffn_setup()

    def _L1_attn_setup():
        import jax, jax.numpy as jnp
        import numpy as np
        DIM = 128
        HEADS = 16
        DIM_HEAD = DIM // HEADS
        LATENT = DIM // 4
        SCALE = DIM_HEAD ** (-0.5)
        key = jax.random.key(seed)
        ks = jax.random.split(key, 8)
        B, S = (2, 256)
        init = lambda k, shape, fan_in: jax.random.normal(k, shape, jnp.float32) * fan_in ** (-0.5)
        return {'x': jax.random.normal(ks[0], (B, S, DIM), jnp.float32), 'Wq': init(ks[1], (DIM, DIM), DIM), 'bq': jnp.zeros((DIM,), jnp.float32), 'Wl': init(ks[2], (DIM, LATENT), DIM), 'bl': jnp.zeros((LATENT,), jnp.float32), 'Wk': init(ks[3], (LATENT, DIM), LATENT), 'bk': jnp.zeros((DIM,), jnp.float32), 'Wv': init(ks[4], (LATENT, DIM), LATENT), 'bv': jnp.zeros((DIM,), jnp.float32), 'Wo': init(ks[5], (DIM, DIM), DIM), 'bo': jnp.zeros((DIM,), jnp.float32)}
    _L1_attn_in = _L1_attn_setup()

    def _L1_ffn_setup():
        import jax, jax.numpy as jnp
        import numpy as np
        B, L, D = (4, 64, 128)
        E, TOP_K = (16, 4)
        F = 4 * D
        key = jax.random.key(seed)
        ks = jax.random.split(key, 6)
        scale = 0.02
        return {'x': jax.random.normal(ks[0], (B, L, D), jnp.float32), 'keys': jax.random.normal(ks[1], (E, D), jnp.float32), 'w1': jax.random.normal(ks[2], (E, F, D), jnp.float32) * scale, 'b1': jnp.zeros((E, F), jnp.float32), 'w2': jax.random.normal(ks[3], (E, D, F), jnp.float32) * scale, 'b2': jnp.zeros((E, D), jnp.float32), 'rw': jax.random.normal(ks[4], (E, D), jnp.float32) * scale, 'rb': jnp.zeros((E,), jnp.float32)}
    _L1_ffn_in = _L1_ffn_setup()
    _d = {'L0_attn_x': _L0_attn_in['x'], 'L0_attn_Wq': _L0_attn_in['Wq'], 'L0_attn_bq': _L0_attn_in['bq'], 'L0_attn_Wk': _L0_attn_in['Wk'], 'L0_attn_bk': _L0_attn_in['bk'], 'L0_attn_Wv': _L0_attn_in['Wv'], 'L0_attn_bv': _L0_attn_in['bv'], 'L0_attn_Wo': _L0_attn_in['Wo'], 'L0_attn_bo': _L0_attn_in['bo'], 'L0_ffn_Ws': _L0_ffn_in['Ws'], 'L0_ffn_bs': _L0_ffn_in['bs'], 'L0_ffn_W1': _L0_ffn_in['W1'], 'L0_ffn_b1': _L0_ffn_in['b1'], 'L0_ffn_W2': _L0_ffn_in['W2'], 'L0_ffn_b2': _L0_ffn_in['b2'], 'L1_attn_Wq': _L1_attn_in['Wq'], 'L1_attn_bq': _L1_attn_in['bq'], 'L1_attn_Wl': _L1_attn_in['Wl'], 'L1_attn_bl': _L1_attn_in['bl'], 'L1_attn_Wk': _L1_attn_in['Wk'], 'L1_attn_bk': _L1_attn_in['bk'], 'L1_attn_Wv': _L1_attn_in['Wv'], 'L1_attn_bv': _L1_attn_in['bv'], 'L1_attn_Wo': _L1_attn_in['Wo'], 'L1_attn_bo': _L1_attn_in['bo'], 'L1_ffn_keys': _L1_ffn_in['keys'], 'L1_ffn_w1': _L1_ffn_in['w1'], 'L1_ffn_b1': _L1_ffn_in['b1'], 'L1_ffn_w2': _L1_ffn_in['w2'], 'L1_ffn_b2': _L1_ffn_in['b2'], 'L1_ffn_rw': _L1_ffn_in['rw'], 'L1_ffn_rb': _L1_ffn_in['rb']}
    _x0 = _d['L0_attn_x']
    _d['L0_attn_x'] = jax.random.normal(jax.random.fold_in(jax.random.key(seed), 1), (8, 256, 128), dtype=_x0.dtype)
    del _x0
    return _d

def reference(L0_attn_x, L0_attn_Wq, L0_attn_bq, L0_attn_Wk, L0_attn_bk, L0_attn_Wv, L0_attn_bv, L0_attn_Wo, L0_attn_bo, L0_ffn_Ws, L0_ffn_bs, L0_ffn_W1, L0_ffn_b1, L0_ffn_W2, L0_ffn_b2, L1_attn_Wq, L1_attn_bq, L1_attn_Wl, L1_attn_bl, L1_attn_Wk, L1_attn_bk, L1_attn_Wv, L1_attn_bv, L1_attn_Wo, L1_attn_bo, L1_ffn_keys, L1_ffn_w1, L1_ffn_b1, L1_ffn_w2, L1_ffn_b2, L1_ffn_rw, L1_ffn_rb):

    def _L0_attn_ref(x, Wq, bq, Wk, bk, Wv, bv, Wo, bo):
        import jax, jax.numpy as jnp
        import numpy as np
        D_MODEL = 128
        NHEAD = 16
        HEAD_DIM = D_MODEL // NHEAD
        MAX_POS = 256

        def _rope_tables(seq_len, dim):
            inv_freq = 1.0 / 10000.0 ** (jnp.arange(0, dim, 2, dtype=jnp.float32) / dim)
            t = jnp.arange(seq_len, dtype=jnp.float32)[:, None]
            freqs = t * inv_freq[None, :]
            emb = jnp.concatenate([freqs, freqs], axis=-1)
            return (jnp.cos(emb), jnp.sin(emb))

        def _rotate_half(x):
            x1, x2 = jnp.split(x, 2, axis=-1)
            return jnp.concatenate([-x2, x1], axis=-1)

        def _apply_rope(x, cos, sin):
            c = cos[None, :, None, :]
            s = sin[None, :, None, :]
            return x * c + _rotate_half(x) * s
        B, L, D = x.shape
        H, hd = (NHEAD, HEAD_DIM)
        q = (x @ Wq.T + bq).reshape(B, L, H, hd)
        k = (x @ Wk.T + bk).reshape(B, L, H, hd)
        v = (x @ Wv.T + bv).reshape(B, L, H, hd)
        cos, sin = _rope_tables(L, hd)
        q = _apply_rope(q, cos, sin)
        k = _apply_rope(k, cos, sin)
        scores = jnp.einsum('bqhd,bkhd->bhqk', q, k) / np.sqrt(hd).astype(np.float32)
        attn = jax.nn.softmax(scores, axis=-1)
        out = jnp.einsum('bhqk,bkhd->bqhd', attn, v).reshape(B, L, D)
        return out @ Wo.T + bo

    def _L0_ffn_ref(x, Ws, bs, W1, b1, W2, b2):
        import jax, jax.numpy as jnp
        import numpy as np
        CAPACITY_FACTOR = 1.0
        B, S, D = x.shape
        E = Ws.shape[1]
        N = B * S
        k = int(CAPACITY_FACTOR * N / E)
        xf = x.reshape(N, D)
        route_prob = jax.nn.softmax(xf @ Ws + bs, axis=-1).T
        route_vals, routes = jax.lax.top_k(route_prob, k)
        xin = xf[routes]
        h = jax.nn.gelu(jnp.einsum('ekd,edf->ekf', xin, W1) + b1[:, None, :])
        out = jnp.einsum('ekf,efd->ekd', h, W2) + b2[:, None, :]
        out = out * route_vals[..., None]
        final = jnp.zeros((N, D), dtype=x.dtype).at[routes.reshape(-1)].add(out.reshape(-1, D))
        return final.reshape(B, S, D)

    def _L1_attn_ref(x, Wq, bq, Wl, bl, Wk, bk, Wv, bv, Wo, bo):
        import jax, jax.numpy as jnp
        import numpy as np
        DIM = 128
        HEADS = 16
        DIM_HEAD = DIM // HEADS
        LATENT = DIM // 4
        SCALE = DIM_HEAD ** (-0.5)
        B, S, D = x.shape
        H, Dh = (HEADS, DIM_HEAD)
        q = (x @ Wq + bq).reshape(B, S, H, Dh)
        latent = x @ Wl + bl
        k = (latent @ Wk + bk).reshape(B, S, H, Dh)
        v = (latent @ Wv + bv).reshape(B, S, H, Dh)
        scores = jnp.einsum('bihd,bjhd->bhij', q, k) * SCALE
        attn = jax.nn.softmax(scores, axis=-1)
        out = jnp.einsum('bhij,bjhd->bihd', attn, v).reshape(B, S, D)
        out = out @ Wo + bo
        return out

    def _L1_ffn_ref(x, keys, w1, b1, w2, b2, rw, rb):
        import jax, jax.numpy as jnp
        import numpy as np
        B, L, D = (4, 64, 128)
        E, TOP_K = (16, 4)
        F = 4 * D
        diff = x[:, :, None, :] - keys
        dist2 = jnp.sum(diff * diff, axis=-1)
        logits = -dist2 + jnp.einsum('bld,ed->ble', x, rw) + rb
        topv, topi = jax.lax.top_k(logits, TOP_K)
        w = jax.nn.softmax(topv, axis=-1)
        hidden = jax.nn.gelu(jnp.einsum('bld,efd->blef', x, w1) + b1, approximate=False)
        exp_out = jnp.einsum('blef,edf->bled', hidden, w2) + b2
        sel = jnp.take_along_axis(exp_out, topi[..., None], axis=2)
        fused = jnp.sum(w[..., None] * sel, axis=2)
        return fused
    x = L0_attn_x
    x = _layernorm(x + _L0_attn_ref(x, L0_attn_Wq, L0_attn_bq, L0_attn_Wk, L0_attn_bk, L0_attn_Wv, L0_attn_bv, L0_attn_Wo, L0_attn_bo), axis=-1)
    x = _layernorm(x + _L0_ffn_ref(x, L0_ffn_Ws, L0_ffn_bs, L0_ffn_W1, L0_ffn_b1, L0_ffn_W2, L0_ffn_b2), axis=-1)
    x = _layernorm(x + _L1_attn_ref(x, L1_attn_Wq, L1_attn_bq, L1_attn_Wl, L1_attn_bl, L1_attn_Wk, L1_attn_bk, L1_attn_Wv, L1_attn_bv, L1_attn_Wo, L1_attn_bo), axis=-1)
    x = _layernorm(x + _L1_ffn_ref(x, L1_ffn_keys, L1_ffn_w1, L1_ffn_b1, L1_ffn_w2, L1_ffn_b2, L1_ffn_rw, L1_ffn_rb), axis=-1)
    return x

_drawn_inputs = setup_inputs


def setup_inputs(seed=0):
    import zlib

    import numpy as np

    out = dict(_drawn_inputs(seed))
    spreads = {'L0_ffn_bs': (0.0, 0.1),
     'L0_ffn_b1': (0.0, 0.294),
     'L0_ffn_b2': (0.0, 0.1),
     'L1_attn_bq': (0.0, 0.411),
     'L1_attn_bl': (0.0, 0.1),
     'L1_attn_bk': (0.0, 2.0),
     'L1_attn_bv': (0.0, 0.1),
     'L1_attn_bo': (0.0, 0.1),
     'L1_ffn_b1': (0.0, 0.347),
     'L1_ffn_b2': (0.0, 0.1),
     'L1_ffn_rb': (0.0, 2.0)}
    factors = {'L0_attn_Wq': 2.75,
     'L0_attn_bq': 8.0,
     'L0_attn_Wk': 2.672,
     'L0_attn_bk': 8.0,
     'L1_ffn_rw': 8.0}
    for name, (base, spread) in spreads.items():
        noise = np.random.default_rng([zlib.crc32(name.encode()), seed]).standard_normal(out[name].shape)
        drawn = base * np.exp(spread * noise) if base else spread * noise
        out[name] = jnp.asarray(drawn.astype(out[name].dtype))
    for name, factor in factors.items():
        out[name] = (out[name] * factor).astype(out[name].dtype)
    return out
```

```python
from contextlib import ExitStack

import numpy as np

import concourse.bass as bass
from concourse import mybir

F32 = mybir.dt.float32
F16 = mybir.dt.float16
BF16 = mybir.dt.bfloat16
I32 = mybir.dt.int32
ALU = mybir.AluOpType
ACT = mybir.ActivationFunctionType
AX = mybir.AxisListType

P = 128
TOK = 2048
NT = TOK // P
L = 256
NB = TOK // L
H = 16
HD = 8
HP = 32
NJ = H // 4
NROW = 3 * HD
MUNIT = 64.0
SCALE = float(np.float32(1.0) / np.sqrt(np.float32(HD)))
EPS = 1e-5
E0, E1 = 8, 16
F = 512
NF = F // P
CAP = TOK // E0
TOPK = 4
LAT = 32
CH = 512
NCH = TOK // CH
NBITS = 30


def soft_units(u):
    return {2: [0], 3: [1], 4: [2], 5: [3], 6: [4], 7: [5, 6], 8: [7], 9: [8], 10: [9], 11: [10, 11],
            12: [12], 13: [13], 14: [14], 15: [15]}.get(u, [])


def program(nc, d):
    ctx = ExitStack()
    with ctx:
        def sb(name, shape, dt=F32):
            return ctx.enter_context(nc.sbuf_tensor(name, shape, dt))

        def sem(name):
            return ctx.enter_context(nc.semaphore(name))

        ident = sb("ident", [P, P])
        ident_h = sb("ident_h", [P, P], F16)
        tri = sb("tri", [P, P], BF16)
        ones_b = sb("ones_b", [P, P], BF16)
        ones = sb("ones", [P, P])
        bits = sb("bits", [P, NBITS * E0], I32)
        ropec = sb("ropec", [P, 2, HD])
        ropes = sb("ropes", [P, 2, HD])
        wqkv0 = sb("wqkv0", [P, 3 * P])
        bqkv0 = sb("bqkv0", [1, 3 * P])
        wo = [sb("wo0", [P, P]), sb("wo1", [P, P])]
        bo = [sb("bo0", [1, P]), sb("bo1", [1, P])]
        wq1 = sb("wq1", [P, P])
        bq1 = sb("bq1", [1, P])
        wl1 = sb("wl1", [P, LAT])
        bl1 = sb("bl1", [LAT, 1])
        wkv1 = sb("wkv1", [LAT + 1, 2 * P])
        ws0 = sb("ws0", [P, E0])
        bs0 = sb("bs0", [1, E0])
        keysT = sb("keysT", [P, E1])
        rwT = sb("rwT", [P, E1])
        rb = sb("rb", [1, E1])
        wr1 = sb("wr1", [P, E1])
        ksq = sb("ksq", [P, E1])
        br1 = sb("br1", [1, E1])
        b1 = sb("b1", [P, 2, NF])
        b2 = [sb("b2_0", [E0, P]), sb("b2_1", [E1, P])]

        X = sb("X", [P, NT, P])
        XT = sb("XT", [P, TOK])
        Y = sb("Y", [P, NT, P])
        stats = sb("stats", [P, NT, 6])
        mv = sb("mv", [P, NT, 2])
        rstd = sb("rstd", [P, NT])
        nmr = sb("nmr", [P, NT])

        xr = sb("xr", [P, 2, L])
        latT = sb("latT", [LAT + 1, L])
        qk = sb("qk", [P, 2, 2 * P])
        vraw = sb("vraw", [P, 2, P])
        rt1 = sb("rt1", [P, 2, 2 * P])
        rt2 = sb("rt2", [P, 2, 2 * P])
        aug = [sb(f"aug{i}", [P, 2, 2 * H, HP], F16) for i in range(2)]
        vaug = [sb(f"vaug{i}", [P, 2, H, HP]) for i in range(2)]
        QT = [sb(f"QT{i}", [P, NJ, L], F16) for i in range(2)]
        KT = [sb(f"KT{i}", [P, NJ, L], F16) for i in range(2)]
        QT2 = sb("QT2", [P, NJ, L], F16)
        mx = sb("mx", [P, 2, H])
        mneg = sb("mneg", [P, 2, H])
        prob = sb("prob", [P, 8, 2, L])
        OT = sb("OT", [P, 2, 2, L])
        rden = sb("rden", [P, 2, 16])
        on = sb("on", [P, 2, H, HD])
        oxT = sb("oxT", [P, L])

        lg = sb("lg", [P, NT, E1])
        pr = sb("pr", [P, NT, E1])
        gate = sb("gate", [P, NT, E1])
        gtm = sb("gtm", [P, NT, E1])
        eqm = sb("eqm", [P, NT, E1])
        eqb = sb("eqb", [P, NT, E0], BF16)
        cum = [sb("cum0", [P, NT, E1]), sb("cum1", [P, NT, E1])]
        cumb = sb("cumb", [P, NT, E0], BF16)
        cmp_ = sb("cmp", [P, NT, E0])
        cnt = sb("cnt", [P, E1], BF16)
        col = sb("col", [P, NT])
        col2 = sb("col2", [P, NT])
        xsq = sb("xsq", [P, NT, P])
        xn2 = sb("xn2", [P, NT])
        top8 = sb("top8", [P, NT, 8])
        thr = sb("thr", [P, E0])
        cand = sb("cand", [P, E0])
        keep = sb("keep", [P, E0])
        need = sb("need", [P, E0])
        gateT = sb("gateT", [E1, TOK])

        w1 = sb("w1", [P, 2, F])
        w2 = sb("w2", [P, 2, NF, P])
        hid = sb("hid", [P, 2, NF, CH])

        bank = [ctx.enter_context(nc.psum_tensor(f"bank{i}", [P, 512], F32)) for i in range(8)]
        half = [b[:, :].bitcast(F16) for b in bank]
        S1B, STB, OTB, M5, M6, M7 = (0, 1), (2, 3), 4, 5, 6, 7

        consts_in = sem("consts_in")
        weights_in = sem("weights_in")
        x_in = sem("x_in")
        zeroed = sem("zeroed")
        xr_ready = sem("xr_ready")
        lat_done = sem("lat_done")
        lat_ready = sem("lat_ready")
        proj_done = sem("proj_done")
        qkv_ready = sem("qkv_ready")
        rope_step = sem("rope_step")
        split_step = sem("split_step")
        aug_ready = sem("aug_ready")
        vaug_ready = sem("vaug_ready")
        tq_done = sem("tq_done")
        tq_ready = sem("tq_ready")
        tk_done = sem("tk_done")
        tk_ready = sem("tk_ready")
        s1_done = sem("s1_done")
        s1_used = sem("s1_used")
        m_step = sem("m_step")
        m_ready = sem("m_ready")
        tq2_done = sem("tq2_done")
        tq2_ready = sem("tq2_ready")
        st_done = sem("st_done")
        exp_done = sem("exp_done")
        av_done = sem("av_done")
        ot_ready = sem("ot_ready")
        bt_done = sem("bt_done")
        rden_ready = sem("rden_ready")
        on_ready = sem("on_ready")
        ox_done = sem("ox_done")
        ox_ready = sem("ox_ready")
        pj_done = sem("pj_done")
        y_ready = sem("y_ready")
        stats_ready = sem("stats_ready")
        var_ready = sem("var_ready")
        std_ready = sem("std_ready")
        rstd_ready = sem("rstd_ready")
        xn_ready = sem("xn_ready")
        xt_done = sem("xt_done")
        xt_ready = sem("xt_ready")
        wr_ready = sem("wr_ready")
        ksq_done = sem("ksq_done")
        br_ready = sem("br_ready")
        lg_done = sem("lg_done")
        rstep = sem("rstep")
        lsh_ready = sem("lsh_ready")
        lexp_ready = sem("lexp_ready")
        xsq_ready = sem("xsq_ready")
        cnt_ready = sem("cnt_ready")
        count_done = sem("count_done")
        tie_ready = sem("tie_ready")
        rank_done = sem("rank_done")
        gate_ready = sem("gate_ready")
        gt_done = sem("gt_done")
        gt_ready = sem("gt_ready")
        gb_done = sem("gb_done")
        acc0_ready = sem("acc0_ready")
        w_in = [sem("w_in0"), sem("w_in1")]
        h_done = sem("h_done")
        gelu_done = sem("gelu_done")
        eo_done = sem("eo_done")
        acc_done = sem("acc_done")
        out_done = sem("out_done")

        N_CONST, N_WEIGHT = 6, 18
        CHL0, CHL1 = E0 * NCH, E1 * NCH

        block = ctx.enter_context(nc.Block())

        @block.sync
        def _(sp):
            for n in ("ident", "ident_h", "tri", "ropec", "ropes", "bits"):
                dst = {"ident": ident, "ident_h": ident_h, "tri": tri, "ropec": ropec, "ropes": ropes,
                       "bits": bits}[n]
                sp.dma_start(dst[:], d["c_" + n]).then_inc(consts_in, 16)
            sp.dma_start(XT[:, :], d["xT"]).then_inc(x_in, 16)
            sp.dma_start(X[:, :, :], d["x"].rearrange("(t p) c -> p t c", p=P)).then_inc(x_in, 16)
            for dst, src in ((wqkv0, "wqkv0"), (bqkv0, "bqkv0"), (wo[0], "wo0"), (wo[1], "wo1"), (bo[0], "bo0"),
                             (bo[1], "bo1"), (wq1, "wq1"), (bq1, "bq1"), (wl1, "wl1"), (bl1, "bl1"),
                             (wkv1, "wkv1"), (ws0, "ws0"), (bs0, "bs0"), (keysT, "keysT"), (rwT, "rwT"),
                             (rb, "rb"), (b2[0], "b2_0"), (b2[1], "b2_1")):
                sp.dma_start(dst[:], d[src]).then_inc(weights_in, 16)

            def expert_weights(lay, e, slot, reuse, chunks):
                if reuse:
                    sp.wait_ge(eo_done, chunks)
                src1 = d[f"w1_{lay}"][bass.ds(e, 1), :, :].rearrange("a p f -> p (a f)")
                src3 = d[f"b1_{lay}"][bass.ds(e, 1), :, :].rearrange("a p f -> p (a f)")
                sp.dma_start(b1[:, slot, :], src3).then_inc(w_in[slot], 16)
                src2 = d[f"w2_{lay}"][bass.ds(e, 1), :, :].rearrange("a (t p) c -> p (a t) c", p=P)
                sp.dma_start(w1[:, slot, :], src1).then_inc(w_in[slot], 16)
                sp.dma_start(w2[:, slot, :, :], src2).then_inc(w_in[slot], 16)

            expert_weights(0, 0, 0, False, 0)
            expert_weights(0, 1, 1, False, 0)
            with sp.Fori(1, E0 // 2) as eh:
                e = 2 * eh
                for s in range(2):
                    expert_weights(0, e + s, s, True, (e + (s - 1)) * NCH)
            expert_weights(1, 0, 0, True, (E0 - 1) * NCH)
            expert_weights(1, 1, 1, True, E0 * NCH)
            with sp.Fori(1, E1 // 2) as eh:
                e = 2 * eh
                for s in range(2):
                    expert_weights(1, e + s, s, True, (e + (s - 1)) * NCH + CHL0)
            out_v = d["out"].rearrange("(t p) c -> p t c", p=P)
            sp.wait_ge(xn_ready, 4 * NT)
            sp.dma_start(out_v, X[:, :, :]).then_inc(out_done, 16)
            sp.wait_ge(out_done, 16)

        @block.gpsimd
        def _(pool):
            nc.gpsimd.memset(ones[:, :], 1.0)
            nc.gpsimd.memset(ones_b[:, :], 1.0)
            for i in range(2):
                nc.gpsimd.memset(aug[i][:, :, 0:H, NROW:HP], 0.0)
                nc.gpsimd.memset(aug[i][:, :, H:2 * H, NROW + 2:HP], 0.0)
                nc.gpsimd.memset(aug[i][:, :, H:2 * H, NROW:NROW + 2], MUNIT)
                nc.gpsimd.memset(vaug[i][:, :, :, HD + 1:HP], 0.0)
                last = nc.gpsimd.memset(vaug[i][:, :, :, HD:HD + 1], 1.0)
            last.then_inc(zeroed, 1)
            pool.wait_ge(zeroed, 2)

            def ring_copy(lay, b, par):
                g = b + NB * lay
                pool.wait_ge(proj_done, 2 * (g - 1)) if not isinstance(b, int) or g >= 2 else None
                nc.gpsimd.tensor_copy(xr[:, par, :], XT[:, bass.ds(b * L, L)]).then_inc(xr_ready, 1)

            def build_aug(lay, b, par):
                g = b + NB * lay
                first = isinstance(b, int) and g < 2
                pool.wait_ge(qkv_ready, 2 * g + 2)
                src = qk
                v4 = lambda t: t[:, :, :].rearrange("p t (h x) -> p t h x", x=HD)
                if lay == 0:
                    n = 2 * P // HD
                    cos = ropec[:, :, :].unsqueeze(2).to_broadcast([P, 2, n, HD])
                    sin = ropes[:, :, :].unsqueeze(2).to_broadcast([P, 2, n, HD])
                    hh = HD // 2
                    for t in range(2):
                        nc.gpsimd.tensor_tensor(v4(rt1)[:, t], v4(qk)[:, t], cos[:, t], ALU.mult).then_inc(rope_step, 1)
                        nc.gpsimd.tensor_tensor(v4(rt2)[:, t, :, 0:hh], v4(qk)[:, t, :, hh:HD], sin[:, t, :, 0:hh],
                                                ALU.mult).then_inc(rope_step, 1)
                        nc.gpsimd.tensor_tensor(v4(rt2)[:, t, :, hh:HD], v4(qk)[:, t, :, 0:hh], sin[:, t, :, hh:HD],
                                                ALU.mult).then_inc(rope_step, 1)
                    pool.wait_ge(rope_step, 7 * g + 6)
                    nc.gpsimd.tensor_tensor(rt1[:, :, :], rt1[:, :, :], rt2[:, :, :], ALU.add).then_inc(rope_step, 1)
                    pool.wait_ge(rope_step, 7 * g + 7)
                    src = rt1
                if not first:
                    pool.wait_ge(tq2_done, g - 1)
                A = aug[par]
                s4 = v4(src)
                one = ones[:, 0:HD].unsqueeze(1).unsqueeze(1).to_broadcast([P, H, 2, HD])
                for t in range(2):
                    qin = s4[:, t, 0:H, :].unsqueeze(2).to_broadcast([P, H, 2, HD])
                    kin = s4[:, t, H:2 * H, :].unsqueeze(2).to_broadcast([P, H, 2, HD])
                    qout = A[:, t, 0:H, 0:2 * HD].rearrange("p h (r x) -> p h r x", x=HD)
                    kout = A[:, t, H:2 * H, 0:4 * HD].rearrange("p h (r y) -> p h r y", r=2)[:, :, :, 0:HD]
                    nc.gpsimd.tensor_tensor(qout, qin, one, ALU.mult).then_inc(split_step, 1)
                    nc.gpsimd.tensor_tensor(kout, kin, one, ALU.mult).then_inc(split_step, 1)
                pool.wait_ge(split_step, 4 * g + 4)
                for t in range(2):
                    nc.gpsimd.tensor_tensor(A[:, t, 0:H, 2 * HD:3 * HD], s4[:, t, 0:H, :], A[:, t, 0:H, 0:HD],
                                            ALU.subtract)
                    last = nc.gpsimd.tensor_tensor(A[:, t, H:2 * H, HD:2 * HD], s4[:, t, H:2 * H, :],
                                                   A[:, t, H:2 * H, 0:HD], ALU.subtract)
                last.then_inc(aug_ready, 1)

            def build_vaug(lay, b, par):
                g = b + NB * lay
                if not (isinstance(b, int) and g < 2):
                    pool.wait_ge(av_done, 4 * (g - 1))
                v = vraw[:, :, :].rearrange("p t (h x) -> p t h x", x=HD)
                one = ones[:, 0:HD].unsqueeze(1).unsqueeze(1).to_broadcast([P, 2, H, HD])
                nc.gpsimd.tensor_tensor(vaug[par][:, :, :, 0:HD], v, one, ALU.mult).then_inc(vaug_ready, 1)

            def pool_iteration(lay, i, par):
                nxt = 1 - par
                ring_copy(lay, i + 1, nxt)
                build_aug(lay, i + 1, nxt)
                build_vaug(lay, i + 1, nxt)

            pool.wait_ge(consts_in, 16 * N_CONST)
            pool.wait_ge(x_in, 32)
            for lay in range(2):
                if lay == 1:
                    pool.wait_ge(xt_ready, 8)
                ring_copy(lay, 0, 0)
                build_aug(lay, 0, 0)
                build_vaug(lay, 0, 0)
                pool_iteration(lay, 0, 0)
                pool_iteration(lay, 1, 1)
                with pool.Fori(1, NB // 2 - 1) as ih:
                    i = 2 * ih
                    pool_iteration(lay, i, 0)
                    pool_iteration(lay, i + 1, 1)
                pool_iteration(lay, NB - 2, 0)
            pool.wait_ge(xn_ready, 3 * NT)
            nc.gpsimd.tensor_tensor(xsq[:, :, :], X[:, :, :], X[:, :, :], ALU.mult).then_inc(xsq_ready, 1)

        @block.tensor
        def _(pe):
            def s1(lay, i, par, u):
                g = i + NB * lay
                qt, jp, q = u // 8, (u % 8) // 4, u % 4
                if u == 0:
                    pe.wait_ge(tq_ready, g + 1)
                    pe.wait_ge(tk_ready, g + 1)
                if not (isinstance(i, int) and g == 0 and u < 2):
                    pe.wait_ge(s1_used, 16 * g + u - 1)
                rows = slice(HP * q, HP * q + NROW)
                for jj in range(2):
                    j = 2 * jp + jj
                    last = nc.tensor.matmul(bank[S1B[u % 2]][:, L * jj:L * jj + L],
                                            QT[par][rows, j, P * qt:P * qt + P], KT[par][rows, j, :],
                                            start=True, stop=True)
                last.then_inc(s1_done, 1)

            def st(lay, b, par, v):
                g = b + NB * lay
                j, q = v // 4, v % 4
                if v == 0:
                    pe.wait_ge(tq2_ready, g + 1)
                if not (isinstance(b, int) and g == 0 and v < 2):
                    pe.wait_ge(exp_done, 16 * g + v - 1)
                rows = slice(HP * q, HP * q + NROW + 2)
                for kt in range(2):
                    last = nc.tensor.matmul(bank[STB[v % 2]][:, L * kt:L * kt + L],
                                            KT[par][rows, j, P * kt:P * kt + P], QT2[rows, j, :],
                                            start=True, stop=True)
                last.then_inc(st_done, 1)

            def av(lay, b, par, j):
                g = b + NB * lay
                if j == 0:
                    pe.wait_ge(vaug_ready, g + 1)
                if j == 0 and not (isinstance(b, int) and g == 0):
                    pe.wait_ge(ot_ready, 2 * g)
                if j == 2:
                    pe.wait_ge(ot_ready, 2 * g + 1)
                pe.wait_ge(exp_done, 16 * g + 4 * j + 4)
                for kt in range(2):
                    for q in range(4):
                        last = nc.tensor.matmul(bank[OTB][HP * q:HP * q + HP, L * (j % 2):L * (j % 2) + L],
                                                vaug[par][:, kt, 4 * j + q, :], prob[:, (4 * j + q) % 8, kt, :],
                                                start=(kt == 0), stop=(kt == 1))
                last.then_inc(av_done, 1)

            def bt(lay, b, pair):
                g = b + NB * lay
                pe.wait_ge(ot_ready, 2 * g + pair + 1)
                for t in range(2):
                    for jj in range(2):
                        at = P * (2 * t + jj)
                        last = nc.tensor.transpose(bank[M7][:, at:at + P], OT[:, pair, jj, P * t:P * t + P], ident[:, :])
                last.then_inc(bt_done, 1)

            def pe_iteration(lay, i, par, mx_on, soft_on, front_on, tail_on):
                g = i + NB * lay
                nxt = 1 - par
                for u in range(16):
                    if mx_on:
                        s1(lay, i, par, u)
                    if u == 0 and tail_on:
                        pe.wait_ge(on_ready, 2 * (g - 2) + 1)
                        bt(lay, i - 2, 1)
                    if u == 1 and soft_on:
                        pe.wait_ge(m_ready, g)
                        if tail_on:
                            pe.wait_ge(on_ready, 2 * (g - 2) + 2)
                        elif lay == 1:
                            pe.wait_ge(y_ready, NB)
                        for j in range(NJ):
                            for t in range(2):
                                last = nc.tensor.transpose(half[M7][:, L * j + P * t:L * j + P * t + P],
                                                           aug[nxt][:, t, 4 * j:4 * j + 4, :], ident_h[:, :])
                        last.then_inc(tq2_done, 1)
                    if soft_on:
                        for v in soft_units(u):
                            st(lay, i - 1, nxt, v)
                    if u == 2 and front_on:
                        front_latent(lay, i + 1, nxt)
                    if u == 4 and front_on:
                        front_proj(lay, i + 1, nxt)
                    if u == 5 and tail_on:
                        pe.wait_ge(tq2_ready, g) if soft_on else None
                        pe.wait_ge(on_ready, 2 * (g - 2) + 2)
                        for t in range(2):
                            last = nc.tensor.transpose(bank[M7][:, P * t:P * t + P], on[:, t, :, :], ident[:, :])
                        last.then_inc(ox_done, 1)
                    if u == 8 and tail_on:
                        pe.wait_ge(ox_ready, g - 1)
                        for t in range(2):
                            nc.tensor.matmul(bank[M7][:, P * t:P * t + P], oxT[:, P * t:P * t + P], wo[lay][:, :],
                                             start=True, stop=False)
                            last = nc.tensor.matmul(bank[M7][:, P * t:P * t + P], ones[0:1, :], bo[lay][0:1, :],
                                                    start=False, stop=True)
                        last.then_inc(pj_done, 1)
                    if u == 8 and soft_on:
                        av(lay, i - 1, nxt, 0)
                    if u == 11 and soft_on:
                        av(lay, i - 1, nxt, 1)
                    if u == 13 and front_on:
                        front_transposes(lay, i + 1, nxt)
                    if u == 14 and soft_on:
                        if tail_on:
                            pe.wait_ge(y_ready, g - 1)
                        else:
                            pe.wait_ge(tq2_ready, g)
                        bt(lay, i - 1, 0)
                    if u == 15 and soft_on:
                        av(lay, i - 1, nxt, 2)
                if soft_on:
                    av(lay, i - 1, nxt, 3)

            def front_latent(lay, b, par):
                g = b + NB * lay
                pe.wait_ge(xr_ready, g + 1)
                if not (isinstance(b, int) and g == 0):
                    pe.wait_ge(tq_ready, g)
                    pe.wait_ge(tk_ready, g)
                if lay == 1:
                    nc.tensor.matmul(bank[M5][0:LAT, 0:L], wl1[:, :], xr[:, par, :], start=True,
                                     stop=True).then_inc(lat_done, 1)

            def front_proj(lay, b, par):
                if lay == 1:
                    pe.wait_ge(lat_ready, b + 1)
                for t in range(2):
                    tok = xr[:, par, P * t:P * t + P]
                    if lay == 0:
                        nc.tensor.matmul(bank[M5 + t][:, 0:3 * P], tok, wqkv0[:, :], start=True, stop=False)
                        last = nc.tensor.matmul(bank[M5 + t][:, 0:3 * P], ones[0:1, :], bqkv0[0:1, :],
                                                start=False, stop=True)
                    else:
                        nc.tensor.matmul(bank[M5 + t][:, 0:P], tok, wq1[:, :], start=True, stop=False)
                        nc.tensor.matmul(bank[M5 + t][:, 0:P], ones[0:1, :], bq1[0:1, :], start=False, stop=True)
                        last = nc.tensor.matmul(bank[M5 + t][:, P:3 * P], latT[:, P * t:P * t + P], wkv1[:, :],
                                                start=True, stop=True)
                    last.then_inc(proj_done, 1)

            def front_transposes(lay, b, par):
                g = b + NB * lay
                pe.wait_ge(aug_ready, g + 1)
                for half_at, base, done in ((M5, 0, tq_done), (M6, H, tk_done)):
                    for j in range(NJ):
                        for t in range(2):
                            last = nc.tensor.transpose(half[half_at][:, L * j + P * t:L * j + P * t + P],
                                                       aug[par][:, t, base + 4 * j:base + 4 * j + 4, :], ident_h[:, :])
                    last.then_inc(done, 1)

            def turn(n):
                for c in range(4):
                    pe.wait_ge(xn_ready, NT * n + 4 * c + 4)
                    for t in range(4):
                        last = nc.tensor.transpose(bank[c][:, P * t:P * t + P], X[:, 4 * c + t, :], ident[:, :])
                    last.then_inc(xt_done, 1)

            def logits(lay, w, brow, E):
                pe.wait_ge(xt_ready, 8 * lay + 4)
                if lay == 1:
                    pe.wait_ge(wr_ready, 2)
                    nc.tensor.matmul(bank[6][0:1, 0:E1], ones[:, 0:1], ksq[:, :], start=True,
                                     stop=True).then_inc(ksq_done, 1)
                    pe.wait_ge(br_ready, 1)
                for t in range(NT):
                    nc.tensor.matmul(bank[5][:, E * t:E * t + E], XT[:, P * t:P * t + P], w[:, :], start=True, stop=False)
                    last = nc.tensor.matmul(bank[5][:, E * t:E * t + E], ones[0:1, :], brow[0:1, :], start=False, stop=True)
                last.then_inc(lg_done, 1)

            def gate_bias(lay, E):
                pe.wait_ge(gate_ready, lay + 1)
                for c in range(4):
                    for t in range(4):
                        last = nc.tensor.transpose(bank[c][0:E, P * t:P * t + P], gate[:, 4 * c + t, 0:E], ident[:, :])
                    last.then_inc(gt_done, 1)
                for c in range(4):
                    pe.wait_ge(gt_ready, 4 * lay + c + 1)
                    for t in range(4):
                        last = nc.tensor.matmul(bank[c][:, P * t:P * t + P], gateT[0:E, P * (4 * c + t):P * (4 * c + t + 1)],
                                                b2[lay][:, :], start=True, stop=True)
                    last.then_inc(gb_done, 1)

            def hidden(slot, c, k, base):
                for f in range(NF):
                    if base is not None:
                        pe.wait_ge(gelu_done, base + f)
                    nc.tensor.matmul(bank[f][:, :], w1[:, slot, P * f:P * f + P], XT[:, CH * c:CH * c + CH],
                                     start=True, stop=True).then_inc(h_done, 1)

            def expert_out(slot, k, kd):
                pe.wait_ge(gelu_done, NF * kd + NF)
                if not (isinstance(kd, int) and kd < 2):
                    pe.wait_ge(acc_done, 4 * kd - 4)
                for t in range(4):
                    for f in range(NF):
                        last = nc.tensor.matmul(bank[4 + k % 2][:, P * t:P * t + P], hid[:, k % 2, f, P * t:P * t + P],
                                                w2[:, slot, f, :], start=(f == 0), stop=(f == NF - 1))
                last.then_inc(eo_done, 1)

            def experts(lay, E):
                base = CHL0 * lay
                wb = 24 * E0 * lay

                def pair(e, last_pair):
                    for k in range(2 * NCH):
                        kd = base + e * NCH + k
                        nk = k + 1
                        if not (last_pair and nk == 2 * NCH):
                            if nk % NCH == 0:
                                slot = (nk // NCH) % 2
                                pe.wait_ge(w_in[slot], 24 * (e + 2 * (nk // (2 * NCH))) + 48 + wb)
                            hidden((nk // NCH) % 2, nk % NCH, nk, NF * kd + 1)
                        expert_out(k // NCH, k, kd)

                pe.wait_ge(w_in[0], 48 + wb)
                pe.wait_ge(acc0_ready, 4 * lay + 4)
                hidden(0, 0, 0, None)
                pair(0, False)
                with pe.Fori(1, E // 2 - 1) as eh:
                    e = 2 * eh
                    pair(e, False)
                pair(E - 2, True)

            pe.wait_ge(consts_in, 16 * N_CONST)
            pe.wait_ge(weights_in, 16 * N_WEIGHT)
            pe.wait_ge(zeroed, 2)
            for lay in range(2):
                if lay == 1:
                    pe.wait_ge(xt_ready, 8)
                front_latent(lay, 0, 0)
                front_proj(lay, 0, 0)
                front_transposes(lay, 0, 0)
                pe_iteration(lay, 0, 0, True, False, True, False)
                pe_iteration(lay, 1, 1, True, True, True, False)
                with pe.Fori(1, NB // 2 - 1) as ih:
                    i = 2 * ih
                    pe_iteration(lay, i, 0, True, True, True, True)
                    pe_iteration(lay, i + 1, 1, True, True, True, True)
                pe_iteration(lay, NB - 2, 0, True, True, True, True)
                pe_iteration(lay, NB - 1, 1, True, True, False, True)
                pe_iteration(lay, NB, 0, False, True, False, True)
                pe_iteration(lay, NB + 1, 1, False, False, False, True)
                turn(2 * lay)
                if lay == 0:
                    logits(0, ws0, bs0, E0)
                    with pe.Fori(0, NBITS) as it:
                        pe.wait_ge(cnt_ready, it + 1)
                        nc.tensor.matmul(bank[6][:, 0:E0], ones_b[:, :], cnt[:, 0:E0], start=True,
                                         stop=True).then_inc(count_done, 1)
                    pe.wait_ge(cnt_ready, NBITS + 1)
                    nc.tensor.matmul(bank[6][:, 0:E0], ones_b[:, :], cnt[:, 0:E0], start=True,
                                     stop=True).then_inc(count_done, 1)
                    pe.wait_ge(tie_ready, 1)
                    nc.tensor.matmul(bank[7][:, 0:NT * E0], tri[:, :], eqb[:, :, :], start=True, stop=False)
                    nc.tensor.matmul(bank[7][:, 0:NT * E0], ones_b[:, :], cumb[:, :, :], start=False,
                                     stop=True).then_inc(rank_done, 1)
                else:
                    logits(1, wr1, br1, E1)
                gate_bias(lay, (E0, E1)[lay])
                experts(lay, (E0, E1)[lay])
                if lay == 0:
                    turn(1)

        @block.scalar
        def _(act):
            def act_iteration(lay, i, par, mx_on, soft_on, front_on, tail_on):
                g = i + NB * lay
                nxt = 1 - par
                for u in range(16):
                    if soft_on:
                        for v in soft_units(u):
                            gb = g - 1
                            act.wait_ge(st_done, 16 * gb + v + 1)
                            if v % 4 == 0 and not (isinstance(i, int) and gb == 0 and v < 8):
                                act.wait_ge(av_done, 4 * gb + v // 4 - 1)
                            nc.scalar.activation(prob[:, v % 8, :, :], bank[STB[v % 2]][:, :], ACT.Exp,
                                                 scale=SCALE).then_inc(exp_done, 1)
                    if u == 2 and front_on:
                        lat_evac(lay, i + 1)
                    if u == 4 and front_on:
                        front_evac(lay, i + 1)
                    if u == 6 and tail_on:
                        act.wait_ge(ox_done, g - 1)
                        nc.scalar.copy(oxT[:, :], bank[M7][:, 0:L]).then_inc(ox_ready, 1)
                    if u == 12 and soft_on:
                        ot_evac(lay, i - 1, 0)
                if front_on:
                    act.wait_ge(tk_done, g + 2)
                    if soft_on:
                        act.wait_ge(st_done, 16 * g)
                    nc.scalar.copy(KT[nxt][:, :, :], half[M6]).then_inc(tk_ready, 1)
                if soft_on:
                    ot_evac(lay, i - 1, 1)

            def ot_evac(lay, b, pair):
                g = b + NB * lay
                act.wait_ge(av_done, 4 * g + 2 * pair + 2)
                if not (isinstance(b, int) and g == 0):
                    act.wait_ge(bt_done, 2 * g + pair - 1)
                nc.scalar.copy(OT[:, pair, :, :], bank[OTB][:, :]).then_inc(ot_ready, 1)

            def lat_evac(lay, b):
                if lay == 1:
                    act.wait_ge(lat_done, b + 1)
                    nc.scalar.activation(latT[0:LAT, :], bank[M5][0:LAT, 0:L], ACT.Identity,
                                         bias=bl1[:, 0:1]).then_inc(lat_ready, 1)

            def front_evac(lay, b):
                g = b + NB * lay
                if not (isinstance(b, int) and g == 0):
                    act.wait_ge(aug_ready, g)
                    act.wait_ge(vaug_ready, g)
                for t in range(2):
                    act.wait_ge(proj_done, 2 * g + t + 1)
                    nc.scalar.copy(qk[:, t, :], bank[M5 + t][:, 0:2 * P])
                    nc.scalar.copy(vraw[:, t, :], bank[M5 + t][:, 2 * P:3 * P]).then_inc(qkv_ready, 1)

            def std(n):
                act.wait_ge(var_ready, n + 1)
                nc.scalar.activation(rstd[:, :], mv[:, :, 1], ACT.Sqrt).then_inc(std_ready, 1)

            def turn_evac(n):
                for c in range(0, 4, 2):
                    act.wait_ge(xt_done, 4 * n + c + 1)
                    nc.scalar.copy(XT[:, CH * c:CH * c + CH], bank[c][:, :]).then_inc(xt_ready, 1)

            def gates_evac(lay, E):
                for c in range(4):
                    act.wait_ge(gt_done, 4 * lay + c + 1)
                    nc.scalar.copy(gateT[0:E, CH * c:CH * c + CH], bank[c][0:E, :]).then_inc(gt_ready, 1)

            def gelus(lay, E, func):
                base = CHL0 * lay

                def chunk(e, k):
                    kd = base + e * NCH + k
                    if not (isinstance(e, int) and kd < 2):
                        act.wait_ge(eo_done, kd - 1)
                    for f in range(NF):
                        act.wait_ge(h_done, NF * kd + f + 1)
                        nc.scalar.activation(hid[:, k % 2, f, :], bank[f][:, :], func,
                                             bias=b1[:, k // NCH, f:f + 1]).then_inc(gelu_done, 1)

                for k in range(2 * NCH):
                    chunk(0, k)
                with act.Fori(1, E // 2) as eh:
                    e = 2 * eh
                    for k in range(2 * NCH):
                        chunk(e, k)

            act.wait_ge(weights_in, 16 * N_WEIGHT)
            act.wait_ge(zeroed, 2)
            for lay in range(2):
                lat_evac(lay, 0)
                front_evac(lay, 0)
                act.wait_ge(tk_done, NB * lay + 1)
                if lay == 1:
                    act.wait_ge(st_done, 16 * NB)
                nc.scalar.copy(KT[0][:, :, :], half[M6]).then_inc(tk_ready, 1)
                act_iteration(lay, 0, 0, True, False, True, False)
                act_iteration(lay, 1, 1, True, True, True, False)
                with act.Fori(1, NB // 2 - 1) as ih:
                    i = 2 * ih
                    act_iteration(lay, i, 0, True, True, True, True)
                    act_iteration(lay, i + 1, 1, True, True, True, True)
                act_iteration(lay, NB - 2, 0, True, True, True, True)
                act_iteration(lay, NB - 1, 1, True, True, False, True)
                act_iteration(lay, NB, 0, False, True, False, True)
                act_iteration(lay, NB + 1, 1, False, False, False, True)
                std(2 * lay)
                turn_evac(2 * lay)
                act.wait_ge(lsh_ready, lay + 1)
                E = (E0, E1)[lay]
                nc.scalar.activation(pr[:, :, 0:E], lg[:, :, 0:E], ACT.Exp).then_inc(lexp_ready, 1)
                gates_evac(lay, E)
                gelus(lay, E, (ACT.Gelu_apprx_tanh, ACT.Gelu)[lay])
                std(2 * lay + 1)
                if lay == 0:
                    turn_evac(1)

        @block.vector
        def _(dve):
            steps = [0]

            def step(ins):
                steps[0] += 1
                ins.then_inc(rstep, 1)
                dve.wait_ge(rstep, steps[0])

            def dve_iteration(lay, i, par, mx_on, soft_on, front_on, tail_on):
                g = i + NB * lay
                nxt = 1 - par
                for u in range(16):
                    if mx_on:
                        qt, jp, q = u // 8, (u % 8) // 4, u % 4
                        dve.wait_ge(s1_done, 16 * g + u + 1)
                        m_at = mx[:, qt, :].rearrange("p (a j q) -> p a j q", a=2, j=2)[:, jp, :, q]
                        nc.vector.tensor_reduce(m_at, bank[S1B[u % 2]][:, :].rearrange("p (j k) -> p j k", j=2), AX.X,
                                                ALU.max).then_inc(s1_used, 1)
                    if u == 1 and tail_on:
                        norm(lay, i - 2, 1)
                    if u == 2 and soft_on:
                        dve.wait_ge(tq2_done, g)
                        if not (isinstance(i, int) and g == 1):
                            dve.wait_ge(st_done, 16 * (g - 1))
                        nc.vector.tensor_copy(QT2[:, :, :], half[M7]).then_inc(tq2_ready, 1)
                    if u == 9 and tail_on:
                        dve.wait_ge(pj_done, g - 1)
                        at = bass.ds(2 * (i - 2), 2)
                        nc.vector.tensor_tensor(Y[:, at, :], bank[M7][:, 0:2 * P].rearrange("p (t c) -> p t c", t=2),
                                                X[:, at, :], ALU.add).then_inc(y_ready, 1)
                    if u == 14 and front_on:
                        q_evac(lay, i + 1, nxt)
                    if u == 15 and soft_on:
                        norm(lay, i - 1, 0)
                if mx_on:
                    dve.wait_ge(s1_used, 16 * g + 16)
                    nc.vector.tensor_scalar(mneg[:, :, :], mx[:, :, :], -1.0 / MUNIT, None, ALU.mult).then_inc(m_step, 1)
                    dve.wait_ge(m_step, 2 * g + 1)
                    nc.vector.tensor_copy(aug[par][:, :, 0:H, NROW], mneg[:, :, :]).then_inc(m_step, 1)
                    dve.wait_ge(m_step, 2 * g + 2)
                    nc.vector.tensor_tensor(aug[par][:, :, 0:H, NROW + 1], mneg[:, :, :], aug[par][:, :, 0:H, NROW],
                                            ALU.subtract).then_inc(m_ready, 1)

            def q_evac(lay, b, par):
                g = b + NB * lay
                dve.wait_ge(tq_done, g + 1)
                if not (isinstance(b, int) and g < 2):
                    dve.wait_ge(s1_done, 16 * (g - 1))
                nc.vector.tensor_copy(QT[par][:, :, :], half[M5]).then_inc(tq_ready, 1)

            def norm(lay, b, pair):
                g = b + NB * lay
                dve.wait_ge(bt_done, 2 * g + pair + 1)
                o = bank[M7][:, :].rearrange("p (h x) -> p h x", x=HP)
                nc.vector.reciprocal(rden[:, pair, :], o[:, :, HD]).then_inc(rden_ready, 1)
                dve.wait_ge(rden_ready, 2 * g + pair + 1)
                if not (isinstance(b, int) and g == 0):
                    dve.wait_ge(ox_done, g)
                for t in range(2):
                    last = nc.vector.tensor_tensor(on[:, t, 8 * pair:8 * pair + 8, :], o[:, 8 * t:8 * t + 8, 0:HD],
                                                   rden[:, pair, 8 * t:8 * t + 8].unsqueeze(2).to_broadcast([P, 8, HD]),
                                                   ALU.mult)
                last.then_inc(on_ready, 1)

            def layernorm(n, src):
                for t in range(NT):
                    last = nc.vector.bn_stats(stats[:, t, :], src[:, t, :])
                last.then_inc(stats_ready, 1)
                dve.wait_ge(stats_ready, 2 * n + 1)
                for t in range(NT):
                    last = nc.vector.bn_aggr(mv[:, t, :], stats[:, t, :])
                last.then_inc(stats_ready, 1)
                dve.wait_ge(stats_ready, 2 * n + 2)
                nc.vector.tensor_scalar(mv[:, :, 1], mv[:, :, 1], EPS, None, ALU.add).then_inc(var_ready, 1)
                dve.wait_ge(std_ready, n + 1)
                step(nc.vector.reciprocal(rstd[:, :], rstd[:, :]))
                step(nc.vector.scalar_tensor_tensor(out=nmr[:, :], in0=mv[:, :, 0], scalar=-1.0, in1=rstd[:, :],
                                                    op0=ALU.mult, op1=ALU.mult))
                for t in range(NT):
                    nc.vector.tensor_scalar(X[:, t, :], src[:, t, :], rstd[:, t:t + 1], nmr[:, t:t + 1], ALU.mult,
                                            ALU.add).then_inc(xn_ready, 1)

            def turn_evac(n):
                for c in range(1, 4, 2):
                    dve.wait_ge(xt_done, 4 * n + c + 1)
                    nc.vector.tensor_copy(XT[:, CH * c:CH * c + CH], bank[c][:, :]).then_inc(xt_ready, 1)

            def bc(ap, E):
                return ap.unsqueeze(2).to_broadcast([P, NT, E])

            def select_first_layer():
                E = E0
                lgv, prv, gv = lg[:, :, 0:E], pr[:, :, 0:E], gate[:, :, 0:E]
                by_e = lambda ap: ap.rearrange("p t e -> p e t")
                dve.wait_ge(lg_done, 1)
                raw = bank[5][:, 0:NT * E].rearrange("p (t e) -> p t e", e=E)
                step(nc.vector.tensor_reduce(col[:, :], raw, AX.X, ALU.max))
                nc.vector.tensor_tensor(lgv, raw, bc(col[:, :], E), ALU.subtract).then_inc(lsh_ready, 1)
                dve.wait_ge(lexp_ready, 1)
                step(nc.vector.tensor_reduce(col2[:, :], prv, AX.X, ALU.add))
                step(nc.vector.reciprocal(col2[:, :], col2[:, :]))
                step(nc.vector.tensor_tensor(prv, prv, bc(col2[:, :], E), ALU.mult))
                step(nc.vector.memset(thr[:, :], 0.0))
                base = steps[0]
                with dve.Fori(0, NBITS) as it:
                    n = base + 5 * it
                    nc.vector.tensor_tensor(cand[:, :].bitcast(I32), thr[:, :].bitcast(I32),
                                            bits[:, bass.ds(it * E, E)], ALU.bitwise_or).then_inc(rstep, 1)
                    dve.wait_ge(rstep, n + 1)
                    nc.vector.tensor_tensor(cmp_[:, :, :], prv, cand[:, :].unsqueeze(1).to_broadcast([P, NT, E]),
                                            ALU.is_ge).then_inc(rstep, 1)
                    dve.wait_ge(rstep, n + 2)
                    with nc.allow_low_precision(reason="counts up to 16"):
                        nc.vector.tensor_reduce(cnt[:, 0:E], by_e(cmp_[:, :, :]), AX.X, ALU.add).then_inc(cnt_ready, 1)
                    dve.wait_ge(count_done, it + 1)
                    nc.vector.scalar_tensor_tensor(out=keep[:, :], in0=bank[6][:, 0:E], scalar=float(CAP),
                                                   in1=cand[:, :], op0=ALU.is_ge, op1=ALU.mult).then_inc(rstep, 1)
                    dve.wait_ge(rstep, n + 3)
                    nc.vector.tensor_tensor(thr[:, :], thr[:, :], keep[:, :], ALU.max).then_inc(rstep, 2)
                    dve.wait_ge(rstep, n + 5)
                steps[0] = base + 5 * NBITS
                tb = thr[:, :].unsqueeze(1).to_broadcast([P, NT, E])
                step(nc.vector.tensor_tensor(gtm[:, :, 0:E], prv, tb, ALU.is_gt))
                step(nc.vector.tensor_tensor(eqm[:, :, 0:E], prv, tb, ALU.is_equal))
                with nc.allow_low_precision(reason="counts up to 16"):
                    nc.vector.tensor_reduce(cnt[:, 0:E], by_e(gtm[:, :, 0:E]), AX.X, ALU.add).then_inc(cnt_ready, 1)
                step(nc.vector.tensor_copy(eqb[:, :, :], eqm[:, :, 0:E]))
                step(nc.vector.memset(cum[0][:, 0:1, 0:E], 0.0))
                step(nc.vector.tensor_copy(cum[0][:, 1:NT, 0:E], eqm[:, 0:NT - 1, 0:E]))
                a, sh = 0, 1
                while sh < NT:
                    step(nc.vector.tensor_copy(cum[1 - a][:, 0:sh, 0:E], cum[a][:, 0:sh, 0:E]))
                    step(nc.vector.tensor_tensor(cum[1 - a][:, sh:NT, 0:E], cum[a][:, sh:NT, 0:E],
                                                 cum[a][:, 0:NT - sh, 0:E], ALU.add))
                    a, sh = 1 - a, 2 * sh
                nc.vector.tensor_copy(cumb[:, :, :], cum[a][:, :, 0:E]).then_inc(tie_ready, 1)
                dve.wait_ge(count_done, NBITS + 1)
                step(nc.vector.tensor_scalar(need[:, :], bank[6][:, 0:E], -1.0, float(CAP), ALU.mult, ALU.add))
                dve.wait_ge(rank_done, 1)
                rank = bank[7][:, 0:NT * E].rearrange("p (t e) -> p t e", e=E)
                step(nc.vector.tensor_tensor(cmp_[:, :, :], rank, need[:, :].unsqueeze(1).to_broadcast([P, NT, E]),
                                             ALU.is_le))
                step(nc.vector.tensor_tensor(cmp_[:, :, :], cmp_[:, :, :], eqm[:, :, 0:E], ALU.mult))
                step(nc.vector.tensor_tensor(gtm[:, :, 0:E], gtm[:, :, 0:E], cmp_[:, :, :], ALU.add))
                nc.vector.tensor_tensor(gv, gtm[:, :, 0:E], prv, ALU.mult).then_inc(gate_ready, 1)

            def select_second_layer():
                E = E1
                dve.wait_ge(xsq_ready, 1)
                step(nc.vector.tensor_reduce(xn2[:, :], xsq[:, :, :], AX.X, ALU.add))
                dve.wait_ge(lg_done, 2)
                raw = bank[5][:, 0:NT * E].rearrange("p (t e) -> p t e", e=E)
                step(nc.vector.tensor_tensor(cum[0][:, :, :], raw, bc(xn2[:, :], E), ALU.subtract))
                for t in range(NT):
                    last = nc.vector.max(top8[:, t, :], cum[0][:, t, :])
                step(last)
                nc.vector.tensor_tensor(lg[:, :, :], cum[0][:, :, :], bc(top8[:, :, 0], E),
                                        ALU.subtract).then_inc(lsh_ready, 1)
                step(nc.vector.tensor_tensor(gtm[:, :, :], cum[0][:, :, :], bc(top8[:, :, TOPK - 1], E), ALU.is_gt))
                step(nc.vector.tensor_tensor(eqm[:, :, :], cum[0][:, :, :], bc(top8[:, :, TOPK - 1], E), ALU.is_equal))
                step(nc.vector.tensor_reduce(col[:, :], gtm[:, :, :], AX.X, ALU.add))
                step(nc.vector.tensor_scalar(col[:, :], col[:, :], -1.0, float(TOPK), ALU.mult, ALU.add))
                step(nc.vector.tensor_copy(cum[0][:, :, :], eqm[:, :, :]))
                a, sh = 0, 1
                while sh < E:
                    step(nc.vector.tensor_copy(cum[1 - a][:, :, 0:sh], cum[a][:, :, 0:sh]))
                    step(nc.vector.tensor_tensor(cum[1 - a][:, :, sh:E], cum[a][:, :, sh:E], cum[a][:, :, 0:E - sh],
                                                 ALU.add))
                    a, sh = 1 - a, 2 * sh
                step(nc.vector.tensor_tensor(cum[1 - a][:, :, :], cum[a][:, :, :], bc(col[:, :], E), ALU.is_le))
                step(nc.vector.tensor_tensor(eqm[:, :, :], eqm[:, :, :], cum[1 - a][:, :, :], ALU.mult))
                step(nc.vector.tensor_tensor(gtm[:, :, :], gtm[:, :, :], eqm[:, :, :], ALU.add))
                dve.wait_ge(lexp_ready, 2)
                step(nc.vector.tensor_tensor(gtm[:, :, :], gtm[:, :, :], pr[:, :, :], ALU.mult))
                step(nc.vector.tensor_reduce(col2[:, :], gtm[:, :, :], AX.X, ALU.add))
                step(nc.vector.reciprocal(col2[:, :], col2[:, :]))
                nc.vector.tensor_tensor(gate[:, :, :], gtm[:, :, :], bc(col2[:, :], E), ALU.mult).then_inc(gate_ready, 1)

            def sums(lay, E):
                base = CHL0 * lay
                for c in range(4):
                    dve.wait_ge(gb_done, 4 * lay + c + 1)
                    nc.vector.tensor_tensor(Y[:, 4 * c:4 * c + 4, :], bank[c][:, :].rearrange("p (t c) -> p t c", c=P),
                                            X[:, 4 * c:4 * c + 4, :], ALU.add).then_inc(acc0_ready, 1)
                dve.wait_ge(acc0_ready, 4 * lay + 4)
                with dve.Fori(0, E // 2) as eh:
                    e = 2 * eh
                    for k in range(2 * NCH):
                        kd = base + e * NCH + k
                        dve.wait_ge(eo_done, kd + 1)
                        for t in range(4):
                            tile = 4 * (k % NCH) + t
                            if k >= NCH:
                                dve.wait_ge(acc_done, 4 * (kd - NCH) + t + 1)
                            nc.vector.scalar_tensor_tensor(out=Y[:, tile, :], in0=bank[4 + k % 2][:, P * t:P * t + P],
                                                           scalar=gate[:, tile, bass.ds(e + k // NCH, 1)],
                                                           in1=Y[:, tile, :], op0=ALU.mult,
                                                           op1=ALU.add).then_inc(acc_done, 1)
                    dve.wait_ge(acc_done, 4 * (base + e * NCH + 2 * NCH))

            nc.vector.memset(latT[LAT:LAT + 1, :], 1.0).then_inc(zeroed, 1)
            dve.wait_ge(weights_in, 16 * N_WEIGHT)
            dve.wait_ge(consts_in, 16 * N_CONST)
            dve.wait_ge(zeroed, 2)
            dve.wait_ge(x_in, 32)
            nc.vector.tensor_tensor(ksq[:, :], keysT[:, :], keysT[:, :], ALU.mult).then_inc(wr_ready, 1)
            nc.vector.scalar_tensor_tensor(out=wr1[:, :], in0=keysT[:, :], scalar=2.0, in1=rwT[:, :], op0=ALU.mult,
                                           op1=ALU.add).then_inc(wr_ready, 1)
            for lay in range(2):
                q_evac(lay, 0, 0)
                dve_iteration(lay, 0, 0, True, False, True, False)
                dve_iteration(lay, 1, 1, True, True, True, False)
                with dve.Fori(1, NB // 2 - 1) as ih:
                    i = 2 * ih
                    dve_iteration(lay, i, 0, True, True, True, True)
                    dve_iteration(lay, i + 1, 1, True, True, True, True)
                dve_iteration(lay, NB - 2, 0, True, True, True, True)
                dve_iteration(lay, NB - 1, 1, True, True, False, True)
                dve_iteration(lay, NB, 0, False, True, False, True)
                dve_iteration(lay, NB + 1, 1, False, False, False, True)
                dve.wait_ge(y_ready, NB * (lay + 1))
                layernorm(2 * lay, Y)
                turn_evac(2 * lay)
                if lay == 0:
                    select_first_layer()
                else:
                    dve.wait_ge(ksq_done, 1)
                    nc.vector.tensor_tensor(br1[:, :], rb[:, :], bank[6][0:1, 0:E1], ALU.subtract).then_inc(br_ready, 1)
                    select_second_layer()
                sums(lay, (E0, E1)[lay])
                layernorm(2 * lay + 1, Y)
                if lay == 0:
                    turn_evac(1)


def shape_constants():
    inv = (np.float32(1.0) / np.float32(10000.0) ** (np.arange(0, HD, 2, dtype=np.float32) / np.float32(HD))).astype(np.float32)
    ang = np.arange(L, dtype=np.float32)[:, None] * inv[None, :]
    cos, sin = np.cos(ang).astype(np.float32), np.sin(ang).astype(np.float32)
    lay = lambda a: np.ascontiguousarray(a.reshape(2, P, HD).transpose(1, 0, 2))
    bit = (1 << np.arange(NBITS - 1, -1, -1)).astype(np.int32)
    return {
        "c_ident": np.eye(P, dtype=np.float32),
        "c_ident_h": np.eye(P, dtype=np.float16),
        "c_tri": None,
        "c_bits": np.tile(np.repeat(bit, E0)[None, :], (P, 1)),
        "c_ropec": lay(np.concatenate([cos, cos], 1)),
        "c_ropes": lay(np.concatenate([-sin, sin], 1)),
    }


def kernel(**inputs):
    import ml_dtypes
    import concourse.bacc as _bacc
    from concourse.bass_utils import run_bass_kernel_spmd as _run

    a = {k: np.asarray(v) for k, v in inputs.items()}
    x = a["L0_attn_x"].reshape(TOK, P)
    row = lambda v: v.reshape(1, -1)
    arrays = {
        "x": x, "xT": x.T,
        "wqkv0": np.concatenate([a["L0_attn_Wq"].T, a["L0_attn_Wk"].T, a["L0_attn_Wv"].T], 1),
        "bqkv0": row(np.concatenate([a["L0_attn_bq"], a["L0_attn_bk"], a["L0_attn_bv"]])),
        "wo0": a["L0_attn_Wo"].T, "bo0": row(a["L0_attn_bo"]),
        "wo1": a["L1_attn_Wo"], "bo1": row(a["L1_attn_bo"]),
        "wq1": a["L1_attn_Wq"], "bq1": row(a["L1_attn_bq"]),
        "wl1": a["L1_attn_Wl"], "bl1": a["L1_attn_bl"].reshape(LAT, 1),
        "wkv1": np.concatenate([np.concatenate([a["L1_attn_Wk"], a["L1_attn_Wv"]], 1),
                                row(np.concatenate([a["L1_attn_bk"], a["L1_attn_bv"]]))], 0),
        "ws0": a["L0_ffn_Ws"], "bs0": row(a["L0_ffn_bs"]),
        "keysT": a["L1_ffn_keys"].T, "rwT": a["L1_ffn_rw"].T, "rb": row(a["L1_ffn_rb"]),
        "w1_0": a["L0_ffn_W1"], "w2_0": a["L0_ffn_W2"],
        "w1_1": a["L1_ffn_w1"].transpose(0, 2, 1), "w2_1": a["L1_ffn_w2"].transpose(0, 2, 1),
        "b1_0": a["L0_ffn_b1"].reshape(E0, NF, P).transpose(0, 2, 1),
        "b1_1": a["L1_ffn_b1"].reshape(E1, NF, P).transpose(0, 2, 1),
        "b2_0": a["L0_ffn_b2"], "b2_1": a["L1_ffn_b2"],
    }
    arrays = {k: np.ascontiguousarray(v) for k, v in arrays.items()}
    consts = shape_constants()
    consts["c_tri"] = np.triu(np.ones((P, P))).astype(ml_dtypes.bfloat16)
    arrays.update(consts)
    nc = _bacc.Bacc("TRN2", target_bir_lowering=False, num_devices=1)
    d = {}
    for name, v in arrays.items():
        d[name] = nc.dram_tensor("in_" + name, v.shape, mybir.dt.from_np(v.dtype), kind="ExternalInput").ap()
    d["out"] = nc.dram_tensor("out", (TOK, P), F32, kind="ExternalOutput").ap()
    program(nc, d)
    r = _run(nc, [{"in_" + k: v for k, v in arrays.items()}], core_ids=[0])
    return np.asarray(r.results[0]["out"]).reshape(NB, L, P)
```

```python
from contextlib import ExitStack

import numpy as np

import concourse.bass as bass
from concourse import mybir

F32 = mybir.dt.float32
F16 = mybir.dt.float16
BF16 = mybir.dt.bfloat16
I32 = mybir.dt.int32
ALU = mybir.AluOpType
ACT = mybir.ActivationFunctionType
AX = mybir.AxisListType

P = 128
TOK = 2048
NT = TOK // P
L = 256
NB = TOK // L
H = 16
HD = 8
HP = 32
NJ = H // 4
NROW = 3 * HD
MUNIT = 64.0
SCALE = float(np.float32(1.0) / np.sqrt(np.float32(HD)))
EPS = 1e-5
E0, E1 = 8, 16
F = 512
NF = F // P
CAP = TOK // E0
TOPK = 4
LAT = 32
CH = 512
NROWS = [E0 * NT, E1 * NT]
KT = [n // P for n in NROWS]
NJT = [E0 * CAP // P, TOK * TOPK // P + E1]
DUMMY = TOK
ROWS = TOK + P
WB, W2AT = F, F + NF
WROW = W2AT + F
AHEAD = 3
NBITS = 30


def soft_units(u):
    return {2: [0], 3: [1], 4: [2], 5: [3], 6: [4], 7: [5, 6], 8: [7], 9: [8], 10: [9], 11: [10, 11],
            12: [12], 13: [13], 14: [14], 15: [15]}.get(u, [])


def program(nc, d):
    ctx = ExitStack()
    with ctx:
        def sb(name, shape, dt=F32):
            return ctx.enter_context(nc.sbuf_tensor(name, shape, dt))

        def sem(name):
            return ctx.enter_context(nc.semaphore(name))

        ident = sb("ident", [P, P])
        ident_h = sb("ident_h", [P, P], F16)
        tri = sb("tri", [P, P], BF16)
        ones_b = sb("ones_b", [P, P], BF16)
        ones = sb("ones", [P, P])
        bits = sb("bits", [P, NBITS * E0], I32)
        ropec = sb("ropec", [P, 2, HD])
        ropes = sb("ropes", [P, 2, HD])
        wqkv0 = sb("wqkv0", [P, 3 * P])
        braw = sb("braw", [3, 4 * P])
        bsplit = sb("bsplit", [3, 4 * P], BF16)
        bpart = [sb(f"bpart{i}", [3, 4 * P], BF16) for i in range(3)]
        brest = sb("brest", [3, 4 * P])
        wo = [sb("wo0", [P, P]), sb("wo1", [P, P])]
        bo = [sb("bo0", [P, P]), sb("bo1", [P, P])]
        XB = sb("XB", [P, NT, P])
        wq1 = sb("wq1", [P, P])
        wl1 = sb("wl1", [P, LAT])
        bl1 = sb("bl1", [LAT, 1])
        wkv1 = sb("wkv1", [LAT + 1, 2 * P])
        ws0 = sb("ws0", [P, E0])
        bs0 = sb("bs0", [1, E0])
        keysT = sb("keysT", [P, E1])
        rwT = sb("rwT", [P, E1])
        rb = sb("rb", [1, E1])
        wr1 = sb("wr1", [P, E1])
        ksq = sb("ksq", [P, E1])
        br1 = sb("br1", [1, E1])
        b2 = [sb("b2_0", [E0, P]), sb("b2_1", [E1, P])]

        X = sb("X", [P, NT, P])
        XT = sb("XT", [P, TOK])
        Y = sb("Y", [P, NT, P])
        stats = sb("stats", [P, NT, 6])
        mv = sb("mv", [P, NT, 2])
        rstd = sb("rstd", [P, NT])
        nmr = sb("nmr", [P, NT])

        xr = sb("xr", [P, 2, L])
        latT = sb("latT", [LAT + 1, L])
        qk = sb("qk", [P, 2, 2 * P])
        vraw = [sb(f"vraw{i}", [P, 2, P]) for i in range(2)]
        rt1 = sb("rt1", [P, 2, 2 * P])
        rt2 = sb("rt2", [P, 2, 2 * P])
        aug = [sb(f"aug{i}", [P, 2, 2 * H, HP], F16) for i in range(2)]
        vaug = [sb(f"vaug{i}", [P, 2, H, HP]) for i in range(2)]
        QT = [sb(f"QT{i}", [P, NJ, L], F16) for i in range(2)]
        KB = [sb(f"KB{i}", [P, NJ, 4, L], F16) for i in range(2)]
        QT2 = sb("QT2", [P, NJ, L], F16)
        mx = sb("mx", [P, 2, H])
        mneg = sb("mneg", [P, 2, H])
        prob = sb("prob", [P, 8, 2, L])
        OT = sb("OT", [P, 2, 2, L])
        rden = sb("rden", [P, 2, 16])
        on = sb("on", [P, 2, H, HD])
        oxT = sb("oxT", [P, L])

        lg = sb("lg", [P, NT, E1])
        pr = sb("pr", [P, NT, E1])
        gate = sb("gate", [P, NT, E1])
        gtm = sb("gtm", [P, NT, E1])
        eqm = sb("eqm", [P, NT, E1])
        eqb = sb("eqb", [P, NT, E0], BF16)
        cum = [sb("cum0", [P, NT, E1]), sb("cum1", [P, NT, E1])]
        cumb = sb("cumb", [P, NT, E0], BF16)
        cmp_ = sb("cmp", [P, NT, E0])
        cnt = sb("cnt", [P, E1], BF16)
        col = sb("col", [P, NT])
        col2 = sb("col2", [P, NT])
        xsq = XB[:, :, :]
        xn2 = sb("xn2", [P, NT])
        top8 = sb("top8", [P, NT, 8])
        thr = sb("thr", [P, E0])
        cand = sb("cand", [P, E0])
        keep = sb("keep", [P, E0])
        need = sb("need", [P, E0])
        gateT = XT[0:E1, :]

        W = sb("W", [P, E1, WROW])
        flat = prob[:, :, :, :].rearrange("p a b c -> p (a b c)")
        cuts = np.cumsum([0, 4 * W2AT, 4 * (P + E1), 2 * NF * P])
        part = [flat[:, int(a):int(b)] for a, b in zip(cuts[:-1], cuts[1:])]
        wc = part[0].rearrange("p (s f) -> p s f", s=4)
        xg = part[1].rearrange("p (s c) -> p s c", s=4)
        hid = part[2].rearrange("p (s f c) -> p s f c", s=2, f=NF)
        xsT = rt1[:, :, 0:P]
        yo = rt2[:, :, :].rearrange("p a (b c) -> p (a b) c", c=P)
        zero = sb("zero", [P, P + E1])

        triX = sb("triX", [P, P + 1], BF16)
        triC = sb("triC", [P, P + 1], BF16)
        same_e = sb("same_e", [P, P], BF16)
        before = sb("before", [P, P], BF16)
        pad_before = sb("pad_before", [P, P], BF16)
        first_row = sb("first_row", [P, P], BF16)
        cross = sb("cross", [P, P], BF16)
        shift = sb("shift", [P, P], BF16)
        dtok = sb("dtok", [P, 2])
        dexp = sb("dexp", [P, 2, P], F16)
        slot_in = sb("slot_in", [P, P], F16)
        tile_at = sb("tile_at", [P, NJT[1]])
        slot_at = sb("slot_at", [P, NJT[1]])
        pcol = sb("pcol", [P, 1])
        selz = sb("selz", [P, 1 + E1 * NT], BF16)
        nrow = sb("nrow", [P, 2], BF16)
        padi = sb("padi", [P, 2], I32)
        padf = sb("padf", [P, 2])
        padb = sb("padb", [P, 2], BF16)
        lo = sb("lo", [P, 2])
        padp = sb("padp", [P, 2])
        lom = sb("lom", [P, 2, NJT[1]])
        RH = sb("RH", [P, 2, P + 1], F16)
        indj = sb("indj", [P, 2, NJT[1]], F16)
        ej_out = sb("ej_out", [P, NJT[1] + 4], I32)
        ej_in = sb("ej_in", [P, NJT[1] + 4], I32)
        ind = sb("ind", [P, 2, 2, P], F16)
        hit = sb("hit", [P, 2, P])
        base_t = sb("base_t", [P, 2, 1])
        tok = sb("tok", [P, 2, 1])
        tpad = sb("tpad", [P, 2, 1])
        idx_all = sb("idx_all", [P, NJT[1]], I32)
        idx_g = sb("idx_g", [P, 4], I32)
        idx_s = sb("idx_s", [P, 4], I32)
        hold = sb("hold", [P, 4])

        bank = [ctx.enter_context(nc.psum_tensor(f"bank{i}", [P, 512], F32)) for i in range(8)]
        half = [b[:, :].bitcast(F16) for b in bank]
        S1B, STB, OTB, M5, M6, M7 = (0, 1), (2, 3), 4, 5, 6, 7

        consts_in = sem("consts_in")
        weights_in = sem("weights_in")
        x_in = sem("x_in")
        zeroed = sem("zeroed")
        xr_ready = [sem("xr_ready0"), sem("xr_ready1")]
        lat_done = sem("lat_done")
        lat_ready = sem("lat_ready")
        proj_done = sem("proj_done")
        qkv_ready = sem("qkv_ready")
        rope_step = sem("rope_step")
        split_step = sem("split_step")
        aug_ready = sem("aug_ready")
        vaug_ready = sem("vaug_ready")
        tq_done = sem("tq_done")
        tq_ready = sem("tq_ready")
        tk_done = sem("tk_done")
        kb_act = sem("kb_act")
        kb_dve = sem("kb_dve")
        bias_step = sem("bias_step")
        xb_ready = sem("xb_ready")
        s1_done = sem("s1_done")
        s1_used = sem("s1_used")
        m_step = sem("m_step")
        m_ready = sem("m_ready")
        tq2_done = sem("tq2_done")
        tq2_ready = sem("tq2_ready")
        st_done = sem("st_done")
        exp_done = sem("exp_done")
        av_done = sem("av_done")
        ot_ready = sem("ot_ready")
        bt_done = sem("bt_done")
        rden_ready = sem("rden_ready")
        on_ready = sem("on_ready")
        ox_done = sem("ox_done")
        ox_ready = sem("ox_ready")
        pj_done = sem("pj_done")
        y_ready = sem("y_ready")
        stats_ready = sem("stats_ready")
        var_ready = sem("var_ready")
        std_ready = sem("std_ready")
        rstd_ready = sem("rstd_ready")
        xn_ready = sem("xn_ready")
        xt_done = sem("xt_done")
        xt_ready = sem("xt_ready")
        wr_ready = sem("wr_ready")
        ksq_done = sem("ksq_done")
        br_ready = sem("br_ready")
        lg_done = sem("lg_done")
        rstep = sem("rstep")
        lsh_ready = sem("lsh_ready")
        lexp_ready = sem("lexp_ready")
        xsq_ready = sem("xsq_ready")
        cnt_ready = sem("cnt_ready")
        count_done = sem("count_done")
        tie_ready = sem("tie_ready")
        rank_done = sem("rank_done")
        gate_ready = sem("gate_ready")
        gt_done = sem("gt_done")
        gt_ready = sem("gt_ready")
        gb_done = sem("gb_done")
        acc0_ready = sem("acc0_ready")
        w_in = sem("w_in")
        sel_ready = sem("sel_ready")
        rh_done = sem("rh_done")
        nrow_ready = sem("nrow_ready")
        ne_done = sem("ne_done")
        pad_ready = sem("pad_ready")
        lo_done = sem("lo_done")
        indj_ready = sem("indj_ready")
        ej_done = sem("ej_done")
        ej_ready = sem("ej_ready")
        scratch_in = sem("scratch_in")
        xs_in = [sem("xs_in0"), sem("xs_in1")]
        back_in = sem("back_in")
        ind_ready = sem("ind_ready")
        list_done = sem("list_done")
        lstep = sem("lstep")
        idx_ready = sem("idx_ready")
        wc_ready = sem("wc_ready")
        gathered = [sem(f"gathered{i}") for i in range(4)]
        scattered = [sem(f"scattered{i}") for i in range(2)]
        held = sem("held")
        tp_done = sem("tp_done")
        xsT_ready = sem("xsT_ready")
        h_done = sem("h_done")
        gelu_done = sem("gelu_done")
        eo_done = sem("eo_done")
        yo_ready = sem("yo_ready")
        out_done = sem("out_done")

        N_CONST, N_WEIGHT = 20, 17
        def qk_of(lay, par):
            return (qk, rt1)[par] if lay == 1 else qk

        xs = [d["xs0"], d["xs1"]]
        sums_d = [[d["sum00"], d["sum01"]], [d["sum10"], d["sum11"]]]

        def wait_for(engine, semaphore, value):
            if not (isinstance(value, int) and value <= 0):
                engine.wait_ge(semaphore, value)

        def slot_steps(lay, engine, step):
            J = NJT[lay]
            for j in range(-4, 4):
                step(j, j % 4)
            with engine.Fori(1, J // 4 - 1) as jh:
                for s in range(4):
                    step(4 * jh + s, s)
            for j in range(J - 4, J + 1):
                step(j, j % 4)

        def tile_expert(engine, lay, table, at, s, regs):
            top = (E0, E1)[lay] - 1
            if isinstance(at, int):
                return engine.value_load(table[0:1, at:at + 1], min_val=0, max_val=top)
            if s == 0:
                engine.load(regs, table[0:1, bass.ds(at, 4)])
            return engine.snap(regs[s], min_val=0, max_val=top)

        def is_tile(lay, j):
            return not isinstance(j, int) or 0 <= j < NJT[lay]

        block = ctx.enter_context(nc.Block())

        @block.sync
        def _(sp):
            for n, dst in (("ident", ident), ("ident_h", ident_h), ("tri", tri), ("ropec", ropec),
                           ("ropes", ropes), ("bits", bits), ("triX", triX), ("triC", triC), ("same_e", same_e),
                           ("before", before), ("pad_before", pad_before), ("first_row", first_row),
                           ("shift", shift), ("cross", cross), ("dtok", dtok), ("dexp", dexp), ("slot_in", slot_in),
                           ("tile_at", tile_at), ("slot_at", slot_at), ("pcol", pcol)):
                sp.dma_start(dst[:], d["c_" + n]).then_inc(consts_in, 16)
            sp.dma_start(XT[:, :], d["xT"]).then_inc(x_in, 16)
            sp.dma_start(X[:, :, :], d["x"].rearrange("(t p) c -> p t c", p=P)).then_inc(x_in, 16)
            for dst, src in ((wqkv0, "wqkv0"), (braw, "braw"), (wo[0], "wo0"), (wo[1], "wo1"),
                             (wq1, "wq1"), (wl1, "wl1"), (bl1, "bl1"),
                             (wkv1, "wkv1"), (ws0, "ws0"), (bs0, "bs0"), (keysT, "keysT"), (rwT, "rwT"),
                             (rb, "rb"), (b2[0], "b2_0"), (b2[1], "b2_1")):
                sp.dma_start(dst[:], d[src]).then_inc(weights_in, 16)
            for lay in range(2):
                sp.dma_start(bo[lay][:, :], d[f"bo{lay}"].to_broadcast([P, P])).then_inc(weights_in, 16)

            def expert_weights(lay, e):
                src1 = d[f"w1_{lay}"][bass.ds(e, 1), :, :].rearrange("a p f -> p (a f)")
                src2 = d[f"b1_{lay}"][bass.ds(e, 1), :, :].rearrange("a p f -> p (a f)")
                src3 = d[f"w2_{lay}"][bass.ds(e, 1), :, :].rearrange("a (t p) c -> p (a t) c", p=P)
                at = bass.ds(e, 1)
                sp.dma_start(W[:, at, 0:WB].rearrange("p a f -> p (a f)"), src1).then_inc(w_in, 16)
                sp.dma_start(W[:, at, WB:W2AT].rearrange("p a f -> p (a f)"), src2).then_inc(w_in, 16)
                sp.dma_start(W[:, at, W2AT:WROW].rearrange("p a (t c) -> p (a t) c", c=P), src3).then_inc(w_in, 16)

            def batch_in(lay, b, slot):
                g = b + NB * lay
                if not (isinstance(b, int) and g < 2):
                    sp.wait_ge(proj_done, 2 * (g - 1))
                sp.dma_start(xr[:, slot, :], XT[:, bass.ds(b * L, L)]).then_inc(xr_ready[slot], 16)

            def batches_in(lay):
                n = (E0, E1)[lay] // (NB // 2)
                batch_in(lay, 0, 0)
                batch_in(lay, 1, 1)
                for e in range(n):
                    expert_weights(lay, e)
                with sp.Fori(1, NB // 2) as bh:
                    batch_in(lay, 2 * bh, 0)
                    batch_in(lay, 2 * bh + 1, 1)
                    for e in range(n):
                        expert_weights(lay, n * bh + e)

            def tokens_out(lay):
                E = (E0, E1)[lay]
                tiles = lambda ap: ap.rearrange("(t p) c -> p t c", p=P)
                sp.wait_ge(xn_ready, NT * (2 * lay + 1))
                sp.dma_start(tiles(xs[lay][0:TOK, 0:P]), X[:, :, :]).then_inc(xs_in[lay], 16)
                sp.wait_ge(gate_ready, lay + 1)
                sp.dma_start(tiles(xs[lay][0:TOK, P:P + E]), gate[:, :, 0:E]).then_inc(xs_in[lay], 16)
                sp.wait_ge(acc0_ready, 4 * (lay + 1))
                sp.dma_start(tiles(sums_d[lay][0][0:TOK, :]), Y[:, :, :]).then_inc(xs_in[lay], 16)
                for par, dst in ((0, Y), (1, XB)):
                    sp.wait_ge(scattered[par], 8 * (NJT[lay] + lay * NJT[0]))
                    sp.dma_start(dst[:, :, :], tiles(sums_d[lay][par][0:TOK, :])).then_inc(back_in, 16)

            sp.wait_ge(x_in, 32)
            batches_in(0)
            sp.wait_ge(zeroed, 2)
            for lay in range(2):
                sp.dma_start(xs[lay][TOK:ROWS, :], zero[:, 0:P + (E0, E1)[lay]]).then_inc(scratch_in, 16)
                sp.dma_start(sums_d[lay][0][TOK:ROWS, :], zero[:, 0:P]).then_inc(scratch_in, 16)
                sp.dma_start(sums_d[lay][1].rearrange("(t p) c -> p t c", p=P),
                             zero[:, 0:P].unsqueeze(1).to_broadcast([P, NT + 1, P])).then_inc(scratch_in, 16)
            tokens_out(0)
            sp.wait_ge(xt_ready, 8)
            batches_in(1)
            tokens_out(1)
            out_v = d["out"].rearrange("(t p) c -> p t c", p=P)
            sp.wait_ge(xn_ready, 4 * NT)
            sp.dma_start(out_v, X[:, :, :]).then_inc(out_done, 16)
            sp.wait_ge(out_done, 16)

        @block.gpsimd
        def _(pool):
            nc.gpsimd.memset(ones[:, :], 1.0)
            nc.gpsimd.memset(zero[:, :], 0.0)
            nc.gpsimd.memset(ones_b[:, :], 1.0)
            for i in range(2):
                nc.gpsimd.memset(aug[i][:, :, 0:H, NROW:HP], 0.0)
                nc.gpsimd.memset(aug[i][:, :, H:2 * H, NROW + 2:HP], 0.0)
                nc.gpsimd.memset(aug[i][:, :, H:2 * H, NROW:NROW + 2], MUNIT)
                nc.gpsimd.memset(vaug[i][:, :, :, HD + 1:HP], 0.0)
                nc.gpsimd.memset(KB[i][:, :, :, :].bitcast(I32), 0)
                last = nc.gpsimd.memset(vaug[i][:, :, :, HD:HD + 1], 1.0)
            last.then_inc(zeroed, 1)
            pool.wait_ge(zeroed, 2)

            v4 = lambda t: t[:, :, :].rearrange("p t (h x) -> p t h x", x=HD)

            def rope(lay, b, par):
                g = b + NB * lay
                pool.wait_ge(qkv_ready, 2 * g + 2)
                if True:
                    n = 2 * P // HD
                    cos = ropec[:, :, :].unsqueeze(2).to_broadcast([P, 2, n, HD])
                    sin = ropes[:, :, :].unsqueeze(2).to_broadcast([P, 2, n, HD])
                    hh = HD // 2
                    if not isinstance(b, int) or b > 0:
                        pool.wait_ge(aug_ready, g)
                    for t in range(2):
                        nc.gpsimd.tensor_tensor(v4(rt1)[:, t], v4(qk)[:, t], cos[:, t], ALU.mult).then_inc(rope_step, 1)
                        nc.gpsimd.tensor_tensor(v4(rt2)[:, t, :, 0:hh], v4(qk)[:, t, :, hh:HD], sin[:, t, :, 0:hh],
                                                ALU.mult).then_inc(rope_step, 1)
                        nc.gpsimd.tensor_tensor(v4(rt2)[:, t, :, hh:HD], v4(qk)[:, t, :, 0:hh], sin[:, t, :, hh:HD],
                                                ALU.mult).then_inc(rope_step, 1)
                    pool.wait_ge(rope_step, 7 * g + 6)
                    nc.gpsimd.tensor_tensor(rt1[:, :, :], rt1[:, :, :], rt2[:, :, :], ALU.add).then_inc(rope_step, 1)

            def build_aug(lay, b, par):
                g = b + NB * lay
                if lay == 0:
                    pool.wait_ge(rope_step, 7 * g + 7)
                else:
                    pool.wait_ge(qkv_ready, 2 * g + 2)
                if not (isinstance(b, int) and g < 2):
                    pool.wait_ge(tq2_done, 2 * (g - 1))
                A = aug[par]
                s4 = v4(qk_of(lay, par) if lay == 1 else rt1)
                one = ones[:, 0:HD].unsqueeze(1).unsqueeze(1).to_broadcast([P, H, 2, HD])
                for t in range(2):
                    qin = s4[:, t, 0:H, :].unsqueeze(2).to_broadcast([P, H, 2, HD])
                    kin = s4[:, t, H:2 * H, :].unsqueeze(2).to_broadcast([P, H, 2, HD])
                    qout = A[:, t, 0:H, 0:2 * HD].rearrange("p h (r x) -> p h r x", x=HD)
                    kout = A[:, t, H:2 * H, 0:4 * HD].rearrange("p h (r y) -> p h r y", r=2)[:, :, :, 0:HD]
                    if t == 0:
                        nc.gpsimd.tensor_tensor(qout, qin, one, ALU.mult).then_inc(split_step, 1)
                    else:
                        nc.gpsimd.tensor_scalar(qout, qin, 1.0, None, ALU.mult).then_inc(split_step, 1)
                    nc.gpsimd.tensor_scalar(kout, kin, 1.0, None, ALU.mult).then_inc(split_step, 1)
                nc.gpsimd.memset(A[:, :, 0:H, NROW:NROW + 2], 0.0)
                pool.wait_ge(split_step, 4 * g + 4)
                for t in range(2):
                    nc.gpsimd.tensor_tensor(A[:, t, 0:H, 2 * HD:3 * HD], s4[:, t, 0:H, :], A[:, t, 0:H, 0:HD],
                                            ALU.subtract)
                    last = nc.gpsimd.tensor_tensor(A[:, t, H:2 * H, HD:2 * HD], s4[:, t, H:2 * H, :],
                                                   A[:, t, H:2 * H, 0:HD], ALU.subtract)
                last.then_inc(aug_ready, 1)

            def build_vaug(lay, b, par):
                g = b + NB * lay
                if not (isinstance(b, int) and g < 2):
                    pool.wait_ge(av_done, 4 * (g - 1))
                v = vraw[par][:, :, :].rearrange("p t (h x) -> p t h x", x=HD)
                one = ones[:, 0:HD].unsqueeze(1).unsqueeze(1).to_broadcast([P, 2, H, HD])
                nc.gpsimd.tensor_tensor(vaug[par][:, :, :, 0:HD], v, one, ALU.mult).then_inc(vaug_ready, 1)

            def pool_iteration(lay, i, par):
                build_vaug(lay, i, par)
                if not (isinstance(i, int) and i > NB - 2):
                    build_aug(lay, i + 1, 1 - par)
                if lay == 0 and not (isinstance(i, int) and i > NB - 3):
                    rope(lay, i + 2, par)

            def pool_slots(lay, j, s):
                kd = j + NJT[0] * lay
                E = (E0, E1)[lay]
                if not (is_tile(lay, j - 1) or is_tile(lay, j + AHEAD)):
                    return
                if is_tile(lay, j + AHEAD):
                    pool.wait_ge(idx_ready, kd + AHEAD + 1)
                if is_tile(lay, j - 1):
                    pool.wait_ge(yo_ready, kd)
                    wait_for(pool, scattered[(s - 1) % 2], 8 * (kd - 1 - (s - 1) % 2))
                wait_for(pool, held, (NJT[0] + AHEAD + 1) * lay + j)
                nc.gpsimd.tensor_tensor(hold[:, s:s + 1], ones[:, 0:1], ones[:, 0:1], ALU.mult).then_inc(held, 1)
                if is_tile(lay, j - 1):
                    nc.gpsimd.indirect_dma_start(sums_d[lay][(s - 1) % 2],
                                                 bass.IndirectOffsetOnAxis(idx_s[:, (s - 1) % 4:(s - 1) % 4 + 1], 0),
                                                 yo[:, (s - 1) % 4, :], None,
                                                 compute_op=ALU.add).then_inc(scattered[(s - 1) % 2], 16)
                if is_tile(lay, j + AHEAD):
                    q = (s + AHEAD) % 4
                    nc.gpsimd.indirect_dma_start(xg[:, q, 0:P + E], None, xs[lay],
                                                 bass.IndirectOffsetOnAxis(idx_g[:, q:q + 1], 0)
                                                 ).then_inc(gathered[q], 16)

            pool.wait_ge(consts_in, 16 * N_CONST)
            pool.wait_ge(x_in, 32)
            pool.wait_ge(weights_in, 16 * N_WEIGHT)
            for lay in range(2):
                if lay == 1:
                    pool.wait_ge(xn_ready, 2 * NT)
                nc.gpsimd.tensor_tensor(XB[:, :, :], X[:, :, :], bo[lay][:, :].unsqueeze(1).to_broadcast([P, NT, P]),
                                        ALU.add).then_inc(xb_ready, 1)
                if lay == 0:
                    rope(lay, 0, 0)
                build_aug(lay, 0, 0)
                if lay == 0:
                    rope(lay, 1, 1)
                pool_iteration(lay, 0, 0)
                pool_iteration(lay, 1, 1)
                with pool.Fori(1, NB // 2 - 1) as ih:
                    i = 2 * ih
                    pool_iteration(lay, i, 0)
                    pool_iteration(lay, i + 1, 1)
                pool_iteration(lay, NB - 2, 0)
                pool_iteration(lay, NB - 1, 1)
                if lay == 1:
                    pool.wait_ge(xn_ready, 3 * NT)
                    nc.gpsimd.tensor_tensor(xsq[:, :, :], X[:, :, :], X[:, :, :], ALU.mult).then_inc(xsq_ready, 1)
                pool.wait_ge(scratch_in, 16 * 6)
                pool.wait_ge(xs_in[lay], 16 * 3)
                slot_steps(lay, pool, lambda j, s: pool_slots(lay, j, s))

        @block.tensor
        def _(pe):
            def s1(lay, i, par, u):
                g = i + NB * lay
                qt, j, qp = u // 8, (u % 8) // 2, u % 2
                if u == 0:
                    pe.wait_ge(tq_ready, g + 1)
                if u in (0, 4):
                    pe.wait_ge(kb_act, 2 * g + u // 4 + 1)
                    pe.wait_ge(kb_dve, 2 * g + u // 4 + 1)
                if not (isinstance(i, int) and g == 0 and u < 2):
                    pe.wait_ge(s1_used, 16 * g + u - 1)
                nc.tensor.matmul(bank[S1B[u % 2]][:, :], QT[par][:, j, P * qt:P * qt + P],
                                 KB[par][:, j, 2 * qp:2 * qp + 2, :], start=True, stop=True).then_inc(s1_done, 1)

            def st(lay, b, par, v):
                g = b + NB * lay
                j, q = v // 4, v % 4
                if v in (0, 8):
                    pe.wait_ge(tq2_ready, 2 * g + v // 8 + 1)
                if not (isinstance(b, int) and g == 0 and v < 2):
                    pe.wait_ge(exp_done, 16 * g + v - 1)
                for kt in range(2):
                    last = nc.tensor.matmul(bank[STB[v % 2]][:, L * kt:L * kt + L],
                                            KB[par][:, j, q, P * kt:P * kt + P], QT2[:, j, :],
                                            start=True, stop=True)
                last.then_inc(st_done, 1)

            def av(lay, b, par, j, kt):
                g = b + NB * lay
                if kt == 0:
                    if j == 0:
                        pe.wait_ge(vaug_ready, g + 1)
                    if j == 0 and not (isinstance(b, int) and g == 0):
                        pe.wait_ge(ot_ready, 2 * g)
                    if j == 2:
                        pe.wait_ge(ot_ready, 2 * g + 1)
                    pe.wait_ge(exp_done, 16 * g + 4 * j + 4)
                for q in range(4):
                    last = nc.tensor.matmul(bank[OTB][HP * q:HP * q + HP, L * (j % 2):L * (j % 2) + L],
                                            vaug[par][:, kt, 4 * j + q, :], prob[:, (4 * j + q) % 8, kt, :],
                                            start=(kt == 0), stop=(kt == 1))
                if kt == 1:
                    last.then_inc(av_done, 1)

            def bt(lay, b, pair):
                g = b + NB * lay
                pe.wait_ge(ot_ready, 2 * g + pair + 1)
                for t in range(2):
                    for jj in range(2):
                        at = P * (2 * t + jj)
                        last = nc.tensor.transpose(bank[M7][:, at:at + P], OT[:, pair, jj, P * t:P * t + P], ident[:, :])
                last.then_inc(bt_done, 1)

            def pe_iteration(lay, i, par, mx_on, soft_on, front_on, tail_on):
                g = i + NB * lay
                nxt = 1 - par
                for u in range(16):
                    if mx_on:
                        s1(lay, i, par, u)
                    if u < 2 and tail_on:
                        av(lay, i - 2, par, 3, u)
                    if u == 1 and soft_on:
                        pe.wait_ge(m_ready, g)
                        for j in range(NJ):
                            for t in range(2):
                                last = nc.tensor.transpose(half[M5][:, L * j + P * t:L * j + P * t + P],
                                                           aug[nxt][:, t, 4 * j:4 * j + 4, :], ident_h[:, :])
                            if j % 2:
                                last.then_inc(tq2_done, 1)
                    if soft_on:
                        for v in soft_units(u):
                            st(lay, i - 1, nxt, v)
                    if front_on and not (isinstance(i, int) and i > NB - 3):
                        if u == 2 and lay == 1:
                            front_latent(lay, i + 2, par)
                        if u == 3 + lay:
                            front_proj(lay, i + 2, par, 0)
                        if u == 5 + lay:
                            front_proj(lay, i + 2, par, 1)
                    if u == 3 and tail_on:
                        pe.wait_ge(on_ready, 2 * (g - 2) + 1)
                        bt(lay, i - 2, 1)
                    if u == 6 and tail_on:
                        pe.wait_ge(on_ready, 2 * (g - 2) + 2)
                        for t in range(2):
                            last = nc.tensor.transpose(bank[M7][:, P * t:P * t + P], on[:, t, :, :], ident[:, :])
                        last.then_inc(ox_done, 1)
                    if u == 9 and tail_on:
                        pe.wait_ge(ox_ready, g - 1)
                        for t in range(2):
                            last = nc.tensor.matmul(bank[M7][:, P * t:P * t + P], oxT[:, P * t:P * t + P], wo[lay][:, :],
                                                    start=True, stop=True)
                        last.then_inc(pj_done, 1)
                    if u in (7, 8) and soft_on:
                        av(lay, i - 1, nxt, 0, u - 7)
                    if u in (10, 11) and soft_on:
                        av(lay, i - 1, nxt, 1, u - 10)
                    if u == 12 and front_on:
                        query_transposes(lay, i + 1, nxt)
                    if u == 13 and front_on:
                        key_transposes(lay, i + 1, nxt)
                    if u == 14 and soft_on:
                        if tail_on:
                            pe.wait_ge(y_ready, g - 1)
                        bt(lay, i - 1, 0)
                    if u in (14, 15) and soft_on:
                        av(lay, i - 1, nxt, 2, u - 14)
            def m5_read(b, g):
                if isinstance(b, int) and b == 1:
                    pe.wait_ge(qkv_ready, 2 * g)
                elif not (isinstance(b, int) and g == 0):
                    pe.wait_ge(tq_ready, g - 1)
                    if not (isinstance(b, int) and b <= 2):
                        pe.wait_ge(tq2_ready, 2 * (g - 2))

            def front_latent(lay, b, par):
                g = b + NB * lay
                pe.wait_ge(xr_ready[par], 8 * (g - par) + 16)
                m5_read(b, g)
                nc.tensor.matmul(bank[M5][0:LAT, 0:L], wl1[:, :], xr[:, par, :], start=True,
                                 stop=True).then_inc(lat_done, 1)

            def front_proj(lay, b, par, t):
                g = b + NB * lay
                if lay == 1 and t == 0:
                    pe.wait_ge(lat_ready, b + 1)
                if lay == 0 and t == 0:
                    pe.wait_ge(xr_ready[par], 8 * (g - par) + 16)
                    m5_read(b, g)
                if t == 1:
                    pe.wait_ge(qkv_ready, 2 * g + 1)
                tok = xr[:, par, P * t:P * t + P]
                if lay == 0:
                    nc.tensor.matmul(bank[M5][:, 0:3 * P], tok, wqkv0[:, :], start=True, stop=False)
                    last = nc.tensor.matmul(bank[M5][:, 0:3 * P], ones_b[0:3, :], bsplit[:, 0:3 * P],
                                            start=False, stop=True)
                else:
                    nc.tensor.matmul(bank[M5][:, 0:P], tok, wq1[:, :], start=True, stop=False)
                    nc.tensor.matmul(bank[M5][:, 0:P], ones_b[0:3, :], bsplit[:, 3 * P:4 * P], start=False, stop=True)
                    last = nc.tensor.matmul(bank[M5][:, P:3 * P], latT[:, P * t:P * t + P], wkv1[:, :],
                                            start=True, stop=True)
                last.then_inc(proj_done, 1)

            def query_transposes(lay, b, par):
                g = b + NB * lay
                pe.wait_ge(aug_ready, g + 1)
                if not (isinstance(b, int) and b == NB - 1):
                    pe.wait_ge(qkv_ready, 2 * g + 4)
                for j in range(NJ):
                    for t in range(2):
                        last = nc.tensor.transpose(half[M5][:, L * j + P * t:L * j + P * t + P],
                                                   aug[par][:, t, 4 * j:4 * j + 4, :], ident_h[:, :])
                last.then_inc(tq_done, 1)

            def key_transposes(lay, b, par):
                g = b + NB * lay
                if not (isinstance(b, int) and b == 0):
                    pe.wait_ge(kb_act, 2 * g)
                    pe.wait_ge(kb_dve, 2 * g)
                for j in range(NJ):
                    for t in range(2):
                        last = nc.tensor.transpose(half[M6][:, L * j + P * t:L * j + P * t + P],
                                                   aug[par][:, t, H + 4 * j:H + 4 * j + 4, :], ident_h[:, :])
                last.then_inc(tk_done, 1)

            def turn(n):
                for c in range(4):
                    pe.wait_ge(xn_ready, NT * n + 4 * c + 4)
                    for t in range(4):
                        last = nc.tensor.transpose(bank[c][:, P * t:P * t + P], X[:, 4 * c + t, :], ident[:, :])
                    last.then_inc(xt_done, 1)

            def logits(lay, w, brow, E):
                pe.wait_ge(xt_ready, 8 * lay + 4)
                if lay == 1:
                    pe.wait_ge(wr_ready, 2)
                    nc.tensor.matmul(bank[6][0:1, 0:E1], ones[:, 0:1], ksq[:, :], start=True,
                                     stop=True).then_inc(ksq_done, 1)
                    pe.wait_ge(br_ready, 1)
                for t in range(NT):
                    nc.tensor.matmul(bank[5][:, E * t:E * t + E], XT[:, P * t:P * t + P], w[:, :], start=True, stop=False)
                    last = nc.tensor.matmul(bank[5][:, E * t:E * t + E], ones[0:1, :], brow[0:1, :], start=False, stop=True)
                last.then_inc(lg_done, 1)

            def gate_bias(lay, E):
                pe.wait_ge(gate_ready, lay + 1)
                for c in range(4):
                    for t in range(4):
                        last = nc.tensor.transpose(bank[c][0:E, P * t:P * t + P], gate[:, 4 * c + t, 0:E], ident[:, :])
                    last.then_inc(gt_done, 1)
                for c in range(4):
                    pe.wait_ge(gt_ready, 4 * lay + c + 1)
                    for t in range(4):
                        last = nc.tensor.matmul(bank[c][:, P * t:P * t + P], gateT[0:E, P * (4 * c + t):P * (4 * c + t + 1)],
                                                b2[lay][:, :], start=True, stop=True)
                    last.then_inc(gb_done, 1)

            def slot_table(lay):
                K = KT[lay]
                pe.wait_ge(sel_ready, lay + 1)
                for k in range(K):
                    nc.tensor.matmul(bank[4 + k][:, 0:P + 1], selz[:, 1 + P * k:1 + P * k + P], triX[:, :], start=True,
                                     stop=False)
                    last = nc.tensor.matmul(bank[4 + k][:, 0:P + 1], selz[:, P * k:P * k + P], triC[:, :],
                                            start=False, stop=True)
                last.then_inc(rh_done, 1)
                pe.wait_ge(nrow_ready, lay + 1)
                nc.tensor.matmul(bank[6][:, 0:K], same_e[:, :], nrow[:, 0:K], start=True, stop=True).then_inc(ne_done, 1)
                pe.wait_ge(pad_ready, lay + 1)
                for k in range(K):
                    at = slice(8 + k, 9 + k)
                    nc.tensor.matmul(bank[6][:, at], before[:, :], nrow[:, k:k + 1], start=True, stop=False)
                    nc.tensor.matmul(bank[6][:, at], pad_before[:, :], padb[:, k:k + 1], start=False, stop=(k == 0))
                    if k == 1:
                        nc.tensor.matmul(bank[6][:, at], ones_b[:, :], nrow[:, 0:1], start=False, stop=False)
                        nc.tensor.matmul(bank[6][:, at], first_row[:, :], padb[:, 0:1], start=False, stop=True)
                    at = slice(16 + k, 17 + k)
                    last = nc.tensor.matmul(bank[6][:, at], shift[:, :], padb[:, k:k + 1], start=True, stop=(k == 0))
                    if k == 1:
                        last = nc.tensor.matmul(bank[6][:, at], cross[:, :], padb[:, 0:1], start=False, stop=True)
                last.then_inc(lo_done, 1)
                pe.wait_ge(indj_ready, lay + 1)
                for k in range(K):
                    last = nc.tensor.matmul(bank[6][:, P:P + NJT[lay]], dexp[:, k, :], indj[:, k, 0:NJT[lay]],
                                            start=(k == 0), stop=(k == K - 1))
                last.then_inc(ej_done, 1)
                pe.wait_ge(ej_ready, lay + 1)

            pe_experts = [pe.alloc_register(f"pe_expert{i}") for i in range(4)]

            def pe_slots(lay, j, s):
                kd = j + NJT[0] * lay
                if is_tile(lay, j + AHEAD):
                    q = (s + AHEAD) % 2
                    pe.wait_ge(ind_ready, kd + AHEAD + 1)
                    wait_for(pe, idx_ready, kd + AHEAD - 1)
                    for k in range(KT[lay]):
                        last = nc.tensor.matmul(bank[6 + q][:, 0:P + 1], ind[:, q, k, :], RH[:, k, :], start=(k == 0),
                                                stop=(k == KT[lay] - 1))
                    last.then_inc(list_done, 1)
                if is_tile(lay, j):
                    pe.wait_ge(xsT_ready, kd + 1)
                    pe.wait_ge(wc_ready, kd + 1)
                    wait_for(pe, gelu_done, kd - 1)
                    for f in range(NF):
                        last = nc.tensor.matmul(bank[2 + s % 2][:, P * f:P * f + P], wc[:, s, P * f:P * f + P],
                                                xsT[:, s % 2, :], start=True, stop=True)
                    last.then_inc(h_done, 1)
                if is_tile(lay, j - 1):
                    q = (s - 1) % 2
                    e = tile_expert(pe, lay, ej_out, j, s, pe_experts)
                    pe.wait_ge(gelu_done, kd)
                    wait_for(pe, yo_ready, kd - 2)
                    for f in range(NF):
                        last = nc.tensor.matmul(bank[4 + q][:, 0:P], hid[:, q, f, :],
                                                W[:, bass.ds(e, 1), W2AT + P * f:W2AT + P * f + P],
                                                start=(f == 0), stop=(f == NF - 1))
                    last.then_inc(eo_done, 1)
                if is_tile(lay, j + 1):
                    q = (s + 1) % 4
                    pe.wait_ge(gathered[q], 4 * (kd + 1 - q) + 16)
                    wait_for(pe, xsT_ready, kd)
                    nc.tensor.transpose(bank[(s + 1) % 2][:, 0:P], xg[:, q, 0:P], ident[:, :]).then_inc(tp_done, 1)

            pe.wait_ge(consts_in, 16 * N_CONST)
            pe.wait_ge(weights_in, 16 * N_WEIGHT)
            pe.wait_ge(zeroed, 2)
            pe.wait_ge(bias_step, 7)
            for lay in range(2):
                if lay == 1:
                    pe.wait_ge(xt_ready, 8)
                if lay == 1:
                    front_latent(lay, 0, 0)
                front_proj(lay, 0, 0, 0)
                front_proj(lay, 0, 0, 1)
                if lay == 1:
                    front_latent(lay, 1, 1)
                front_proj(lay, 1, 1, 0)
                front_proj(lay, 1, 1, 1)
                query_transposes(lay, 0, 0)
                key_transposes(lay, 0, 0)
                pe_iteration(lay, 0, 0, True, False, True, False)
                pe_iteration(lay, 1, 1, True, True, True, False)
                with pe.Fori(1, NB // 2 - 1) as ih:
                    i = 2 * ih
                    pe_iteration(lay, i, 0, True, True, True, True)
                    pe_iteration(lay, i + 1, 1, True, True, True, True)
                pe_iteration(lay, NB - 2, 0, True, True, True, True)
                pe_iteration(lay, NB - 1, 1, True, True, False, True)
                pe_iteration(lay, NB, 0, False, True, False, True)
                pe_iteration(lay, NB + 1, 1, False, False, False, True)
                turn(2 * lay)
                if lay == 0:
                    logits(0, ws0, bs0, E0)
                    with pe.Fori(0, NBITS) as it:
                        pe.wait_ge(cnt_ready, it + 1)
                        nc.tensor.matmul(bank[6][:, 0:E0], ones_b[:, :], cnt[:, 0:E0], start=True,
                                         stop=True).then_inc(count_done, 1)
                    pe.wait_ge(cnt_ready, NBITS + 1)
                    nc.tensor.matmul(bank[6][:, 0:E0], ones_b[:, :], cnt[:, 0:E0], start=True,
                                     stop=True).then_inc(count_done, 1)
                    pe.wait_ge(tie_ready, 1)
                    nc.tensor.matmul(bank[7][:, 0:NT * E0], tri[:, :], eqb[:, :, :], start=True, stop=False)
                    nc.tensor.matmul(bank[7][:, 0:NT * E0], ones_b[:, :], cumb[:, :, :], start=False,
                                     stop=True).then_inc(rank_done, 1)
                else:
                    logits(1, wr1, br1, E1)
                slot_table(lay)
                gate_bias(lay, (E0, E1)[lay])
                pe.wait_ge(acc0_ready, 4 * lay + 4)
                pe.wait_ge(w_in, 48 * (E0 + E1 * lay))
                slot_steps(lay, pe, lambda j, s: pe_slots(lay, j, s))
                if lay == 0:
                    turn(1)

        @block.scalar
        def _(act):
            def act_iteration(lay, i, par, mx_on, soft_on, front_on, tail_on):
                g = i + NB * lay
                nxt = 1 - par
                for u in range(16):
                    if u == 1 and soft_on:
                        for part in range(2):
                            act.wait_ge(tq2_done, 2 * g)
                            if part == 0 and not (isinstance(i, int) and g == 1):
                                act.wait_ge(st_done, 16 * (g - 1))
                            at = slice(2 * part, 2 * part + 2)
                            nc.scalar.copy(QT2[:, at, :], half[M5][:, 2 * L * part:2 * L * part + 2 * L])\
                                .then_inc(tq2_ready, 1)
                    if soft_on:
                        for v in soft_units(u):
                            gb = g - 1
                            act.wait_ge(st_done, 16 * gb + v + 1)
                            if v % 4 == 0 and not (isinstance(i, int) and gb == 0 and v < 8):
                                act.wait_ge(av_done, 4 * gb + v // 4 - 1)
                            nc.scalar.activation(prob[:, v % 8, :, :], bank[STB[v % 2]][:, :], ACT.Exp,
                                                 scale=SCALE).then_inc(exp_done, 1)
                    if u == 1 and tail_on:
                        ot_evac(lay, i - 2, 1)
                    proj_on = front_on and not (isinstance(i, int) and i > NB - 3)
                    if u == 2 and proj_on and lay == 1:
                        lat_evac(i + 2)
                    if proj_on and u == 3 + lay:
                        front_evac(lay, i + 2, par, 0)
                    if proj_on and u == 5 + lay:
                        front_evac(lay, i + 2, par, 1)
                    if u == 7 and tail_on:
                        act.wait_ge(ox_done, g - 1)
                        nc.scalar.copy(oxT[:, :], bank[M7][:, 0:L]).then_inc(ox_ready, 1)
                    if u == 12 and soft_on:
                        ot_evac(lay, i - 1, 0)
                    if u == 14 and front_on:
                        keys_evac(lay, i + 1, nxt, 0)
                if front_on:
                    keys_evac(lay, i + 1, nxt, 1)

            def ot_evac(lay, b, pair):
                g = b + NB * lay
                act.wait_ge(av_done, 4 * g + 2 * pair + 2)
                if not (isinstance(b, int) and g == 0):
                    act.wait_ge(bt_done, 2 * g + pair - 1)
                nc.scalar.copy(OT[:, pair, :, :], bank[OTB][:, :]).then_inc(ot_ready, 1)

            def lat_evac(b):
                act.wait_ge(lat_done, b + 1)
                if not isinstance(b, int) or b > 0:
                    act.wait_ge(proj_done, 2 * (b + NB))
                nc.scalar.activation(latT[0:LAT, :], bank[M5][0:LAT, 0:L], ACT.Identity,
                                     bias=bl1[:, 0:1]).then_inc(lat_ready, 1)

            def keys_evac(lay, b, par, pair):
                g = b + NB * lay
                act.wait_ge(tk_done, g + 1)
                if not (isinstance(b, int) and g < 2):
                    act.wait_ge(st_done, 16 * (g - 2) + 8 * pair + 8)
                for q in range(2):
                    rows, js = slice(HP * q, HP * q + HP), slice(2 * pair, 2 * pair + 2)
                    last = nc.scalar.copy(KB[par][rows, js, q, :],
                                          half[M6][rows, 2 * L * pair:2 * L * pair + 2 * L].rearrange(
                                              "p (j k) -> p j k", j=2))
                last.then_inc(kb_act, 1)

            def front_evac(lay, b, par, t):
                g = b + NB * lay
                if t == 0 and lay == 0 and not (isinstance(b, int) and g == 0):
                    act.wait_ge(rope_step, 7 * g - 1)
                if t == 0 and lay == 1:
                    act.wait_ge(aug_ready, g - 1)
                if t == 0 and not (isinstance(b, int) and g < 2):
                    act.wait_ge(vaug_ready, g - 1)
                act.wait_ge(proj_done, 2 * g + t + 1)
                nc.scalar.copy(qk_of(lay, par)[:, t, :], bank[M5][:, 0:2 * P])
                nc.scalar.copy(vraw[par][:, t, :], bank[M5][:, 2 * P:3 * P]).then_inc(qkv_ready, 1)

            def std(n):
                act.wait_ge(var_ready, n + 1)
                nc.scalar.activation(rstd[:, :], mv[:, :, 1], ACT.Sqrt).then_inc(std_ready, 1)

            def turn_evac(n):
                for c in range(0, 4, 2):
                    act.wait_ge(xt_done, 4 * n + c + 1)
                    nc.scalar.copy(XT[:, CH * c:CH * c + CH], bank[c][:, :]).then_inc(xt_ready, 1)

            def gates_evac(lay, E):
                for c in range(4):
                    act.wait_ge(gt_done, 4 * lay + c + 1)
                    nc.scalar.copy(gateT[0:E, CH * c:CH * c + CH], bank[c][0:E, :]).then_inc(gt_ready, 1)

            act_experts = [act.alloc_register(f"act_expert{i}") for i in range(4)]

            def act_slots(lay, j, s):
                kd = j + NJT[0] * lay
                if is_tile(lay, j):
                    act.wait_ge(h_done, kd + 1)
                    wait_for(act, eo_done, kd - 1)
                    for f in range(NF):
                        last = nc.scalar.activation(hid[:, s % 2, f, :], bank[2 + s % 2][:, P * f:P * f + P],
                                                    (ACT.Gelu_apprx_tanh, ACT.Gelu)[lay],
                                                    bias=wc[:, s, WB + f:WB + f + 1])
                    last.then_inc(gelu_done, 1)
                if is_tile(lay, j + 1):
                    act.wait_ge(tp_done, kd + 2)
                    wait_for(act, h_done, kd)
                    nc.scalar.copy(xsT[:, (s + 1) % 2, :], bank[(s + 1) % 2][:, 0:P]).then_inc(xsT_ready, 1)
                if is_tile(lay, j + 2):
                    e = tile_expert(act, lay, ej_in, j + 4, s, act_experts)
                    nc.scalar.copy(wc[:, (s + 2) % 4, :], W[:, bass.ds(e, 1), 0:W2AT]).then_inc(wc_ready, 1)

            act.wait_ge(weights_in, 16 * N_WEIGHT)
            act.wait_ge(zeroed, 2)
            for lay in range(2):
                if lay == 1:
                    lat_evac(0)
                front_evac(lay, 0, 0, 0)
                front_evac(lay, 0, 0, 1)
                if lay == 1:
                    lat_evac(1)
                front_evac(lay, 1, 1, 0)
                front_evac(lay, 1, 1, 1)
                keys_evac(lay, 0, 0, 0)
                keys_evac(lay, 0, 0, 1)
                act_iteration(lay, 0, 0, True, False, True, False)
                act_iteration(lay, 1, 1, True, True, True, False)
                with act.Fori(1, NB // 2 - 1) as ih:
                    i = 2 * ih
                    act_iteration(lay, i, 0, True, True, True, True)
                    act_iteration(lay, i + 1, 1, True, True, True, True)
                act_iteration(lay, NB - 2, 0, True, True, True, True)
                act_iteration(lay, NB - 1, 1, True, True, False, True)
                act_iteration(lay, NB, 0, False, True, False, True)
                act_iteration(lay, NB + 1, 1, False, False, False, True)
                std(2 * lay)
                turn_evac(2 * lay)
                act.wait_ge(lsh_ready, lay + 1)
                E = (E0, E1)[lay]
                nc.scalar.activation(pr[:, :, 0:E], lg[:, :, 0:E], ACT.Exp).then_inc(lexp_ready, 1)
                gates_evac(lay, E)
                act.wait_ge(w_in, 48 * (E0 + E1 * lay))
                act.wait_ge(ej_ready, lay + 1)
                slot_steps(lay, act, lambda j, s: act_slots(lay, j, s))
                std(2 * lay + 1)
                if lay == 0:
                    turn_evac(1)

        @block.vector
        def _(dve):
            steps = [0]

            def step(ins):
                steps[0] += 1
                ins.then_inc(rstep, 1)
                dve.wait_ge(rstep, steps[0])

            def dve_iteration(lay, i, par, mx_on, soft_on, front_on, tail_on):
                g = i + NB * lay
                nxt = 1 - par
                for u in range(16):
                    if mx_on:
                        qt, h = u // 8, 2 * (u % 8)
                        dve.wait_ge(s1_done, 16 * g + u + 1)
                        m_at = mx[:, qt, h:h + 2]
                        nc.vector.tensor_reduce(m_at, bank[S1B[u % 2]][:, :].rearrange("p (j k) -> p j k", j=2), AX.X,
                                                ALU.max).then_inc(s1_used, 1)
                    if u == 4 and tail_on:
                        norm(lay, i - 2, 1)
                    if u == 10 and tail_on:
                        dve.wait_ge(pj_done, g - 1)
                        at = bass.ds(2 * (i - 2), 2)
                        nc.vector.tensor_tensor(Y[:, at, :], bank[M7][:, 0:2 * P].rearrange("p (t c) -> p t c", t=2),
                                                XB[:, at, :], ALU.add).then_inc(y_ready, 1)
                    if u == 13 and front_on:
                        q_evac(lay, i + 1, nxt)
                    if u == 14 and front_on:
                        keys_evac(lay, i + 1, nxt, 0)
                    if u == 15 and soft_on:
                        norm(lay, i - 1, 0)
                if mx_on:
                    dve.wait_ge(s1_used, 16 * g + 16)
                    nc.vector.tensor_scalar(mneg[:, :, :], mx[:, :, :], -1.0 / MUNIT, None, ALU.mult).then_inc(m_step, 1)
                    dve.wait_ge(m_step, 2 * g + 1)
                    nc.vector.tensor_copy(aug[par][:, :, 0:H, NROW], mneg[:, :, :]).then_inc(m_step, 1)
                    dve.wait_ge(m_step, 2 * g + 2)
                    nc.vector.tensor_tensor(aug[par][:, :, 0:H, NROW + 1], mneg[:, :, :], aug[par][:, :, 0:H, NROW],
                                            ALU.subtract).then_inc(m_ready, 1)
                if front_on:
                    keys_evac(lay, i + 1, nxt, 1)

            def keys_evac(lay, b, par, pair):
                g = b + NB * lay
                dve.wait_ge(tk_done, g + 1)
                if not (isinstance(b, int) and g < 2):
                    dve.wait_ge(st_done, 16 * (g - 2) + 8 * pair + 8)
                for q in range(2, 4):
                    rows, js = slice(HP * q, HP * q + HP), slice(2 * pair, 2 * pair + 2)
                    last = nc.vector.tensor_copy(KB[par][rows, js, q, :],
                                                 half[M6][rows, 2 * L * pair:2 * L * pair + 2 * L].rearrange(
                                                     "p (j k) -> p j k", j=2))
                last.then_inc(kb_dve, 1)

            def q_evac(lay, b, par):
                g = b + NB * lay
                dve.wait_ge(tq_done, g + 1)
                if not (isinstance(b, int) and g < 2):
                    dve.wait_ge(s1_done, 16 * (g - 1))
                nc.vector.tensor_copy(QT[par][:, :, :], half[M5]).then_inc(tq_ready, 1)

            def norm(lay, b, pair):
                g = b + NB * lay
                dve.wait_ge(bt_done, 2 * g + pair + 1)
                o = bank[M7][:, :].rearrange("p (h x) -> p h x", x=HP)
                nc.vector.reciprocal(rden[:, pair, :], o[:, :, HD]).then_inc(rden_ready, 1)
                dve.wait_ge(rden_ready, 2 * g + pair + 1)
                if not (isinstance(b, int) and g == 0):
                    dve.wait_ge(ox_done, g)
                for t in range(2):
                    last = nc.vector.tensor_tensor(on[:, t, 8 * pair:8 * pair + 8, :], o[:, 8 * t:8 * t + 8, 0:HD],
                                                   rden[:, pair, 8 * t:8 * t + 8].unsqueeze(2).to_broadcast([P, 8, HD]),
                                                   ALU.mult)
                last.then_inc(on_ready, 1)

            def layernorm(n, src):
                for t in range(NT):
                    last = nc.vector.bn_stats(stats[:, t, :], src[:, t, :])
                last.then_inc(stats_ready, 1)
                dve.wait_ge(stats_ready, 2 * n + 1)
                for t in range(NT):
                    last = nc.vector.bn_aggr(mv[:, t, :], stats[:, t, :])
                last.then_inc(stats_ready, 1)
                dve.wait_ge(stats_ready, 2 * n + 2)
                nc.vector.tensor_scalar(mv[:, :, 1], mv[:, :, 1], EPS, None, ALU.add).then_inc(var_ready, 1)
                dve.wait_ge(std_ready, n + 1)
                step(nc.vector.reciprocal(rstd[:, :], rstd[:, :]))
                step(nc.vector.scalar_tensor_tensor(out=nmr[:, :], in0=mv[:, :, 0], scalar=-1.0, in1=rstd[:, :],
                                                    op0=ALU.mult, op1=ALU.mult))
                for t in range(NT):
                    nc.vector.tensor_scalar(X[:, t, :], src[:, t, :], rstd[:, t:t + 1], nmr[:, t:t + 1], ALU.mult,
                                            ALU.add).then_inc(xn_ready, 1)

            def turn_evac(n):
                for c in range(1, 4, 2):
                    dve.wait_ge(xt_done, 4 * n + c + 1)
                    nc.vector.tensor_copy(XT[:, CH * c:CH * c + CH], bank[c][:, :]).then_inc(xt_ready, 1)

            def bc(ap, E):
                return ap.unsqueeze(2).to_broadcast([P, NT, E])

            def select_first_layer():
                E = E0
                lgv, prv, gv = lg[:, :, 0:E], pr[:, :, 0:E], gate[:, :, 0:E]
                by_e = lambda ap: ap.rearrange("p t e -> p e t")
                dve.wait_ge(lg_done, 1)
                raw = bank[5][:, 0:NT * E].rearrange("p (t e) -> p t e", e=E)
                step(nc.vector.tensor_reduce(col[:, :], raw, AX.X, ALU.max))
                nc.vector.tensor_tensor(lgv, raw, bc(col[:, :], E), ALU.subtract).then_inc(lsh_ready, 1)
                dve.wait_ge(lexp_ready, 1)
                step(nc.vector.tensor_reduce(col2[:, :], prv, AX.X, ALU.add))
                step(nc.vector.reciprocal(col2[:, :], col2[:, :]))
                step(nc.vector.tensor_tensor(prv, prv, bc(col2[:, :], E), ALU.mult))
                step(nc.vector.memset(thr[:, :], 0.0))
                base = steps[0]
                with dve.Fori(0, NBITS) as it:
                    n = base + 5 * it
                    nc.vector.tensor_tensor(cand[:, :].bitcast(I32), thr[:, :].bitcast(I32),
                                            bits[:, bass.ds(it * E, E)], ALU.bitwise_or).then_inc(rstep, 1)
                    dve.wait_ge(rstep, n + 1)
                    nc.vector.tensor_tensor(cmp_[:, :, :], prv, cand[:, :].unsqueeze(1).to_broadcast([P, NT, E]),
                                            ALU.is_ge).then_inc(rstep, 1)
                    dve.wait_ge(rstep, n + 2)
                    with nc.allow_low_precision(reason="counts up to 16"):
                        nc.vector.tensor_reduce(cnt[:, 0:E], by_e(cmp_[:, :, :]), AX.X, ALU.add).then_inc(cnt_ready, 1)
                    dve.wait_ge(count_done, it + 1)
                    nc.vector.scalar_tensor_tensor(out=keep[:, :], in0=bank[6][:, 0:E], scalar=float(CAP),
                                                   in1=cand[:, :], op0=ALU.is_ge, op1=ALU.mult).then_inc(rstep, 1)
                    dve.wait_ge(rstep, n + 3)
                    nc.vector.tensor_tensor(thr[:, :], thr[:, :], keep[:, :], ALU.max).then_inc(rstep, 2)
                    dve.wait_ge(rstep, n + 5)
                steps[0] = base + 5 * NBITS
                tb = thr[:, :].unsqueeze(1).to_broadcast([P, NT, E])
                step(nc.vector.tensor_tensor(gtm[:, :, 0:E], prv, tb, ALU.is_gt))
                step(nc.vector.tensor_tensor(eqm[:, :, 0:E], prv, tb, ALU.is_equal))
                with nc.allow_low_precision(reason="counts up to 16"):
                    nc.vector.tensor_reduce(cnt[:, 0:E], by_e(gtm[:, :, 0:E]), AX.X, ALU.add).then_inc(cnt_ready, 1)
                step(nc.vector.tensor_copy(eqb[:, :, :], eqm[:, :, 0:E]))
                step(nc.vector.memset(cum[0][:, 0:1, 0:E], 0.0))
                step(nc.vector.tensor_copy(cum[0][:, 1:NT, 0:E], eqm[:, 0:NT - 1, 0:E]))
                a, sh = 0, 1
                while sh < NT:
                    step(nc.vector.tensor_copy(cum[1 - a][:, 0:sh, 0:E], cum[a][:, 0:sh, 0:E]))
                    step(nc.vector.tensor_tensor(cum[1 - a][:, sh:NT, 0:E], cum[a][:, sh:NT, 0:E],
                                                 cum[a][:, 0:NT - sh, 0:E], ALU.add))
                    a, sh = 1 - a, 2 * sh
                nc.vector.tensor_copy(cumb[:, :, :], cum[a][:, :, 0:E]).then_inc(tie_ready, 1)
                dve.wait_ge(count_done, NBITS + 1)
                step(nc.vector.tensor_scalar(need[:, :], bank[6][:, 0:E], -1.0, float(CAP), ALU.mult, ALU.add))
                dve.wait_ge(rank_done, 1)
                rank = bank[7][:, 0:NT * E].rearrange("p (t e) -> p t e", e=E)
                step(nc.vector.tensor_tensor(cmp_[:, :, :], rank, need[:, :].unsqueeze(1).to_broadcast([P, NT, E]),
                                             ALU.is_le))
                step(nc.vector.tensor_tensor(cmp_[:, :, :], cmp_[:, :, :], eqm[:, :, 0:E], ALU.mult))
                step(nc.vector.tensor_tensor(gtm[:, :, 0:E], gtm[:, :, 0:E], cmp_[:, :, :], ALU.add))
                nc.vector.tensor_copy(selz[:, 1:1 + E * NT].rearrange("p (e t) -> p e t", t=NT),
                                      by_e(gtm[:, :, 0:E])).then_inc(sel_ready, 1)
                nc.vector.tensor_tensor(gv, gtm[:, :, 0:E], prv, ALU.mult).then_inc(gate_ready, 1)

            def select_second_layer():
                E = E1
                dve.wait_ge(xsq_ready, 1)
                step(nc.vector.tensor_reduce(xn2[:, :], xsq[:, :, :], AX.X, ALU.add))
                dve.wait_ge(lg_done, 2)
                raw = bank[5][:, 0:NT * E].rearrange("p (t e) -> p t e", e=E)
                step(nc.vector.tensor_tensor(cum[0][:, :, :], raw, bc(xn2[:, :], E), ALU.subtract))
                for t in range(NT):
                    last = nc.vector.max(top8[:, t, :], cum[0][:, t, :])
                step(last)
                nc.vector.tensor_tensor(lg[:, :, :], cum[0][:, :, :], bc(top8[:, :, 0], E),
                                        ALU.subtract).then_inc(lsh_ready, 1)
                step(nc.vector.tensor_tensor(gtm[:, :, :], cum[0][:, :, :], bc(top8[:, :, TOPK - 1], E), ALU.is_gt))
                step(nc.vector.tensor_tensor(eqm[:, :, :], cum[0][:, :, :], bc(top8[:, :, TOPK - 1], E), ALU.is_equal))
                step(nc.vector.tensor_reduce(col[:, :], gtm[:, :, :], AX.X, ALU.add))
                step(nc.vector.tensor_scalar(col[:, :], col[:, :], -1.0, float(TOPK), ALU.mult, ALU.add))
                step(nc.vector.tensor_copy(cum[0][:, :, :], eqm[:, :, :]))
                a, sh = 0, 1
                while sh < E:
                    step(nc.vector.tensor_copy(cum[1 - a][:, :, 0:sh], cum[a][:, :, 0:sh]))
                    step(nc.vector.tensor_tensor(cum[1 - a][:, :, sh:E], cum[a][:, :, sh:E], cum[a][:, :, 0:E - sh],
                                                 ALU.add))
                    a, sh = 1 - a, 2 * sh
                step(nc.vector.tensor_tensor(cum[1 - a][:, :, :], cum[a][:, :, :], bc(col[:, :], E), ALU.is_le))
                step(nc.vector.tensor_tensor(eqm[:, :, :], eqm[:, :, :], cum[1 - a][:, :, :], ALU.mult))
                step(nc.vector.tensor_tensor(gtm[:, :, :], gtm[:, :, :], eqm[:, :, :], ALU.add))
                nc.vector.tensor_copy(selz[:, 1:1 + E * NT].rearrange("p (e t) -> p e t", t=NT),
                                      gtm[:, :, :].rearrange("p t e -> p e t")).then_inc(sel_ready, 1)
                dve.wait_ge(sel_ready, 2)
                dve.wait_ge(lexp_ready, 2)
                step(nc.vector.tensor_tensor(gtm[:, :, :], gtm[:, :, :], pr[:, :, :], ALU.mult))
                step(nc.vector.tensor_reduce(col2[:, :], gtm[:, :, :], AX.X, ALU.add))
                step(nc.vector.reciprocal(col2[:, :], col2[:, :]))
                nc.vector.tensor_tensor(gate[:, :, :], gtm[:, :, :], bc(col2[:, :], E), ALU.mult).then_inc(gate_ready, 1)

            def sums(lay):
                for c in range(4):
                    dve.wait_ge(gb_done, 4 * lay + c + 1)
                    nc.vector.tensor_tensor(Y[:, 4 * c:4 * c + 4, :], bank[c][:, :].rearrange("p (t c) -> p t c", c=P),
                                            X[:, 4 * c:4 * c + 4, :], ALU.add).then_inc(acc0_ready, 1)

            def slot_table(lay):
                K, J = KT[lay], NJT[lay]
                dve.wait_ge(rh_done, lay + 1)
                for k in range(K):
                    last = nc.vector.tensor_copy(nrow[:, k:k + 1], bank[4 + k][:, P:P + 1])
                last.then_inc(nrow_ready, 1)
                dve.wait_ge(ne_done, lay + 1)
                step(nc.vector.tensor_scalar(padf[:, 0:K], bank[6][:, 0:K], -1.0, float(TOK), ALU.mult, ALU.add))
                step(nc.vector.tensor_copy(padi[:, 0:K], padf[:, 0:K]))
                step(nc.vector.tensor_scalar(padi[:, 0:K], padi[:, 0:K], P - 1, None, ALU.bitwise_and))
                nc.vector.tensor_copy(padb[:, 0:K], padi[:, 0:K]).then_inc(pad_ready, 1)
                dve.wait_ge(lo_done, lay + 1)
                nc.vector.tensor_copy(lo[:, 0:K], bank[6][:, 8:8 + K])
                step(nc.vector.tensor_copy(padp[:, 0:K], bank[6][:, 16:16 + K]))
                step(nc.vector.tensor_tensor(lom[:, 0:K, 0:J], lo[:, 0:K].unsqueeze(2).to_broadcast([P, K, J]),
                                             tile_at[:, 0:J].unsqueeze(1).to_broadcast([P, K, J]), ALU.subtract))
                nc.vector.tensor_scalar(indj[:, 0:K, 0:J], lom[:, 0:K, 0:J], 0.0, None, ALU.is_le).then_inc(indj_ready, 1)
                for k in range(K):
                    nc.vector.tensor_scalar(RH[:, k, 0:P], bank[4 + k][:, 0:P], padp[:, k:k + 1], None, ALU.add)
                step(nc.vector.tensor_copy(RH[:, 0:K, P], dtok[:, 0:K]))
                dve.wait_ge(ej_done, lay + 1)
                nc.vector.tensor_copy(ej_in[:, 2:2 + J], bank[6][:, P:P + J])
                nc.vector.tensor_copy(ej_out[:, 1:1 + J], bank[6][:, P:P + J]).then_inc(ej_ready, 1)
                dve.wait_ge(ej_ready, lay + 1)

            dve_experts = [dve.alloc_register(f"dve_expert{i}") for i in range(4)]

            def dve_slots(lay, j, s):
                kd = j + NJT[0] * lay
                E = (E0, E1)[lay]
                if is_tile(lay, j + AHEAD + 1):
                    q = (s + AHEAD + 1) % 2
                    wait_for(dve, list_done, kd + AHEAD)
                    for k in range(KT[lay]):
                        last = nc.vector.tensor_scalar(ind[:, q, k, :], slot_in[:, :],
                                                       lom[:, k, bass.ds(j + AHEAD + 1, 1)], None, ALU.is_ge)
                    last.then_inc(ind_ready, 1)
                if is_tile(lay, j + AHEAD):
                    q, at = (s + AHEAD) % 2, bass.ds(j + AHEAD, 1)
                    k2 = 2 * (kd + AHEAD)
                    dve.wait_ge(list_done, kd + AHEAD + 1)
                    nc.vector.tensor_scalar(hit[:, q, :], bank[6 + q][:, 0:P], slot_at[:, at], bank[6 + q][:, P:P + 1],
                                            ALU.is_le, ALU.add, accum_out=tok[:, q, :]).then_inc(lstep, 1)
                    dve.wait_ge(lstep, k2 + 1)
                    nc.vector.scalar_tensor_tensor(out=tpad[:, q, :], in0=tok[:, q, :], scalar=float(DUMMY),
                                                   in1=pcol[:, :], op0=ALU.is_ge, op1=ALU.mult).then_inc(lstep, 1)
                    dve.wait_ge(lstep, k2 + 2)
                    nc.vector.tensor_tensor(idx_all[:, at], tok[:, q, :], tpad[:, q, :], ALU.add)
                    nc.vector.tensor_tensor(idx_g[:, (s + AHEAD) % 4:(s + AHEAD) % 4 + 1], tok[:, q, :], tpad[:, q, :],
                                            ALU.add).then_inc(idx_ready, 1)
                if is_tile(lay, j - 1):
                    q = (s - 1) % 2
                    e = tile_expert(dve, lay, ej_out, j, s, dve_experts)
                    wait_for(dve, scattered[q], 8 * (kd - 1 - q) - 16)
                    nc.vector.tensor_copy(idx_s[:, (s - 1) % 4:(s - 1) % 4 + 1], idx_all[:, bass.ds(j - 1, 1)])
                    dve.wait_ge(eo_done, kd)
                    nc.vector.tensor_scalar(yo[:, (s - 1) % 4, :], bank[4 + q][:, 0:P], xg[:, (s - 1) % 4, bass.ds(e + P, 1)], None,
                                            ALU.mult).then_inc(yo_ready, 1)

            nc.vector.memset(selz[:, 0:1], 0.0)
            nc.vector.memset(latT[LAT:LAT + 1, :], 1.0).then_inc(zeroed, 1)
            dve.wait_ge(weights_in, 16 * N_WEIGHT)
            dve.wait_ge(consts_in, 16 * N_CONST)
            dve.wait_ge(zeroed, 2)
            dve.wait_ge(x_in, 32)
            nc.vector.tensor_tensor(ksq[:, :], keysT[:, :], keysT[:, :], ALU.mult).then_inc(wr_ready, 1)
            nc.vector.scalar_tensor_tensor(out=wr1[:, :], in0=keysT[:, :], scalar=2.0, in1=rwT[:, :], op0=ALU.mult,
                                           op1=ALU.add).then_inc(wr_ready, 1)
            def bias_next(ins, n):
                ins.then_inc(bias_step, 1)
                dve.wait_ge(bias_step, n)

            bias_next(nc.vector.tensor_copy(bpart[0][:, :], braw[:, :]), 1)
            bias_next(nc.vector.tensor_tensor(brest[:, :], braw[:, :], bpart[0][:, :], ALU.subtract), 2)
            bias_next(nc.vector.tensor_copy(bpart[1][:, :], brest[:, :]), 3)
            bias_next(nc.vector.tensor_tensor(bpart[2][:, :], brest[:, :], bpart[1][:, :], ALU.subtract), 4)
            bias_next(nc.vector.tensor_scalar(brest[:, :], bpart[0][:, :], ident[0:3, 0:1], None, ALU.mult), 5)
            for r in range(1, 3):
                out = bsplit if r == 2 else brest
                bias_next(nc.vector.scalar_tensor_tensor(out=out[:, :], in0=bpart[r][:, :], scalar=ident[0:3, r:r + 1],
                                                         in1=brest[:, :], op0=ALU.mult, op1=ALU.add), 5 + r)
            for lay in range(2):
                q_evac(lay, 0, 0)
                keys_evac(lay, 0, 0, 0)
                keys_evac(lay, 0, 0, 1)
                dve.wait_ge(xb_ready, lay + 1)
                dve_iteration(lay, 0, 0, True, False, True, False)
                dve_iteration(lay, 1, 1, True, True, True, False)
                with dve.Fori(1, NB // 2 - 1) as ih:
                    i = 2 * ih
                    dve_iteration(lay, i, 0, True, True, True, True)
                    dve_iteration(lay, i + 1, 1, True, True, True, True)
                dve_iteration(lay, NB - 2, 0, True, True, True, True)
                dve_iteration(lay, NB - 1, 1, True, True, False, True)
                dve_iteration(lay, NB, 0, False, True, False, True)
                dve_iteration(lay, NB + 1, 1, False, False, False, True)
                dve.wait_ge(y_ready, NB * (lay + 1))
                layernorm(2 * lay, Y)
                turn_evac(2 * lay)
                if lay == 0:
                    select_first_layer()
                else:
                    dve.wait_ge(ksq_done, 1)
                    nc.vector.tensor_tensor(br1[:, :], rb[:, :], bank[6][0:1, 0:E1], ALU.subtract).then_inc(br_ready, 1)
                    select_second_layer()
                slot_table(lay)
                sums(lay)
                slot_steps(lay, dve, lambda j, s: dve_slots(lay, j, s))
                dve.wait_ge(back_in, 32 * (lay + 1))
                step(nc.vector.tensor_tensor(Y[:, :, :], Y[:, :, :], XB[:, :, :], ALU.add))
                layernorm(2 * lay + 1, Y)
                if lay == 0:
                    turn_evac(1)


def shape_constants():
    inv = (np.float32(1.0) / np.float32(10000.0) ** (np.arange(0, HD, 2, dtype=np.float32) / np.float32(HD))).astype(np.float32)
    ang = np.arange(L, dtype=np.float32)[:, None] * inv[None, :]
    cos, sin = np.cos(ang).astype(np.float32), np.sin(ang).astype(np.float32)
    lay = lambda a: np.ascontiguousarray(a.reshape(2, P, HD).transpose(1, 0, 2))
    bit = (1 << np.arange(NBITS - 1, -1, -1)).astype(np.int32)
    wide = lambda v: np.tile(v.astype(np.float32)[None, :], (P, 1))
    rows = np.arange(E1 * NT)
    first = (rows % NT == 0) & (rows > 0)
    return {
        "c_ident": np.eye(P, dtype=np.float32),
        "c_ident_h": np.eye(P, dtype=np.float16),
        "c_slot_in": wide(np.arange(P)).astype(np.float16),
        "c_tile_at": wide(P * np.arange(NJT[1])),
        "c_slot_at": wide(P * np.arange(NJT[1])) + np.arange(P, dtype=np.float32)[:, None],
        "c_pcol": np.arange(P, dtype=np.float32)[:, None],
        "c_dtok": np.ascontiguousarray(np.where(first, -P * (NT - 1), np.where(rows > 0, P, 0)).astype(np.float32).reshape(2, P).T),
        "c_dexp": np.ascontiguousarray(np.repeat(first.astype(np.float16).reshape(2, P).T[:, :, None], P, axis=2)),
        "c_bits": np.tile(np.repeat(bit, E0)[None, :], (P, 1)),
        "c_ropec": lay(np.concatenate([cos, cos], 1)),
        "c_ropes": lay(np.concatenate([-sin, sin], 1)),
    }


def kernel(**inputs):
    import ml_dtypes
    import concourse.bacc as _bacc
    from concourse.bass_utils import run_bass_kernel_spmd as _run

    a = {k: np.asarray(v) for k, v in inputs.items()}
    x = a["L0_attn_x"].reshape(TOK, P)
    row = lambda v: v.reshape(1, -1)
    arrays = {
        "x": x, "xT": x.T,
        "wqkv0": np.concatenate([a["L0_attn_Wq"].T, a["L0_attn_Wk"].T, a["L0_attn_Wv"].T], 1),
        "braw": np.repeat(row(np.concatenate([a["L0_attn_bq"], a["L0_attn_bk"], a["L0_attn_bv"], a["L1_attn_bq"]])),
                          3, axis=0),
        "wo0": a["L0_attn_Wo"].T, "bo0": row(a["L0_attn_bo"]),
        "wo1": a["L1_attn_Wo"], "bo1": row(a["L1_attn_bo"]),
        "wq1": a["L1_attn_Wq"],
        "wl1": a["L1_attn_Wl"], "bl1": a["L1_attn_bl"].reshape(LAT, 1),
        "wkv1": np.concatenate([np.concatenate([a["L1_attn_Wk"], a["L1_attn_Wv"]], 1),
                                row(np.concatenate([a["L1_attn_bk"], a["L1_attn_bv"]]))], 0),
        "ws0": a["L0_ffn_Ws"], "bs0": row(a["L0_ffn_bs"]),
        "keysT": a["L1_ffn_keys"].T, "rwT": a["L1_ffn_rw"].T, "rb": row(a["L1_ffn_rb"]),
        "w1_0": a["L0_ffn_W1"], "w2_0": a["L0_ffn_W2"],
        "w1_1": a["L1_ffn_w1"].transpose(0, 2, 1), "w2_1": a["L1_ffn_w2"].transpose(0, 2, 1),
        "b1_0": a["L0_ffn_b1"].reshape(E0, NF, P).transpose(0, 2, 1),
        "b1_1": a["L1_ffn_b1"].reshape(E1, NF, P).transpose(0, 2, 1),
        "b2_0": a["L0_ffn_b2"], "b2_1": a["L1_ffn_b2"],
    }
    arrays = {k: np.ascontiguousarray(v) for k, v in arrays.items()}
    consts = shape_constants()
    k, r = np.arange(P)[:, None], np.arange(P)[None, :]
    zero, one = np.zeros((P, 1)), np.ones((P, 1))
    flags = {
        "tri": k <= r, "triX": np.concatenate([k <= r, one], 1), "triC": np.concatenate([k > r, zero], 1),
        "same_e": k // NT == r // NT, "before": k < r, "pad_before": (k % NT == 0) & (k // NT < r // NT),
        "first_row": (k % NT == 0) & (r >= 0), "shift": (k == r - 1) & (r % NT == 0), "cross": (k == P - 1) & (r == 0),
    }
    for name, v in flags.items():
        consts["c_" + name] = v.astype(ml_dtypes.bfloat16)
    arrays.update(consts)
    nc = _bacc.Bacc("TRN2", target_bir_lowering=False, num_devices=1)
    d = {}
    for name, v in arrays.items():
        d[name] = nc.dram_tensor("in_" + name, v.shape, mybir.dt.from_np(v.dtype), kind="ExternalInput").ap()
    for lay, E in ((0, E0), (1, E1)):
        d[f"xs{lay}"] = nc.dram_tensor(f"xs{lay}", (ROWS, P + E), F32, kind="Internal").ap()
        for par in range(2):
            d[f"sum{lay}{par}"] = nc.dram_tensor(f"sum{lay}{par}", (ROWS, P), F32, kind="Internal").ap()
    d["out"] = nc.dram_tensor("out", (TOK, P), F32, kind="ExternalOutput").ap()
    program(nc, d)
    r = _run(nc, [{"in_" + k: v for k, v in arrays.items()}], core_ids=[0])
    return np.asarray(r.results[0]["out"]).reshape(NB, L, P)
```

```python
from contextlib import ExitStack

import numpy as np

import concourse.bass as bass
from concourse import mybir

F32 = mybir.dt.float32
F16 = mybir.dt.float16
BF16 = mybir.dt.bfloat16
I32 = mybir.dt.int32
ALU = mybir.AluOpType
ACT = mybir.ActivationFunctionType
AX = mybir.AxisListType

P = 128
TOK = 2048
NT = TOK // P
L = 256
NB = TOK // L
H = 16
HD = 8
HP = 32
NJ = H // 4
NROW = 3 * HD
MUNIT = 64.0
SCALE = float(np.float32(1.0) / np.sqrt(np.float32(HD)))
EPS = 1e-5
E0, E1 = 8, 16
F = 512
NF = F // P
CAP = TOK // E0
TOPK = 4
LAT = 32
CH = 512
NROWS = [E0 * NT, E1 * NT]
KT = [n // P for n in NROWS]
NJT = [E0 * CAP // P, TOK * TOPK // P + E1]
DUMMY = TOK
ROWS = TOK + P
WB, W2AT = F, F + NF
WROW = W2AT + F
AHEAD = 4
NBITS = 30


def soft_units(u):
    return {2: [0], 3: [1], 4: [2], 5: [3], 6: [4], 7: [5, 6], 8: [7], 9: [8], 10: [9], 11: [10, 11],
            12: [12], 13: [13], 14: [14], 15: [15]}.get(u, [])


def program(nc, d):
    ctx = ExitStack()
    with ctx:
        def sb(name, shape, dt=F32):
            return ctx.enter_context(nc.sbuf_tensor(name, shape, dt))

        def sem(name):
            return ctx.enter_context(nc.semaphore(name))

        ident = sb("ident", [P, P])
        ident_h = sb("ident_h", [P, P], F16)
        tri = sb("tri", [P, P], BF16)
        ones_b = sb("ones_b", [P, P], BF16)
        ones = sb("ones", [P, P])
        bits = sb("bits", [P, NBITS // 2 * 3 * E0], I32)
        ropec = sb("ropec", [P, 2, HD])
        ropes = sb("ropes", [P, 2, HD])
        wqkv0 = sb("wqkv0", [P, 3 * P])
        braw = sb("braw", [3, 4 * P])
        bsplit = sb("bsplit", [3, 4 * P], BF16)
        bpart = [sb(f"bpart{i}", [3, 4 * P], BF16) for i in range(3)]
        brest = sb("brest", [3, 4 * P])
        wo = [sb("wo0", [P, P]), sb("wo1", [P, P])]
        bo = [sb("bo0", [P, P]), sb("bo1", [P, P])]
        XB = sb("XB", [P, NT, P])
        wq1 = sb("wq1", [P, P])
        wl1 = sb("wl1", [P, LAT])
        bl1 = sb("bl1", [LAT, 1])
        wkv1 = sb("wkv1", [LAT + 1, 2 * P])
        ws0 = sb("ws0", [P, E0])
        bs0 = sb("bs0", [P, E0])
        keysT = sb("keysT", [P, E1])
        rwT = sb("rwT", [P, E1])
        rb = sb("rb", [P, E1])
        wr1 = sb("wr1", [P, E1])
        ksq = sb("ksq", [P, E1])
        br1 = sb("br1", [P, E1])
        b2 = [sb("b2_0", [E0, P]), sb("b2_1", [E1, P])]

        X = sb("X", [P, NT, P])
        XT = sb("XT", [P, TOK])
        Y = sb("Y", [P, NT, P])
        stats = sb("stats", [P, NT, 6])
        mv = sb("mv", [P, NT, 2])
        rstd = sb("rstd", [P, NT])
        nmr = sb("nmr", [P, NT])

        xr = sb("xr", [P, 2, L])
        latT = sb("latT", [LAT + 1, L])
        qk = sb("qk", [P, 2, 2 * P])
        vraw = [sb(f"vraw{i}", [P, 2, P]) for i in range(2)]
        rt1 = sb("rt1", [P, 2, 2 * P])
        rt2 = sb("rt2", [P, 2, 2 * P])
        aug = [sb(f"aug{i}", [P, 2, 2 * H, HP], F16) for i in range(2)]
        vaug = [sb(f"vaug{i}", [P, 2, H, HP]) for i in range(2)]
        QT = [sb(f"QT{i}", [P, NJ, L], F16) for i in range(2)]
        KB = [sb(f"KB{i}", [P, NJ, 4, L], F16) for i in range(2)]
        QT2 = sb("QT2", [P, NJ, L], F16)
        mx = sb("mx", [P, 2, H])
        mneg = sb("mneg", [P, 2, H])
        prob = sb("prob", [P, 8, 2, L])
        OT = sb("OT", [P, 2, 2, L])
        rden = sb("rden", [P, 2, 16])
        on = sb("on", [P, 2, H, HD])
        oxT = sb("oxT", [P, L])

        lg = sb("lg", [P, NT, E1])
        pr = sb("pr", [P, NT, E1])
        gate = sb("gate", [P, NT, E1])
        gtm = sb("gtm", [P, NT, E1])
        eqm = sb("eqm", [P, NT, E1])
        eqb = sb("eqb", [P, NT, E0], BF16)
        cum = [sb("cum0", [P, NT, E1]), sb("cum1", [P, NT, E1])]
        cumb = sb("cumb", [P, NT, E0], BF16)
        cmp_ = sb("cmp", [P, NT, 3 * E0])
        cnt = sb("cnt", [P, 3 * E0], BF16)
        col = sb("col", [P, NT])
        col2 = sb("col2", [P, NT])
        xsq = XB[:, :, :]
        xn2 = sb("xn2", [P, NT])
        top8 = sb("top8", [P, NT, 8])
        thr = sb("thr", [P, E0])
        cand = sb("cand", [P, 3 * E0])
        keep = sb("keep", [P, 3 * E0])
        best = sb("best", [P, E0])
        need = sb("need", [P, E0])
        gateT = XT[0:E1, :]

        W = sb("W", [P, E1, WROW])
        flat = prob[:, :, :, :].rearrange("p a b c -> p (a b c)")
        cuts = np.cumsum([0, 4 * W2AT, 4 * (P + E1), 2 * NF * P])
        part = [flat[:, int(a):int(b)] for a, b in zip(cuts[:-1], cuts[1:])]
        wc = part[0].rearrange("p (s f) -> p s f", s=4)
        xg = part[1].rearrange("p (s c) -> p s c", s=4)
        hid = part[2].rearrange("p (s f c) -> p s f c", s=2, f=NF)
        xsT = rt1[:, :, 0:P]
        yo = rt2[:, :, :].rearrange("p a (b c) -> p (a b) c", c=P)
        zero = sb("zero", [P, P + E1])

        triX = sb("triX", [P, P + 1], BF16)
        triC = sb("triC", [P, P + 1], BF16)
        same_e = sb("same_e", [P, P], BF16)
        before = sb("before", [P, P], BF16)
        pad_before = sb("pad_before", [P, P], BF16)
        first_row = sb("first_row", [P, P], BF16)
        cross = sb("cross", [P, P], BF16)
        shift = sb("shift", [P, P], BF16)
        dtok = sb("dtok", [P, 2])
        dexp = sb("dexp", [P, 2, P], F16)
        slot_in = sb("slot_in", [P, P], F16)
        tile_at = sb("tile_at", [P, NJT[1]])
        slot_at = sb("slot_at", [P, NJT[1]])
        pcol = sb("pcol", [P, 1])
        selz = sb("selz", [P, 1 + E1 * NT], BF16)
        nrow = sb("nrow", [P, 2], BF16)
        padi = sb("padi", [P, 2], I32)
        padf = sb("padf", [P, 2])
        padb = sb("padb", [P, 2], BF16)
        lo = sb("lo", [P, 2])
        padp = sb("padp", [P, 2])
        lom = sb("lom", [P, 2, NJT[1]])
        RH = sb("RH", [P, 2, P + 1], F16)
        indj = sb("indj", [P, 2, NJT[1]], F16)
        ej_out = sb("ej_out", [P, NJT[1] + 4], I32)
        ej_gate = sb("ej_gate", [P, NJT[1]], I32)
        gcol = sb("gcol", [P, 4])
        ej_in = sb("ej_in", [P, NJT[1] + 4], I32)
        ind = sb("ind", [P, 2, 2, P], F16)
        hit = sb("hit", [P, 2, P])
        base_t = sb("base_t", [P, 2, 1])
        tok = sb("tok", [P, 2, 1])
        tpad = sb("tpad", [P, 2, 1])
        idx_all = sb("idx_all", [P, NJT[1]], I32)
        idx_g = sb("idx_g", [P, 4], I32)
        idx_s = sb("idx_s", [P, 4], I32)
        hold = sb("hold", [P, 4])

        bank = [ctx.enter_context(nc.psum_tensor(f"bank{i}", [P, 512], F32)) for i in range(8)]
        half = [b[:, :].bitcast(F16) for b in bank]
        S1B, STB, OTB, M5, M6, M7 = (0, 1), (2, 3), 4, 5, 6, 7

        consts_in = sem("consts_in")
        weights_in = sem("weights_in")
        first_in = sem("first_in")
        x_in = sem("x_in")
        zeroed = sem("zeroed")
        xr_ready = [sem("xr_ready0"), sem("xr_ready1")]
        lat_done = sem("lat_done")
        lat_ready = sem("lat_ready")
        proj_done = sem("proj_done")
        qkv_ready = sem("qkv_ready")
        rope_step = sem("rope_step")
        split_step = sem("split_step")
        aug_ready = sem("aug_ready")
        vaug_ready = sem("vaug_ready")
        tq_done = sem("tq_done")
        tq_ready = sem("tq_ready")
        tk_done = sem("tk_done")
        kb_act = sem("kb_act")
        kb_dve = sem("kb_dve")
        bias_step = sem("bias_step")
        xb_ready = sem("xb_ready")
        s1_done = sem("s1_done")
        s1_used = sem("s1_used")
        m_step = sem("m_step")
        m_ready = sem("m_ready")
        tq2_done = sem("tq2_done")
        tq2_ready = sem("tq2_ready")
        st_done = sem("st_done")
        exp_done = sem("exp_done")
        av_done = sem("av_done")
        ot_ready = sem("ot_ready")
        bt_done = sem("bt_done")
        rden_ready = sem("rden_ready")
        on_ready = sem("on_ready")
        ox_done = sem("ox_done")
        ox_ready = sem("ox_ready")
        pj_done = sem("pj_done")
        y_ready = sem("y_ready")
        batch_stats = sem("batch_stats")
        stats_ready = sem("stats_ready")
        var_ready = sem("var_ready")
        std_ready = sem("std_ready")
        rstd_ready = sem("rstd_ready")
        xn_dve = sem("xn_dve")
        xn_act = sem("xn_act")
        xt_done = sem("xt_done")
        xt_ready = sem("xt_ready")
        wr_ready = sem("wr_ready")
        ksq_done = sem("ksq_done")
        lg_done = sem("lg_done")
        rstep = sem("rstep")
        lsh_ready = sem("lsh_ready")
        lexp_ready = sem("lexp_ready")
        xsq_ready = sem("xsq_ready")
        cnt_ready = sem("cnt_ready")
        count_done = sem("count_done")
        tie_ready = sem("tie_ready")
        rank_done = sem("rank_done")
        gate_ready = sem("gate_ready")
        gt_done = sem("gt_done")
        gt_ready = sem("gt_ready")
        gb_done = sem("gb_done")
        biased = sem("biased")
        w_in = sem("w_in")
        sel_ready = sem("sel_ready")
        rh_done = sem("rh_done")
        nrow_ready = sem("nrow_ready")
        ne_done = sem("ne_done")
        pad_ready = sem("pad_ready")
        lo_done = sem("lo_done")
        indj_ready = sem("indj_ready")
        ej_done = sem("ej_done")
        ej_ready = sem("ej_ready")
        scratch_in = sem("scratch_in")
        xs_in = [sem("xs_in0"), sem("xs_in1")]
        back_in = [sem("back_in0"), sem("back_in1")]
        ind_ready = sem("ind_ready")
        list_done = sem("list_done")
        lstep = sem("lstep")
        idx_ready = sem("idx_ready")
        wc_ready = sem("wc_ready")
        gathered = [sem(f"gathered{i}") for i in range(4)]
        scattered = [sem(f"scattered{i}") for i in range(2)]
        held = sem("held")
        tp_done = sem("tp_done")
        xsT_ready = sem("xsT_ready")
        h_done = sem("h_done")
        gelu_done = sem("gelu_done")
        eo_done = sem("eo_done")
        yo_ready = sem("yo_ready")
        gcol_ready = sem("gcol_ready")
        idx_s_ready = sem("idx_s_ready")
        out_done = sem("out_done")

        N_FIRST, N_CONST, N_WEIGHT = 7, 16, 15
        def qk_of(lay, par):
            return (qk, rt1)[par] if lay == 1 else qk

        xs = [d["xs0"], d["xs1"]]
        sums_d = [[d["sum00"], d["sum01"]], [d["sum10"], d["sum11"]]]

        def wait_for(engine, semaphore, value):
            if not (isinstance(value, int) and value <= 0):
                engine.wait_ge(semaphore, value)

        def slot_steps(lay, engine, step):
            J = NJT[lay]
            for j in range(-AHEAD, 4):
                step(j, j % 4)
            with engine.Fori(1, J // 4 - 1) as jh:
                for s in range(4):
                    step(4 * jh + s, s)
            for j in range(J - 4, J + 1):
                step(j, j % 4)

        def tile_expert(engine, lay, table, at, s, regs):
            top = (E0, E1)[lay] - 1
            if isinstance(at, int):
                return engine.value_load(table[0:1, at:at + 1], min_val=0, max_val=top)
            if s == 0:
                engine.load(regs, table[0:1, bass.ds(at, 4)])
            return engine.snap(regs[s], min_val=0, max_val=top)

        def normalised(engine, n):
            engine.wait_ge(xn_dve, NT // 2 * n)
            engine.wait_ge(xn_act, NT // 2 * n)

        def is_tile(lay, j):
            return not isinstance(j, int) or 0 <= j < NJT[lay]

        block = ctx.enter_context(nc.Block())

        v4 = lambda t: t[:, :, :].rearrange("p t (h x) -> p t h x", x=HD)

        def rope(engine, lay, b, par):
            g = b + NB * lay
            engine.wait_ge(qkv_ready, 2 * g + 2)
            n = 2 * P // HD
            cos = ropec[:, :, :].unsqueeze(2).to_broadcast([P, 2, n, HD])
            sin = ropes[:, :, :].unsqueeze(2).to_broadcast([P, 2, n, HD])
            hh = HD // 2
            if not isinstance(b, int) or b > 0:
                engine.wait_ge(aug_ready, g)
            for t in range(2):
                engine.tensor_tensor(v4(rt1)[:, t], v4(qk)[:, t], cos[:, t], ALU.mult).then_inc(rope_step, 1)
                engine.tensor_tensor(v4(rt2)[:, t, :, 0:hh], v4(qk)[:, t, :, hh:HD], sin[:, t, :, 0:hh],
                                        ALU.mult).then_inc(rope_step, 1)
                engine.tensor_tensor(v4(rt2)[:, t, :, hh:HD], v4(qk)[:, t, :, 0:hh], sin[:, t, :, hh:HD],
                                        ALU.mult).then_inc(rope_step, 1)
            engine.wait_ge(rope_step, 7 * g + 6)
            engine.tensor_tensor(rt1[:, :, :], rt1[:, :, :], rt2[:, :, :], ALU.add).then_inc(rope_step, 1)

        def build_aug(engine, lay, b, par):
            g = b + NB * lay
            if isinstance(b, int) and b == 1:
                engine.wait_ge(aug_ready, g)
            if lay == 0:
                engine.wait_ge(rope_step, 7 * g + 7)
            else:
                engine.wait_ge(qkv_ready, 2 * g + 2)
            if not (isinstance(b, int) and g < 2):
                engine.wait_ge(tq2_done, 2 * (g - 1))
            A = aug[par]
            s4 = v4(qk_of(lay, par) if lay == 1 else rt1)
            one = ones[:, 0:HD].unsqueeze(1).unsqueeze(1).to_broadcast([P, H, 2, HD])
            for t in range(2):
                qin = s4[:, t, 0:H, :].unsqueeze(2).to_broadcast([P, H, 2, HD])
                kin = s4[:, t, H:2 * H, :].unsqueeze(2).to_broadcast([P, H, 2, HD])
                qout = A[:, t, 0:H, 0:2 * HD].rearrange("p h (r x) -> p h r x", x=HD)
                kout = A[:, t, H:2 * H, 0:4 * HD].rearrange("p h (r y) -> p h r y", r=2)[:, :, :, 0:HD]
                if t == 0:
                    engine.tensor_tensor(qout, qin, one, ALU.mult).then_inc(split_step, 1)
                else:
                    engine.tensor_scalar(qout, qin, 1.0, None, ALU.mult).then_inc(split_step, 1)
                engine.tensor_scalar(kout, kin, 1.0, None, ALU.mult).then_inc(split_step, 1)
            engine.memset(A[:, :, 0:H, NROW:NROW + 2], 0.0)
            engine.wait_ge(split_step, 4 * g + 4)
            for t in range(2):
                engine.tensor_tensor(A[:, t, 0:H, 2 * HD:3 * HD], s4[:, t, 0:H, :], A[:, t, 0:H, 0:HD],
                                        ALU.subtract)
                last = engine.tensor_tensor(A[:, t, H:2 * H, HD:2 * HD], s4[:, t, H:2 * H, :],
                                               A[:, t, H:2 * H, 0:HD], ALU.subtract)
            last.then_inc(aug_ready, 1)

        @block.sync
        def _(sp):
            sp.dma_start(XT[:, 0:2 * L], d["xT"][:, 0:2 * L]).then_inc(first_in, 16)
            for n, dst in (("wqkv0", wqkv0), ("braw", braw), ("c_ident", ident), ("c_ropec", ropec),
                           ("c_ropes", ropes), ("c_ident_h", ident_h)):
                sp.dma_start(dst[:], d[n]).then_inc(first_in, 16)
            sp.dma_start(X[:, :, :], d["x"].rearrange("(t p) c -> p t c", p=P)).then_inc(x_in, 16)
            sp.dma_start(XT[:, 2 * L:TOK], d["xT"][:, 2 * L:TOK]).then_inc(x_in, 16)
            for lay in range(2):
                sp.dma_start(bo[lay][:, :], d[f"bo{lay}"].to_broadcast([P, P])).then_inc(weights_in, 16)
                sp.dma_start(wo[lay][:, :], d[f"wo{lay}"]).then_inc(weights_in, 16)
            for dst, src in ((wq1, "wq1"), (wl1, "wl1"), (bl1, "bl1"), (wkv1, "wkv1"), (ws0, "ws0"),
                             (keysT, "keysT"), (rwT, "rwT"), (b2[0], "b2_0"), (b2[1], "b2_1")):
                sp.dma_start(dst[:], d[src]).then_inc(weights_in, 16)
            sp.dma_start(bs0[:, :], d["bs0"].to_broadcast([P, E0])).then_inc(weights_in, 16)
            sp.dma_start(rb[:, :], d["rb"].to_broadcast([P, E1])).then_inc(weights_in, 16)
            for n, dst in (("tri", tri), ("bits", bits), ("triX", triX), ("triC", triC), ("same_e", same_e),
                           ("before", before), ("pad_before", pad_before), ("first_row", first_row),
                           ("shift", shift), ("cross", cross), ("dtok", dtok), ("dexp", dexp), ("slot_in", slot_in),
                           ("tile_at", tile_at), ("slot_at", slot_at), ("pcol", pcol)):
                sp.dma_start(dst[:], d["c_" + n]).then_inc(consts_in, 16)

            def expert_weights(lay, e):
                src1 = d[f"w1_{lay}"][bass.ds(e, 1), :, :].rearrange("a p f -> p (a f)")
                src2 = d[f"b1_{lay}"][bass.ds(e, 1), :, :].rearrange("a p f -> p (a f)")
                src3 = d[f"w2_{lay}"][bass.ds(e, 1), :, :].rearrange("a (t p) c -> p (a t) c", p=P)
                at = bass.ds(e, 1)
                sp.dma_start(W[:, at, 0:WB].rearrange("p a f -> p (a f)"), src1).then_inc(w_in, 16)
                sp.dma_start(W[:, at, WB:W2AT].rearrange("p a f -> p (a f)"), src2).then_inc(w_in, 16)
                sp.dma_start(W[:, at, W2AT:WROW].rearrange("p a (t c) -> p (a t) c", c=P), src3).then_inc(w_in, 16)

            def batch_in(lay, b, slot):
                g = b + NB * lay
                if not (isinstance(b, int) and g < 4):
                    sp.wait_ge(proj_done, 2 * (g - 1))
                sp.dma_start(xr[:, slot, :], XT[:, bass.ds(b * L, L)]).then_inc(xr_ready[slot], 16)

            def batches_in(lay):
                n = (E0, E1)[lay] // (NB // 2)
                for s in range(2):
                    batch_in(lay, 2 + s, s)
                for e in range(n):
                    expert_weights(lay, e)
                for e in range(n, 2 * n):
                    expert_weights(lay, e)
                with sp.Fori(2, NB // 2) as bh:
                    batch_in(lay, 2 * bh, 0)
                    batch_in(lay, 2 * bh + 1, 1)
                    for e in range(n):
                        expert_weights(lay, n * bh + e)

            def tokens_out(lay):
                E = (E0, E1)[lay]
                tiles = lambda ap: ap.rearrange("(t p) c -> p t c", p=P)
                normalised(sp, 2 * lay + 1)
                sp.dma_start(tiles(xs[lay][0:TOK, 0:P]), X[:, :, :]).then_inc(xs_in[lay], 16)
                sp.wait_ge(gate_ready, lay + 1)
                sp.dma_start(tiles(xs[lay][0:TOK, P:P + E]), gate[:, :, 0:E]).then_inc(xs_in[lay], 16)
                for par, dst in ((0, Y), (1, XB)):
                    sp.wait_ge(scattered[par], 8 * (NJT[lay] + lay * NJT[0]))
                    sp.dma_start(dst[:, :, :], tiles(sums_d[lay][par][0:TOK, :])).then_inc(back_in[par], 16)

            sp.wait_ge(x_in, 32)
            batches_in(0)
            sp.wait_ge(zeroed, 2)
            for lay in range(2):
                sp.dma_start(xs[lay][TOK:ROWS, :], zero[:, 0:P + (E0, E1)[lay]]).then_inc(scratch_in, 16)
                for par in range(2):
                    sp.dma_start(sums_d[lay][par].rearrange("(t p) c -> p t c", p=P),
                                 zero[:, 0:P].unsqueeze(1).to_broadcast([P, NT + 1, P])).then_inc(scratch_in, 16)
            tokens_out(0)
            sp.wait_ge(xt_ready, 8)
            batches_in(1)
            tokens_out(1)
            out_v = d["out"].rearrange("(t p) c -> p t c", p=P)
            normalised(sp, 4)
            sp.dma_start(out_v, X[:, :, :]).then_inc(out_done, 16)
            sp.wait_ge(out_done, 16)

        @block.gpsimd
        def _(pool):
            nc.gpsimd.memset(ones[:, :], 1.0)
            nc.gpsimd.memset(zero[:, :], 0.0)
            nc.gpsimd.memset(ones_b[:, :], 1.0)
            for i in range(2):
                nc.gpsimd.memset(aug[i][:, :, 0:H, NROW:HP], 0.0)
                nc.gpsimd.memset(aug[i][:, :, H:2 * H, NROW + 2:HP], 0.0)
                nc.gpsimd.memset(aug[i][:, :, H:2 * H, NROW:NROW + 2], MUNIT)
                nc.gpsimd.memset(vaug[i][:, :, :, HD + 1:HP], 0.0)
                nc.gpsimd.memset(KB[i][:, :, :, :].bitcast(I32), 0)
                last = nc.gpsimd.memset(vaug[i][:, :, :, HD:HD + 1], 1.0)
            last.then_inc(zeroed, 1)
            pool.wait_ge(zeroed, 2)

            def build_vaug(lay, b, par):
                g = b + NB * lay
                if isinstance(b, int) and b == 0:
                    pool.wait_ge(qkv_ready, 2 * g + 2)
                if not (isinstance(b, int) and g < 2):
                    pool.wait_ge(av_done, 4 * (g - 1))
                v = vraw[par][:, :, :].rearrange("p t (h x) -> p t h x", x=HD)
                one = ones[:, 0:HD].unsqueeze(1).unsqueeze(1).to_broadcast([P, 2, H, HD])
                nc.gpsimd.tensor_tensor(vaug[par][:, :, :, 0:HD], v, one, ALU.mult).then_inc(vaug_ready, 1)

            def pool_iteration(lay, i, par):
                build_vaug(lay, i, par)
                if not (isinstance(i, int) and i > NB - 2):
                    build_aug(pool, lay, i + 1, 1 - par)
                if lay == 0 and not (isinstance(i, int) and i > NB - 3):
                    rope(pool, lay, i + 2, par)

            def pool_slots(lay, j, s):
                kd = j + NJT[0] * lay
                E = (E0, E1)[lay]
                if not (is_tile(lay, j - 1) or is_tile(lay, j + AHEAD)):
                    return
                if is_tile(lay, j + AHEAD):
                    pool.wait_ge(idx_ready, kd + AHEAD + 1)
                if is_tile(lay, j - 1):
                    pool.wait_ge(yo_ready, kd)
                    pool.wait_ge(idx_s_ready, kd)
                    wait_for(pool, scattered[(s - 1) % 2], 8 * (kd - 1 - (s - 1) % 2))
                wait_for(pool, held, (NJT[0] + AHEAD + 1) * lay + j + (AHEAD if isinstance(j, int) else AHEAD - 3))
                nc.gpsimd.tensor_tensor(hold[:, s:s + 1], ones[:, 0:1], ones[:, 0:1], ALU.mult).then_inc(held, 1)
                if is_tile(lay, j + AHEAD):
                    q = (s + AHEAD) % 4
                    nc.gpsimd.indirect_dma_start(xg[:, q, 0:P + E], None, xs[lay],
                                                 bass.IndirectOffsetOnAxis(idx_g[:, q:q + 1], 0)
                                                 ).then_inc(gathered[q], 16)
                if is_tile(lay, j - 1):
                    nc.gpsimd.indirect_dma_start(sums_d[lay][(s - 1) % 2],
                                                 bass.IndirectOffsetOnAxis(idx_s[:, (s - 1) % 4:(s - 1) % 4 + 1], 0),
                                                 yo[:, (s - 1) % 4, :], None,
                                                 compute_op=ALU.add).then_inc(scattered[(s - 1) % 2], 16)

            pool.wait_ge(first_in, 16 * N_FIRST)
            for lay in range(2):
                if lay == 0:
                    rope(pool, lay, 1, 1)
                    pool.wait_ge(x_in, 32)
                    pool.wait_ge(weights_in, 16 * N_WEIGHT)
                if lay == 1:
                    normalised(pool, 2)
                nc.gpsimd.tensor_tensor(XB[:, :, :], X[:, :, :], bo[lay][:, :].unsqueeze(1).to_broadcast([P, NT, P]),
                                        ALU.add).then_inc(xb_ready, 1)
                pool_iteration(lay, 0, 0)
                pool_iteration(lay, 1, 1)
                with pool.Fori(1, NB // 2 - 1) as ih:
                    i = 2 * ih
                    pool_iteration(lay, i, 0)
                    pool_iteration(lay, i + 1, 1)
                pool_iteration(lay, NB - 2, 0)
                pool_iteration(lay, NB - 1, 1)
                if lay == 1:
                    normalised(pool, 3)
                    nc.gpsimd.tensor_tensor(xsq[:, :, :], X[:, :, :], X[:, :, :], ALU.mult).then_inc(xsq_ready, 1)
                pool.wait_ge(scratch_in, 16 * 6)
                pool.wait_ge(xs_in[lay], 16 * 2)
                slot_steps(lay, pool, lambda j, s: pool_slots(lay, j, s))

        @block.tensor
        def _(pe):
            def s1(lay, i, par, u):
                g = i + NB * lay
                qt, j, qp = u // 8, (u % 8) // 2, u % 2
                if u == 0:
                    pe.wait_ge(tq_ready, g + 1)
                if u in (0, 4):
                    pe.wait_ge(kb_act, 2 * g + u // 4 + 1)
                    pe.wait_ge(kb_dve, 2 * g + u // 4 + 1)
                if not (isinstance(i, int) and g == 0 and u < 2):
                    pe.wait_ge(s1_used, 16 * g + u - 1)
                nc.tensor.matmul(bank[S1B[u % 2]][:, :], QT[par][:, j, P * qt:P * qt + P],
                                 KB[par][:, j, 2 * qp:2 * qp + 2, :], start=True, stop=True).then_inc(s1_done, 1)

            def st(lay, b, par, v):
                g = b + NB * lay
                j, q = v // 4, v % 4
                if v in (0, 8):
                    pe.wait_ge(tq2_ready, 2 * g + v // 8 + 1)
                if not (isinstance(b, int) and g == 0 and v < 2):
                    pe.wait_ge(exp_done, 16 * g + v - 1)
                for kt in range(2):
                    last = nc.tensor.matmul(bank[STB[v % 2]][:, L * kt:L * kt + L],
                                            KB[par][:, j, q, P * kt:P * kt + P], QT2[:, j, :],
                                            start=True, stop=True)
                last.then_inc(st_done, 1)

            def av(lay, b, par, j, kt):
                g = b + NB * lay
                if kt == 0:
                    if j == 0:
                        pe.wait_ge(vaug_ready, g + 1)
                    if j == 0 and not (isinstance(b, int) and g == 0):
                        pe.wait_ge(ot_ready, 2 * g)
                    if j == 2:
                        pe.wait_ge(ot_ready, 2 * g + 1)
                    pe.wait_ge(exp_done, 16 * g + 4 * j + 4)
                for q in range(4):
                    last = nc.tensor.matmul(bank[OTB][HP * q:HP * q + HP, L * (j % 2):L * (j % 2) + L],
                                            vaug[par][:, kt, 4 * j + q, :], prob[:, (4 * j + q) % 8, kt, :],
                                            start=(kt == 0), stop=(kt == 1))
                if kt == 1:
                    last.then_inc(av_done, 1)

            def bt(lay, b, pair):
                g = b + NB * lay
                pe.wait_ge(ot_ready, 2 * g + pair + 1)
                for t in range(2):
                    for jj in range(2):
                        at = P * (2 * t + jj)
                        last = nc.tensor.transpose(bank[M7][:, at:at + P], OT[:, pair, jj, P * t:P * t + P], ident[:, :])
                last.then_inc(bt_done, 1)

            def pe_iteration(lay, i, par, mx_on, soft_on, front_on, tail_on):
                g = i + NB * lay
                nxt = 1 - par
                for u in range(16):
                    if mx_on:
                        s1(lay, i, par, u)
                    if u < 2 and tail_on:
                        av(lay, i - 2, par, 3, u)
                    if u == 1 and soft_on:
                        pe.wait_ge(m_ready, g)
                        for j in range(NJ):
                            for t in range(2):
                                last = nc.tensor.transpose(half[M5][:, L * j + P * t:L * j + P * t + P],
                                                           aug[nxt][:, t, 4 * j:4 * j + 4, :], ident_h[:, :])
                            if j % 2:
                                last.then_inc(tq2_done, 1)
                    if soft_on:
                        for v in soft_units(u):
                            st(lay, i - 1, nxt, v)
                    if front_on and not (isinstance(i, int) and i > NB - 3):
                        if u == 2 and lay == 1:
                            front_latent(lay, i + 2, par)
                        if u == 3 + lay:
                            front_proj(lay, i + 2, par, 0)
                        if u == 5 + lay:
                            front_proj(lay, i + 2, par, 1)
                    if u == 3 and tail_on:
                        pe.wait_ge(on_ready, 2 * (g - 2) + 1)
                        bt(lay, i - 2, 1)
                    if u == 6 and tail_on:
                        pe.wait_ge(on_ready, 2 * (g - 2) + 2)
                        for t in range(2):
                            last = nc.tensor.transpose(bank[M7][:, P * t:P * t + P], on[:, t, :, :], ident[:, :])
                        last.then_inc(ox_done, 1)
                    if u == 9 and tail_on:
                        pe.wait_ge(ox_ready, g - 1)
                        for t in range(2):
                            last = nc.tensor.matmul(bank[M7][:, P * t:P * t + P], oxT[:, P * t:P * t + P], wo[lay][:, :],
                                                    start=True, stop=True)
                        last.then_inc(pj_done, 1)
                    if u in (7, 8) and soft_on:
                        av(lay, i - 1, nxt, 0, u - 7)
                    if u in (10, 11) and soft_on:
                        av(lay, i - 1, nxt, 1, u - 10)
                    if u == 12 and front_on:
                        query_transposes(lay, i + 1, nxt)
                    if u == 13 and front_on:
                        key_transposes(lay, i + 1, nxt)
                    if u == 14 and soft_on:
                        if tail_on:
                            pe.wait_ge(y_ready, g - 1)
                        bt(lay, i - 1, 0)
                    if u in (14, 15) and soft_on:
                        av(lay, i - 1, nxt, 2, u - 14)
            def stream(b, par, at, n):
                if isinstance(b, int) and b < 2:
                    return XT[:, b * L + at:b * L + at + n]
                return xr[:, par, at:at + n]

            def xr_wait(lay, b, par):
                if not (isinstance(b, int) and b < 2):
                    pe.wait_ge(xr_ready[par], 8 * (b - par) + 8 * (NB - 2) * lay)

            def m5_read(b, g):
                if isinstance(b, int) and b == 1:
                    pe.wait_ge(qkv_ready, 2 * g)
                elif not (isinstance(b, int) and g == 0):
                    pe.wait_ge(tq_ready, g - 1)
                    if not (isinstance(b, int) and b <= 2):
                        pe.wait_ge(tq2_ready, 2 * (g - 2))

            def front_latent(lay, b, par):
                g = b + NB * lay
                xr_wait(lay, b, par)
                m5_read(b, g)
                nc.tensor.matmul(bank[M5][0:LAT, 0:L], wl1[:, :], stream(b, par, 0, L), start=True,
                                 stop=True).then_inc(lat_done, 1)

            def front_proj(lay, b, par, t):
                g = b + NB * lay
                if lay == 1 and t == 0:
                    pe.wait_ge(lat_ready, b + 1)
                if lay == 0 and t == 0:
                    xr_wait(lay, b, par)
                    m5_read(b, g)
                if t == 1:
                    pe.wait_ge(qkv_ready, 2 * g + 1)
                tok = stream(b, par, P * t, P)
                if lay == 0:
                    nc.tensor.matmul(bank[M5][:, 0:3 * P], tok, wqkv0[:, :], start=True, stop=False)
                    last = nc.tensor.matmul(bank[M5][:, 0:3 * P], ones_b[0:3, :], bsplit[:, 0:3 * P],
                                            start=False, stop=True)
                else:
                    nc.tensor.matmul(bank[M5][:, 0:P], tok, wq1[:, :], start=True, stop=False)
                    nc.tensor.matmul(bank[M5][:, 0:P], ones_b[0:3, :], bsplit[:, 3 * P:4 * P], start=False, stop=True)
                    last = nc.tensor.matmul(bank[M5][:, P:3 * P], latT[:, P * t:P * t + P], wkv1[:, :],
                                            start=True, stop=True)
                last.then_inc(proj_done, 1)

            def query_transposes(lay, b, par):
                g = b + NB * lay
                pe.wait_ge(aug_ready, g + 1)
                if not (isinstance(b, int) and b == NB - 1):
                    pe.wait_ge(qkv_ready, 2 * g + 4)
                for j in range(NJ):
                    for t in range(2):
                        last = nc.tensor.transpose(half[M5][:, L * j + P * t:L * j + P * t + P],
                                                   aug[par][:, t, 4 * j:4 * j + 4, :], ident_h[:, :])
                last.then_inc(tq_done, 1)

            def key_transposes(lay, b, par):
                g = b + NB * lay
                if not (isinstance(b, int) and b == 0):
                    pe.wait_ge(kb_act, 2 * g)
                    pe.wait_ge(kb_dve, 2 * g)
                for j in range(NJ):
                    for t in range(2):
                        last = nc.tensor.transpose(half[M6][:, L * j + P * t:L * j + P * t + P],
                                                   aug[par][:, t, H + 4 * j:H + 4 * j + 4, :], ident_h[:, :])
                last.then_inc(tk_done, 1)

            def turn(n):
                for c in range(4):
                    if c < 2:
                        pe.wait_ge(xn_dve, NT // 2 * n + 4 * c + 4)
                    else:
                        pe.wait_ge(xn_act, NT // 2 * n + 4 * (c - 2) + 4)
                    for t in range(4):
                        last = nc.tensor.transpose(bank[c][:, P * t:P * t + P], X[:, 4 * c + t, :], ident[:, :])
                    last.then_inc(xt_done, 1)

            def logits(lay, w, E):
                pe.wait_ge(xt_ready, 8 * lay + 4)
                if lay == 1:
                    pe.wait_ge(wr_ready, 2)
                    nc.tensor.matmul(bank[6][:, 0:E1], ones[:, :], ksq[:, :], start=True,
                                     stop=True).then_inc(ksq_done, 1)
                for t in range(NT):
                    last = nc.tensor.matmul(bank[5][:, E * t:E * t + E], XT[:, P * t:P * t + P], w[:, :], start=True,
                                            stop=True)
                last.then_inc(lg_done, 1)

            def gate_bias(lay, E):
                pe.wait_ge(gate_ready, lay + 1)
                for c in range(4):
                    for t in range(4):
                        last = nc.tensor.transpose(bank[c][0:E, P * t:P * t + P], gate[:, 4 * c + t, 0:E], ident[:, :])
                    last.then_inc(gt_done, 1)
                for c in range(4):
                    pe.wait_ge(gt_ready, 4 * lay + c + 1)
                    for t in range(4):
                        last = nc.tensor.matmul(bank[c][:, P * t:P * t + P], gateT[0:E, P * (4 * c + t):P * (4 * c + t + 1)],
                                                b2[lay][:, :], start=True, stop=True)
                    last.then_inc(gb_done, 1)

            def slot_table(lay):
                K = KT[lay]
                pe.wait_ge(sel_ready, lay + 1)
                for k in range(K):
                    nc.tensor.matmul(bank[4 + k][:, 0:P + 1], selz[:, 1 + P * k:1 + P * k + P], triX[:, :], start=True,
                                     stop=False)
                    last = nc.tensor.matmul(bank[4 + k][:, 0:P + 1], selz[:, P * k:P * k + P], triC[:, :],
                                            start=False, stop=True)
                last.then_inc(rh_done, 1)
                pe.wait_ge(nrow_ready, lay + 1)
                nc.tensor.matmul(bank[6][:, 0:K], same_e[:, :], nrow[:, 0:K], start=True, stop=True).then_inc(ne_done, 1)
                pe.wait_ge(pad_ready, lay + 1)
                for k in range(K):
                    at = slice(8 + k, 9 + k)
                    nc.tensor.matmul(bank[6][:, at], before[:, :], nrow[:, k:k + 1], start=True, stop=False)
                    nc.tensor.matmul(bank[6][:, at], pad_before[:, :], padb[:, k:k + 1], start=False, stop=(k == 0))
                    if k == 1:
                        nc.tensor.matmul(bank[6][:, at], ones_b[:, :], nrow[:, 0:1], start=False, stop=False)
                        nc.tensor.matmul(bank[6][:, at], first_row[:, :], padb[:, 0:1], start=False, stop=True)
                    at = slice(16 + k, 17 + k)
                    last = nc.tensor.matmul(bank[6][:, at], shift[:, :], padb[:, k:k + 1], start=True, stop=(k == 0))
                    if k == 1:
                        last = nc.tensor.matmul(bank[6][:, at], cross[:, :], padb[:, 0:1], start=False, stop=True)
                last.then_inc(lo_done, 1)
                pe.wait_ge(indj_ready, lay + 1)
                for k in range(K):
                    last = nc.tensor.matmul(bank[6][:, P:P + NJT[lay]], dexp[:, k, :], indj[:, k, 0:NJT[lay]],
                                            start=(k == 0), stop=(k == K - 1))
                last.then_inc(ej_done, 1)
                pe.wait_ge(ej_ready, lay + 1)

            pe_experts = [pe.alloc_register(f"pe_expert{i}") for i in range(4)]

            def pe_slots(lay, j, s):
                kd = j + NJT[0] * lay
                if is_tile(lay, j + 1):
                    q = (s + 1) % 4
                    pe.wait_ge(gathered[q], 4 * (kd + 1 - q) + 16)
                    wait_for(pe, xsT_ready, kd)
                    nc.tensor.transpose(bank[(s + 1) % 2][:, 0:P], xg[:, q, 0:P], ident[:, :]).then_inc(tp_done, 1)
                if is_tile(lay, j):
                    pe.wait_ge(xsT_ready, kd + 1)
                    pe.wait_ge(wc_ready, kd + 1)
                    wait_for(pe, gelu_done, kd - 1)
                    for f in range(NF):
                        last = nc.tensor.matmul(bank[2 + s % 2][:, P * f:P * f + P], wc[:, s, P * f:P * f + P],
                                                xsT[:, s % 2, :], start=True, stop=True)
                    last.then_inc(h_done, 1)
                if is_tile(lay, j + AHEAD):
                    q = (s + AHEAD) % 2
                    pe.wait_ge(ind_ready, kd + AHEAD + 1)
                    wait_for(pe, idx_ready, kd + AHEAD - 1)
                    for k in range(KT[lay]):
                        last = nc.tensor.matmul(bank[6 + q][:, 0:P + 1], ind[:, q, k, :], RH[:, k, :], start=(k == 0),
                                                stop=(k == KT[lay] - 1))
                    last.then_inc(list_done, 1)
                if is_tile(lay, j - 1):
                    q = (s - 1) % 2
                    e = tile_expert(pe, lay, ej_out, j, s, pe_experts)
                    pe.wait_ge(gelu_done, kd)
                    wait_for(pe, yo_ready, kd - 2)
                    for f in range(NF):
                        last = nc.tensor.matmul(bank[4 + q][:, 0:P], hid[:, q, f, :],
                                                W[:, bass.ds(e, 1), W2AT + P * f:W2AT + P * f + P],
                                                start=(f == 0), stop=(f == NF - 1))
                    last.then_inc(eo_done, 1)

            pe.wait_ge(first_in, 16 * N_FIRST)
            pe.wait_ge(zeroed, 2)
            pe.wait_ge(bias_step, 7)
            for lay in range(2):
                if lay == 1:
                    pe.wait_ge(xt_ready, 8)
                if lay == 1:
                    front_latent(lay, 0, 0)
                front_proj(lay, 0, 0, 0)
                front_proj(lay, 0, 0, 1)
                if lay == 1:
                    front_latent(lay, 1, 1)
                front_proj(lay, 1, 1, 0)
                front_proj(lay, 1, 1, 1)
                query_transposes(lay, 0, 0)
                key_transposes(lay, 0, 0)
                if lay == 0:
                    pe.wait_ge(weights_in, 16 * N_WEIGHT)
                    pe.wait_ge(consts_in, 16 * N_CONST)
                pe_iteration(lay, 0, 0, True, False, True, False)
                pe_iteration(lay, 1, 1, True, True, True, False)
                with pe.Fori(1, NB // 2 - 1) as ih:
                    i = 2 * ih
                    pe_iteration(lay, i, 0, True, True, True, True)
                    pe_iteration(lay, i + 1, 1, True, True, True, True)
                pe_iteration(lay, NB - 2, 0, True, True, True, True)
                pe_iteration(lay, NB - 1, 1, True, True, False, True)
                pe_iteration(lay, NB, 0, False, True, False, True)
                pe_iteration(lay, NB + 1, 1, False, False, False, True)
                turn(2 * lay)
                if lay == 0:
                    logits(0, ws0, E0)
                    with pe.Fori(0, NBITS // 2) as it:
                        pe.wait_ge(cnt_ready, it + 1)
                        nc.tensor.matmul(bank[6][:, 0:3 * E0], ones_b[:, :], cnt[:, :], start=True,
                                         stop=True).then_inc(count_done, 1)
                    pe.wait_ge(cnt_ready, NBITS // 2 + 1)
                    nc.tensor.matmul(bank[6][:, 0:E0], ones_b[:, :], cnt[:, 0:E0], start=True,
                                     stop=True).then_inc(count_done, 1)
                    pe.wait_ge(tie_ready, 1)
                    nc.tensor.matmul(bank[7][:, 0:NT * E0], tri[:, :], eqb[:, :, :], start=True, stop=False)
                    nc.tensor.matmul(bank[7][:, 0:NT * E0], ones_b[:, :], cumb[:, :, :], start=False,
                                     stop=True).then_inc(rank_done, 1)
                else:
                    logits(1, wr1, E1)
                slot_table(lay)
                pe.wait_ge(w_in, 48 * (E0 + E1 * lay))
                slot_steps(lay, pe, lambda j, s: pe_slots(lay, j, s))
                gate_bias(lay, (E0, E1)[lay])
                if lay == 0:
                    turn(1)

        @block.scalar
        def _(act):
            def act_iteration(lay, i, par, mx_on, soft_on, front_on, tail_on):
                g = i + NB * lay
                nxt = 1 - par
                for u in range(16):
                    if u == 1 and soft_on:
                        for part in range(2):
                            act.wait_ge(tq2_done, 2 * g)
                            if part == 0 and not (isinstance(i, int) and g == 1):
                                act.wait_ge(st_done, 16 * (g - 1))
                            at = slice(2 * part, 2 * part + 2)
                            nc.scalar.copy(QT2[:, at, :], half[M5][:, 2 * L * part:2 * L * part + 2 * L])\
                                .then_inc(tq2_ready, 1)
                    if soft_on:
                        for v in soft_units(u):
                            gb = g - 1
                            act.wait_ge(st_done, 16 * gb + v + 1)
                            if v % 4 == 0 and not (isinstance(i, int) and gb == 0 and v < 8):
                                act.wait_ge(av_done, 4 * gb + v // 4 - 1)
                            nc.scalar.activation(prob[:, v % 8, :, :], bank[STB[v % 2]][:, :], ACT.Exp,
                                                 scale=SCALE).then_inc(exp_done, 1)
                    if u == 1 and tail_on:
                        ot_evac(lay, i - 2, 1)
                    proj_on = front_on and not (isinstance(i, int) and i > NB - 3)
                    if u == 2 and proj_on and lay == 1:
                        lat_evac(i + 2)
                    if proj_on and u == 3 + lay:
                        front_evac(lay, i + 2, par, 0)
                    if proj_on and u == 5 + lay:
                        front_evac(lay, i + 2, par, 1)
                    if u == 7 and tail_on:
                        act.wait_ge(ox_done, g - 1)
                        nc.scalar.copy(oxT[:, :], bank[M7][:, 0:L]).then_inc(ox_ready, 1)
                    if u == 12 and soft_on:
                        ot_evac(lay, i - 1, 0)
                    if u == 14 and front_on:
                        keys_evac(lay, i + 1, nxt, 0)
                if front_on:
                    keys_evac(lay, i + 1, nxt, 1)

            def ot_evac(lay, b, pair):
                g = b + NB * lay
                act.wait_ge(av_done, 4 * g + 2 * pair + 2)
                if not (isinstance(b, int) and g == 0):
                    act.wait_ge(bt_done, 2 * g + pair - 1)
                nc.scalar.copy(OT[:, pair, :, :], bank[OTB][:, :]).then_inc(ot_ready, 1)

            def lat_evac(b):
                act.wait_ge(lat_done, b + 1)
                if not isinstance(b, int) or b > 0:
                    act.wait_ge(proj_done, 2 * (b + NB))
                nc.scalar.activation(latT[0:LAT, :], bank[M5][0:LAT, 0:L], ACT.Identity,
                                     bias=bl1[:, 0:1]).then_inc(lat_ready, 1)

            def keys_evac(lay, b, par, pair):
                g = b + NB * lay
                act.wait_ge(tk_done, g + 1)
                if not (isinstance(b, int) and g < 2):
                    act.wait_ge(st_done, 16 * (g - 2) + 8 * pair + 8)
                for q in range(2):
                    rows, js = slice(HP * q, HP * q + HP), slice(2 * pair, 2 * pair + 2)
                    last = nc.scalar.copy(KB[par][rows, js, q, :],
                                          half[M6][rows, 2 * L * pair:2 * L * pair + 2 * L].rearrange(
                                              "p (j k) -> p j k", j=2))
                last.then_inc(kb_act, 1)

            def front_evac(lay, b, par, t):
                g = b + NB * lay
                if t == 0 and lay == 0 and not (isinstance(b, int) and g == 0):
                    act.wait_ge(rope_step, 7 * g - 1)
                if t == 0 and lay == 1:
                    act.wait_ge(aug_ready, g - 1)
                if t == 0 and not (isinstance(b, int) and g < 2):
                    act.wait_ge(vaug_ready, g - 1)
                act.wait_ge(proj_done, 2 * g + t + 1)
                nc.scalar.copy(qk_of(lay, par)[:, t, :], bank[M5][:, 0:2 * P])
                nc.scalar.copy(vraw[par][:, t, :], bank[M5][:, 2 * P:3 * P]).then_inc(qkv_ready, 1)

            def std(n):
                act.wait_ge(var_ready, n + 1)
                nc.scalar.activation(rstd[:, :], mv[:, :, 1], ACT.Sqrt).then_inc(std_ready, 1)
                act.wait_ge(rstd_ready, n + 1)
                for t in range(NT // 2, NT):
                    nc.scalar.activation(X[:, t, :], Y[:, t, :], ACT.Identity, bias=nmr[:, t:t + 1],
                                         scale=rstd[:, t:t + 1]).then_inc(xn_act, 1)

            def turn_evac(n):
                for c in range(0, 4, 2):
                    act.wait_ge(xt_done, 4 * n + c + 1)
                    nc.scalar.copy(XT[:, CH * c:CH * c + CH], bank[c][:, :]).then_inc(xt_ready, 1)

            def gates_evac(lay, E):
                for c in range(4):
                    act.wait_ge(gt_done, 4 * lay + c + 1)
                    nc.scalar.copy(gateT[0:E, CH * c:CH * c + CH], bank[c][0:E, :]).then_inc(gt_ready, 1)

            act_experts = [act.alloc_register(f"act_expert{i}") for i in range(4)]

            def act_slots(lay, j, s):
                kd = j + NJT[0] * lay
                if is_tile(lay, j + 1):
                    act.wait_ge(tp_done, kd + 2)
                    wait_for(act, h_done, kd)
                    nc.scalar.copy(xsT[:, (s + 1) % 2, :], bank[(s + 1) % 2][:, 0:P]).then_inc(xsT_ready, 1)
                if is_tile(lay, j):
                    act.wait_ge(h_done, kd + 1)
                    wait_for(act, eo_done, kd - 1)
                    for f in range(NF):
                        last = nc.scalar.activation(hid[:, s % 2, f, :], bank[2 + s % 2][:, P * f:P * f + P],
                                                    (ACT.Gelu_apprx_tanh, ACT.Gelu)[lay],
                                                    bias=wc[:, s, WB + f:WB + f + 1])
                    last.then_inc(gelu_done, 1)
                if is_tile(lay, j - 1):
                    q = (s - 1) % 4
                    act.wait_ge(gcol_ready, kd)
                    wait_for(act, scattered[q % 2], 8 * (kd - 1 - q % 2) - 16)
                    act.wait_ge(eo_done, kd)
                    nc.scalar.activation(yo[:, q, :], bank[4 + q % 2][:, 0:P], ACT.Copy,
                                         scale=gcol[:, q:q + 1]).then_inc(yo_ready, 1)
                if is_tile(lay, j + 2):
                    e = tile_expert(act, lay, ej_in, j + 4, s, act_experts)
                    nc.scalar.copy(wc[:, (s + 2) % 4, :], W[:, bass.ds(e, 1), 0:W2AT]).then_inc(wc_ready, 1)

            act.wait_ge(zeroed, 2)
            for lay in range(2):
                if lay == 1:
                    act.wait_ge(weights_in, 16 * N_WEIGHT)
                    lat_evac(0)
                front_evac(lay, 0, 0, 0)
                front_evac(lay, 0, 0, 1)
                if lay == 1:
                    lat_evac(1)
                front_evac(lay, 1, 1, 0)
                front_evac(lay, 1, 1, 1)
                keys_evac(lay, 0, 0, 0)
                keys_evac(lay, 0, 0, 1)
                act_iteration(lay, 0, 0, True, False, True, False)
                act_iteration(lay, 1, 1, True, True, True, False)
                with act.Fori(1, NB // 2 - 1) as ih:
                    i = 2 * ih
                    act_iteration(lay, i, 0, True, True, True, True)
                    act_iteration(lay, i + 1, 1, True, True, True, True)
                act_iteration(lay, NB - 2, 0, True, True, True, True)
                act_iteration(lay, NB - 1, 1, True, True, False, True)
                act_iteration(lay, NB, 0, False, True, False, True)
                act_iteration(lay, NB + 1, 1, False, False, False, True)
                std(2 * lay)
                turn_evac(2 * lay)
                act.wait_ge(lsh_ready, lay + 1)
                E = (E0, E1)[lay]
                nc.scalar.activation(pr[:, :, 0:E], lg[:, :, 0:E], ACT.Exp).then_inc(lexp_ready, 1)
                act.wait_ge(w_in, 48 * (E0 + E1 * lay))
                act.wait_ge(ej_ready, lay + 1)
                slot_steps(lay, act, lambda j, s: act_slots(lay, j, s))
                gates_evac(lay, E)
                std(2 * lay + 1)
                if lay == 0:
                    turn_evac(1)

        @block.vector
        def _(dve):
            steps = [0]

            def step(ins):
                steps[0] += 1
                ins.then_inc(rstep, 1)
                dve.wait_ge(rstep, steps[0])

            def dve_iteration(lay, i, par, mx_on, soft_on, front_on, tail_on):
                g = i + NB * lay
                nxt = 1 - par
                for u in range(16):
                    if mx_on:
                        qt, h = u // 8, 2 * (u % 8)
                        dve.wait_ge(s1_done, 16 * g + u + 1)
                        m_at = mx[:, qt, h:h + 2]
                        nc.vector.tensor_reduce(m_at, bank[S1B[u % 2]][:, :].rearrange("p (j k) -> p j k", j=2), AX.X,
                                                ALU.max).then_inc(s1_used, 1)
                    if u == 4 and tail_on:
                        norm(lay, i - 2, 1)
                    if u == 10 and tail_on:
                        dve.wait_ge(pj_done, g - 1)
                        at = bass.ds(2 * (i - 2), 2)
                        nc.vector.tensor_tensor(Y[:, at, :], bank[M7][:, 0:2 * P].rearrange("p (t c) -> p t c", t=2),
                                                XB[:, at, :], ALU.add).then_inc(y_ready, 1)
                    if u == 13 and front_on:
                        q_evac(lay, i + 1, nxt)
                    if u == 11 and tail_on:
                        dve.wait_ge(y_ready, g - 1)
                        for t in range(2):
                            last = nc.vector.bn_stats(stats[:, bass.ds(2 * (i - 2) + t, 1), :], Y[:, bass.ds(2 * (i - 2) + t, 1), :])
                        last.then_inc(batch_stats, 1)
                    if u == 14 and front_on:
                        keys_evac(lay, i + 1, nxt, 0)
                    if u == 15 and soft_on:
                        norm(lay, i - 1, 0)
                if mx_on:
                    dve.wait_ge(s1_used, 16 * g + 16)
                    nc.vector.tensor_scalar(mneg[:, :, :], mx[:, :, :], -1.0 / MUNIT, None, ALU.mult).then_inc(m_step, 1)
                    dve.wait_ge(m_step, 2 * g + 1)
                    nc.vector.tensor_copy(aug[par][:, :, 0:H, NROW], mneg[:, :, :]).then_inc(m_step, 1)
                    dve.wait_ge(m_step, 2 * g + 2)
                    nc.vector.tensor_tensor(aug[par][:, :, 0:H, NROW + 1], mneg[:, :, :], aug[par][:, :, 0:H, NROW],
                                            ALU.subtract).then_inc(m_ready, 1)
                if front_on:
                    keys_evac(lay, i + 1, nxt, 1)

            def keys_evac(lay, b, par, pair):
                g = b + NB * lay
                dve.wait_ge(tk_done, g + 1)
                if not (isinstance(b, int) and g < 2):
                    dve.wait_ge(st_done, 16 * (g - 2) + 8 * pair + 8)
                for q in range(2, 4):
                    rows, js = slice(HP * q, HP * q + HP), slice(2 * pair, 2 * pair + 2)
                    last = nc.vector.tensor_copy(KB[par][rows, js, q, :],
                                                 half[M6][rows, 2 * L * pair:2 * L * pair + 2 * L].rearrange(
                                                     "p (j k) -> p j k", j=2))
                last.then_inc(kb_dve, 1)

            def q_evac(lay, b, par):
                g = b + NB * lay
                dve.wait_ge(tq_done, g + 1)
                if not (isinstance(b, int) and g < 2):
                    dve.wait_ge(s1_done, 16 * (g - 1))
                nc.vector.tensor_copy(QT[par][:, :, :], half[M5]).then_inc(tq_ready, 1)

            def norm(lay, b, pair):
                g = b + NB * lay
                dve.wait_ge(bt_done, 2 * g + pair + 1)
                o = bank[M7][:, :].rearrange("p (h x) -> p h x", x=HP)
                nc.vector.reciprocal(rden[:, pair, :], o[:, :, HD]).then_inc(rden_ready, 1)
                dve.wait_ge(rden_ready, 2 * g + pair + 1)
                if not (isinstance(b, int) and g == 0):
                    dve.wait_ge(ox_done, g)
                for t in range(2):
                    last = nc.vector.tensor_tensor(on[:, t, 8 * pair:8 * pair + 8, :], o[:, 8 * t:8 * t + 8, 0:HD],
                                                   rden[:, pair, 8 * t:8 * t + 8].unsqueeze(2).to_broadcast([P, 8, HD]),
                                                   ALU.mult)
                last.then_inc(on_ready, 1)

            def layernorm(n, src):
                if n % 2 == 0:
                    dve.wait_ge(batch_stats, NB * (n // 2 + 1))
                else:
                    for t in range(NT):
                        last = nc.vector.bn_stats(stats[:, t, :], src[:, t, :])
                    last.then_inc(stats_ready, 1)
                    dve.wait_ge(stats_ready, n + n // 2 + 1)
                for t in range(NT):
                    last = nc.vector.bn_aggr(mv[:, t, :], stats[:, t, :])
                last.then_inc(stats_ready, 1)
                dve.wait_ge(stats_ready, (n + 1) + (n + 1) // 2)
                nc.vector.tensor_scalar(mv[:, :, 1], mv[:, :, 1], EPS, None, ALU.add).then_inc(var_ready, 1)
                dve.wait_ge(std_ready, n + 1)
                step(nc.vector.reciprocal(rstd[:, :], rstd[:, :]))
                nc.vector.scalar_tensor_tensor(out=nmr[:, :], in0=mv[:, :, 0], scalar=-1.0, in1=rstd[:, :],
                                               op0=ALU.mult, op1=ALU.mult).then_inc(rstd_ready, 1)
                dve.wait_ge(rstd_ready, n + 1)
                for t in range(NT // 2):
                    nc.vector.tensor_scalar(X[:, t, :], src[:, t, :], rstd[:, t:t + 1], nmr[:, t:t + 1], ALU.mult,
                                            ALU.add).then_inc(xn_dve, 1)

            def turn_evac(n):
                for c in range(1, 4, 2):
                    dve.wait_ge(xt_done, 4 * n + c + 1)
                    nc.vector.tensor_copy(XT[:, CH * c:CH * c + CH], bank[c][:, :]).then_inc(xt_ready, 1)

            def bc(ap, E):
                return ap.unsqueeze(2).to_broadcast([P, NT, E])

            def select_first_layer():
                E = E0
                lgv, prv, gv = lg[:, :, 0:E], pr[:, :, 0:E], gate[:, :, 0:E]
                by_e = lambda ap: ap.rearrange("p t e -> p e t")
                dve.wait_ge(lg_done, 1)
                raw = bank[5][:, 0:NT * E].rearrange("p (t e) -> p t e", e=E)
                step(nc.vector.tensor_tensor(lgv, raw, bs0[:, :].unsqueeze(1).to_broadcast([P, NT, E]), ALU.add))
                step(nc.vector.tensor_reduce(col[:, :], lgv, AX.X, ALU.max))
                nc.vector.tensor_tensor(lgv, lgv, bc(col[:, :], E), ALU.subtract).then_inc(lsh_ready, 1)
                dve.wait_ge(lexp_ready, 1)
                step(nc.vector.tensor_reduce(col2[:, :], prv, AX.X, ALU.add))
                step(nc.vector.reciprocal(col2[:, :], col2[:, :]))
                step(nc.vector.tensor_tensor(prv, prv, bc(col2[:, :], E), ALU.mult))
                step(nc.vector.memset(thr[:, :], 0.0))
                base = steps[0]
                C = 3 * E
                three = lambda ap: ap.rearrange("p (c e) -> p c e", e=E)
                with dve.Fori(0, NBITS // 2 // 3) as it:
                    for u in range(3):
                        n = base + 18 * it + 6 * u
                        nc.vector.tensor_tensor(three(cand[:, :].bitcast(I32)),
                                                thr[:, :].bitcast(I32).unsqueeze(1).to_broadcast([P, 3, E]),
                                                three(bits[:, bass.ds((3 * it + u) * C, C)]),
                                                ALU.bitwise_or).then_inc(rstep, 1)
                        dve.wait_ge(rstep, n + 1)
                        nc.vector.tensor_tensor(cmp_[:, :, :].rearrange("p t (c e) -> p t c e", e=E),
                                                prv.unsqueeze(2).to_broadcast([P, NT, 3, E]),
                                                three(cand[:, :]).unsqueeze(1).to_broadcast([P, NT, 3, E]),
                                                ALU.is_ge).then_inc(rstep, 1)
                        dve.wait_ge(rstep, n + 2)
                        with nc.allow_low_precision(reason="counts up to 16"):
                            nc.vector.tensor_reduce(cnt[:, :], by_e(cmp_[:, :, :]), AX.X, ALU.add).then_inc(cnt_ready, 1)
                        dve.wait_ge(count_done, 3 * it + u + 1)
                        nc.vector.scalar_tensor_tensor(out=keep[:, :], in0=bank[6][:, 0:C], scalar=float(CAP),
                                                       in1=cand[:, :], op0=ALU.is_ge, op1=ALU.mult).then_inc(rstep, 1)
                        dve.wait_ge(rstep, n + 3)
                        nc.vector.tensor_reduce(best[:, :], keep[:, :].rearrange("p (c e) -> p e c", e=E), AX.X,
                                                ALU.max).then_inc(rstep, 1)
                        dve.wait_ge(rstep, n + 4)
                        nc.vector.tensor_tensor(thr[:, :], thr[:, :], best[:, :], ALU.max).then_inc(rstep, 2)
                        dve.wait_ge(rstep, n + 6)
                steps[0] = base + 3 * NBITS
                tb = thr[:, :].unsqueeze(1).to_broadcast([P, NT, E])
                step(nc.vector.tensor_tensor(gtm[:, :, 0:E], prv, tb, ALU.is_gt))
                step(nc.vector.tensor_tensor(eqm[:, :, 0:E], prv, tb, ALU.is_equal))
                with nc.allow_low_precision(reason="counts up to 16"):
                    nc.vector.tensor_reduce(cnt[:, 0:E], by_e(gtm[:, :, 0:E]), AX.X, ALU.add).then_inc(cnt_ready, 1)
                step(nc.vector.tensor_copy(eqb[:, :, :], eqm[:, :, 0:E]))
                step(nc.vector.memset(cum[0][:, 0:1, 0:E], 0.0))
                step(nc.vector.tensor_copy(cum[0][:, 1:NT, 0:E], eqm[:, 0:NT - 1, 0:E]))
                a, sh = 0, 1
                while sh < NT:
                    step(nc.vector.tensor_copy(cum[1 - a][:, 0:sh, 0:E], cum[a][:, 0:sh, 0:E]))
                    step(nc.vector.tensor_tensor(cum[1 - a][:, sh:NT, 0:E], cum[a][:, sh:NT, 0:E],
                                                 cum[a][:, 0:NT - sh, 0:E], ALU.add))
                    a, sh = 1 - a, 2 * sh
                nc.vector.tensor_copy(cumb[:, :, :], cum[a][:, :, 0:E]).then_inc(tie_ready, 1)
                dve.wait_ge(count_done, NBITS // 2 + 1)
                step(nc.vector.tensor_scalar(need[:, :], bank[6][:, 0:E], -1.0, float(CAP), ALU.mult, ALU.add))
                dve.wait_ge(rank_done, 1)
                rank = bank[7][:, 0:NT * E].rearrange("p (t e) -> p t e", e=E)
                step(nc.vector.tensor_tensor(cmp_[:, :, 0:E], rank, need[:, :].unsqueeze(1).to_broadcast([P, NT, E]),
                                             ALU.is_le))
                step(nc.vector.tensor_tensor(cmp_[:, :, 0:E], cmp_[:, :, 0:E], eqm[:, :, 0:E], ALU.mult))
                step(nc.vector.tensor_tensor(gtm[:, :, 0:E], gtm[:, :, 0:E], cmp_[:, :, 0:E], ALU.add))
                nc.vector.tensor_copy(selz[:, 1:1 + E * NT].rearrange("p (e t) -> p e t", t=NT),
                                      by_e(gtm[:, :, 0:E])).then_inc(sel_ready, 1)
                nc.vector.tensor_tensor(gv, gtm[:, :, 0:E], prv, ALU.mult).then_inc(gate_ready, 1)

            def select_second_layer():
                E = E1
                dve.wait_ge(xsq_ready, 1)
                step(nc.vector.tensor_reduce(xn2[:, :], xsq[:, :, :], AX.X, ALU.add))
                dve.wait_ge(lg_done, 2)
                raw = bank[5][:, 0:NT * E].rearrange("p (t e) -> p t e", e=E)
                step(nc.vector.tensor_tensor(cum[0][:, :, :], raw, br1[:, :].unsqueeze(1).to_broadcast([P, NT, E]),
                                             ALU.add))
                step(nc.vector.tensor_tensor(cum[0][:, :, :], cum[0][:, :, :], bc(xn2[:, :], E), ALU.subtract))
                for t in range(NT):
                    last = nc.vector.max(top8[:, t, :], cum[0][:, t, :])
                step(last)
                nc.vector.tensor_tensor(lg[:, :, :], cum[0][:, :, :], bc(top8[:, :, 0], E),
                                        ALU.subtract).then_inc(lsh_ready, 1)
                step(nc.vector.tensor_tensor(gtm[:, :, :], cum[0][:, :, :], bc(top8[:, :, TOPK - 1], E), ALU.is_gt))
                step(nc.vector.tensor_tensor(eqm[:, :, :], cum[0][:, :, :], bc(top8[:, :, TOPK - 1], E), ALU.is_equal))
                step(nc.vector.tensor_reduce(col[:, :], gtm[:, :, :], AX.X, ALU.add))
                step(nc.vector.tensor_scalar(col[:, :], col[:, :], -1.0, float(TOPK), ALU.mult, ALU.add))
                step(nc.vector.tensor_copy(cum[0][:, :, :], eqm[:, :, :]))
                a, sh = 0, 1
                while sh < E:
                    step(nc.vector.tensor_copy(cum[1 - a][:, :, 0:sh], cum[a][:, :, 0:sh]))
                    step(nc.vector.tensor_tensor(cum[1 - a][:, :, sh:E], cum[a][:, :, sh:E], cum[a][:, :, 0:E - sh],
                                                 ALU.add))
                    a, sh = 1 - a, 2 * sh
                step(nc.vector.tensor_tensor(cum[1 - a][:, :, :], cum[a][:, :, :], bc(col[:, :], E), ALU.is_le))
                step(nc.vector.tensor_tensor(eqm[:, :, :], eqm[:, :, :], cum[1 - a][:, :, :], ALU.mult))
                step(nc.vector.tensor_tensor(gtm[:, :, :], gtm[:, :, :], eqm[:, :, :], ALU.add))
                nc.vector.tensor_copy(selz[:, 1:1 + E * NT].rearrange("p (e t) -> p e t", t=NT),
                                      gtm[:, :, :].rearrange("p t e -> p e t")).then_inc(sel_ready, 1)
                dve.wait_ge(sel_ready, 2)
                dve.wait_ge(lexp_ready, 2)
                step(nc.vector.tensor_tensor(gtm[:, :, :], gtm[:, :, :], pr[:, :, :], ALU.mult))
                step(nc.vector.tensor_reduce(col2[:, :], gtm[:, :, :], AX.X, ALU.add))
                step(nc.vector.reciprocal(col2[:, :], col2[:, :]))
                nc.vector.tensor_tensor(gate[:, :, :], gtm[:, :, :], bc(col2[:, :], E), ALU.mult).then_inc(gate_ready, 1)

            def sums(lay):
                dve.wait_ge(xs_in[lay], 32)
                for c in range(4):
                    dve.wait_ge(gb_done, 4 * lay + c + 1)
                    nc.vector.tensor_tensor(X[:, 4 * c:4 * c + 4, :], bank[c][:, :].rearrange("p (t c) -> p t c", c=P),
                                            X[:, 4 * c:4 * c + 4, :], ALU.add).then_inc(biased, 1)
                dve.wait_ge(biased, 4 * lay + 4)

            def slot_table(lay):
                K, J = KT[lay], NJT[lay]
                dve.wait_ge(rh_done, lay + 1)
                for k in range(K):
                    last = nc.vector.tensor_copy(nrow[:, k:k + 1], bank[4 + k][:, P:P + 1])
                last.then_inc(nrow_ready, 1)
                dve.wait_ge(ne_done, lay + 1)
                step(nc.vector.tensor_scalar(padf[:, 0:K], bank[6][:, 0:K], -1.0, float(TOK), ALU.mult, ALU.add))
                step(nc.vector.tensor_copy(padi[:, 0:K], padf[:, 0:K]))
                step(nc.vector.tensor_scalar(padi[:, 0:K], padi[:, 0:K], P - 1, None, ALU.bitwise_and))
                nc.vector.tensor_copy(padb[:, 0:K], padi[:, 0:K]).then_inc(pad_ready, 1)
                dve.wait_ge(lo_done, lay + 1)
                nc.vector.tensor_copy(lo[:, 0:K], bank[6][:, 8:8 + K])
                step(nc.vector.tensor_copy(padp[:, 0:K], bank[6][:, 16:16 + K]))
                step(nc.vector.tensor_tensor(lom[:, 0:K, 0:J], lo[:, 0:K].unsqueeze(2).to_broadcast([P, K, J]),
                                             tile_at[:, 0:J].unsqueeze(1).to_broadcast([P, K, J]), ALU.subtract))
                nc.vector.tensor_scalar(indj[:, 0:K, 0:J], lom[:, 0:K, 0:J], 0.0, None, ALU.is_le).then_inc(indj_ready, 1)
                for k in range(K):
                    nc.vector.tensor_scalar(RH[:, k, 0:P], bank[4 + k][:, 0:P], padp[:, k:k + 1], None, ALU.add)
                step(nc.vector.tensor_copy(RH[:, 0:K, P], dtok[:, 0:K]))
                dve.wait_ge(ej_done, lay + 1)
                nc.vector.tensor_copy(ej_in[:, 2:2 + J], bank[6][:, P:P + J])
                nc.vector.tensor_copy(ej_gate[:, 0:J], bank[6][:, P:P + J])
                nc.vector.tensor_copy(ej_out[:, 1:1 + J], bank[6][:, P:P + J]).then_inc(ej_ready, 1)
                dve.wait_ge(ej_ready, lay + 1)

            dve_experts = [dve.alloc_register(f"dve_expert{i}") for i in range(4)]

            def dve_slots(lay, j, s):
                kd = j + NJT[0] * lay
                E = (E0, E1)[lay]
                if is_tile(lay, j + AHEAD):
                    q = (s + AHEAD) % 2
                    wait_for(dve, list_done, kd + AHEAD - 1)
                    for k in range(KT[lay]):
                        last = nc.vector.tensor_scalar(ind[:, q, k, :], slot_in[:, :],
                                                       lom[:, k, bass.ds(j + AHEAD, 1)], None, ALU.is_ge)
                    last.then_inc(ind_ready, 1)
                if is_tile(lay, j):
                    e = tile_expert(dve, lay, ej_gate, j, s, dve_experts)
                    dve.wait_ge(gathered[s], 4 * (kd - s) + 16)
                    wait_for(dve, yo_ready, kd - 3)
                    nc.vector.tensor_copy(gcol[:, s:s + 1], xg[:, s, bass.ds(e + P, 1)]).then_inc(gcol_ready, 1)
                if is_tile(lay, j + AHEAD):
                    q, at = (s + AHEAD) % 2, bass.ds(j + AHEAD, 1)
                    k2 = 2 * (kd + AHEAD)
                    dve.wait_ge(list_done, kd + AHEAD + 1)
                    nc.vector.tensor_scalar(hit[:, q, :], bank[6 + q][:, 0:P], slot_at[:, at], bank[6 + q][:, P:P + 1],
                                            ALU.is_le, ALU.add, accum_out=tok[:, q, :]).then_inc(lstep, 1)
                    dve.wait_ge(lstep, k2 + 1)
                    nc.vector.scalar_tensor_tensor(out=tpad[:, q, :], in0=tok[:, q, :], scalar=float(DUMMY),
                                                   in1=pcol[:, :], op0=ALU.is_ge, op1=ALU.mult).then_inc(lstep, 1)
                    dve.wait_ge(lstep, k2 + 2)
                    nc.vector.tensor_tensor(idx_all[:, at], tok[:, q, :], tpad[:, q, :], ALU.add)
                    nc.vector.tensor_tensor(idx_g[:, (s + AHEAD) % 4:(s + AHEAD) % 4 + 1], tok[:, q, :], tpad[:, q, :],
                                            ALU.add).then_inc(idx_ready, 1)
                if is_tile(lay, j - 1):
                    wait_for(dve, scattered[(s - 1) % 2], 8 * (kd - 1 - (s - 1) % 2) - 16)
                    nc.vector.tensor_copy(idx_s[:, (s - 1) % 4:(s - 1) % 4 + 1],
                                          idx_all[:, bass.ds(j - 1, 1)]).then_inc(idx_s_ready, 1)

            nc.vector.memset(selz[:, 0:1], 0.0)
            nc.vector.memset(latT[LAT:LAT + 1, :], 1.0).then_inc(zeroed, 1)
            dve.wait_ge(first_in, 16 * N_FIRST)
            dve.wait_ge(zeroed, 2)
            def bias_next(ins, n):
                ins.then_inc(bias_step, 1)
                dve.wait_ge(bias_step, n)

            bias_next(nc.vector.tensor_copy(bpart[0][:, :], braw[:, :]), 1)
            bias_next(nc.vector.tensor_tensor(brest[:, :], braw[:, :], bpart[0][:, :], ALU.subtract), 2)
            bias_next(nc.vector.tensor_copy(bpart[1][:, :], brest[:, :]), 3)
            bias_next(nc.vector.tensor_tensor(bpart[2][:, :], brest[:, :], bpart[1][:, :], ALU.subtract), 4)
            bias_next(nc.vector.tensor_scalar(brest[:, :], bpart[0][:, :], ident[0:3, 0:1], None, ALU.mult), 5)
            for r in range(1, 3):
                out = bsplit if r == 2 else brest
                bias_next(nc.vector.scalar_tensor_tensor(out=out[:, :], in0=bpart[r][:, :], scalar=ident[0:3, r:r + 1],
                                                         in1=brest[:, :], op0=ALU.mult, op1=ALU.add), 5 + r)
            for lay in range(2):
                if lay == 0:
                    rope(dve, lay, 0, 0)
                build_aug(dve, lay, 0, 0)
                q_evac(lay, 0, 0)
                keys_evac(lay, 0, 0, 0)
                keys_evac(lay, 0, 0, 1)
                dve.wait_ge(xb_ready, lay + 1)
                dve_iteration(lay, 0, 0, True, False, True, False)
                dve_iteration(lay, 1, 1, True, True, True, False)
                with dve.Fori(1, NB // 2 - 1) as ih:
                    i = 2 * ih
                    dve_iteration(lay, i, 0, True, True, True, True)
                    dve_iteration(lay, i + 1, 1, True, True, True, True)
                dve_iteration(lay, NB - 2, 0, True, True, True, True)
                dve_iteration(lay, NB - 1, 1, True, True, False, True)
                dve_iteration(lay, NB, 0, False, True, False, True)
                dve_iteration(lay, NB + 1, 1, False, False, False, True)
                dve.wait_ge(y_ready, NB * (lay + 1))
                if lay == 0:
                    dve.wait_ge(weights_in, 16 * N_WEIGHT)
                    dve.wait_ge(consts_in, 16 * N_CONST)
                else:
                    nc.vector.tensor_tensor(ksq[:, :], keysT[:, :], keysT[:, :], ALU.mult).then_inc(wr_ready, 1)
                    nc.vector.scalar_tensor_tensor(out=wr1[:, :], in0=keysT[:, :], scalar=2.0, in1=rwT[:, :],
                                                   op0=ALU.mult, op1=ALU.add).then_inc(wr_ready, 1)
                layernorm(2 * lay, Y)
                turn_evac(2 * lay)
                if lay == 0:
                    select_first_layer()
                else:
                    dve.wait_ge(ksq_done, 1)
                    step(nc.vector.tensor_tensor(br1[:, :], rb[:, :], bank[6][:, 0:E1], ALU.subtract))
                    select_second_layer()
                slot_table(lay)
                slot_steps(lay, dve, lambda j, s: dve_slots(lay, j, s))
                sums(lay)
                dve.wait_ge(back_in[0], 16 * (lay + 1))
                step(nc.vector.tensor_tensor(X[:, :, :], X[:, :, :], Y[:, :, :], ALU.add))
                dve.wait_ge(back_in[1], 16 * (lay + 1))
                step(nc.vector.tensor_tensor(Y[:, :, :], X[:, :, :], XB[:, :, :], ALU.add))
                layernorm(2 * lay + 1, Y)
                if lay == 0:
                    turn_evac(1)


def shape_constants():
    inv = (np.float32(1.0) / np.float32(10000.0) ** (np.arange(0, HD, 2, dtype=np.float32) / np.float32(HD))).astype(np.float32)
    ang = np.arange(L, dtype=np.float32)[:, None] * inv[None, :]
    cos, sin = np.cos(ang).astype(np.float32), np.sin(ang).astype(np.float32)
    lay = lambda a: np.ascontiguousarray(a.reshape(2, P, HD).transpose(1, 0, 2))
    low = 1 << np.arange(NBITS - 2, -1, -2)
    bit = np.stack([low, 2 * low, 3 * low], 1).reshape(-1).astype(np.int32)
    wide = lambda v: np.tile(v.astype(np.float32)[None, :], (P, 1))
    rows = np.arange(E1 * NT)
    first = (rows % NT == 0) & (rows > 0)
    return {
        "c_ident": np.eye(P, dtype=np.float32),
        "c_ident_h": np.eye(P, dtype=np.float16),
        "c_slot_in": wide(np.arange(P)).astype(np.float16),
        "c_tile_at": wide(P * np.arange(NJT[1])),
        "c_slot_at": wide(P * np.arange(NJT[1])) + np.arange(P, dtype=np.float32)[:, None],
        "c_pcol": np.arange(P, dtype=np.float32)[:, None],
        "c_dtok": np.ascontiguousarray(np.where(first, -P * (NT - 1), np.where(rows > 0, P, 0)).astype(np.float32).reshape(2, P).T),
        "c_dexp": np.ascontiguousarray(np.repeat(first.astype(np.float16).reshape(2, P).T[:, :, None], P, axis=2)),
        "c_bits": np.tile(np.repeat(bit, E0)[None, :], (P, 1)),
        "c_ropec": lay(np.concatenate([cos, cos], 1)),
        "c_ropes": lay(np.concatenate([-sin, sin], 1)),
    }


def kernel(**inputs):
    import ml_dtypes
    import concourse.bacc as _bacc
    from concourse.bass_utils import run_bass_kernel_spmd as _run

    a = {k: np.asarray(v) for k, v in inputs.items()}
    x = a["L0_attn_x"].reshape(TOK, P)
    row = lambda v: v.reshape(1, -1)
    arrays = {
        "x": x, "xT": x.T,
        "wqkv0": np.concatenate([a["L0_attn_Wq"].T, a["L0_attn_Wk"].T, a["L0_attn_Wv"].T], 1),
        "braw": np.repeat(row(np.concatenate([a["L0_attn_bq"], a["L0_attn_bk"], a["L0_attn_bv"], a["L1_attn_bq"]])),
                          3, axis=0),
        "wo0": a["L0_attn_Wo"].T, "bo0": row(a["L0_attn_bo"]),
        "wo1": a["L1_attn_Wo"], "bo1": row(a["L1_attn_bo"]),
        "wq1": a["L1_attn_Wq"],
        "wl1": a["L1_attn_Wl"], "bl1": a["L1_attn_bl"].reshape(LAT, 1),
        "wkv1": np.concatenate([np.concatenate([a["L1_attn_Wk"], a["L1_attn_Wv"]], 1),
                                row(np.concatenate([a["L1_attn_bk"], a["L1_attn_bv"]]))], 0),
        "ws0": a["L0_ffn_Ws"], "bs0": row(a["L0_ffn_bs"]),
        "keysT": a["L1_ffn_keys"].T, "rwT": a["L1_ffn_rw"].T, "rb": row(a["L1_ffn_rb"]),
        "w1_0": a["L0_ffn_W1"], "w2_0": a["L0_ffn_W2"],
        "w1_1": a["L1_ffn_w1"].transpose(0, 2, 1), "w2_1": a["L1_ffn_w2"].transpose(0, 2, 1),
        "b1_0": a["L0_ffn_b1"].reshape(E0, NF, P).transpose(0, 2, 1),
        "b1_1": a["L1_ffn_b1"].reshape(E1, NF, P).transpose(0, 2, 1),
        "b2_0": a["L0_ffn_b2"], "b2_1": a["L1_ffn_b2"],
    }
    arrays = {k: np.ascontiguousarray(v) for k, v in arrays.items()}
    consts = shape_constants()
    k, r = np.arange(P)[:, None], np.arange(P)[None, :]
    zero, one = np.zeros((P, 1)), np.ones((P, 1))
    flags = {
        "tri": k <= r, "triX": np.concatenate([k <= r, one], 1), "triC": np.concatenate([k > r, zero], 1),
        "same_e": k // NT == r // NT, "before": k < r, "pad_before": (k % NT == 0) & (k // NT < r // NT),
        "first_row": (k % NT == 0) & (r >= 0), "shift": (k == r - 1) & (r % NT == 0), "cross": (k == P - 1) & (r == 0),
    }
    for name, v in flags.items():
        consts["c_" + name] = v.astype(ml_dtypes.bfloat16)
    arrays.update(consts)
    nc = _bacc.Bacc("TRN2", target_bir_lowering=False, num_devices=1)
    d = {}
    for name, v in arrays.items():
        d[name] = nc.dram_tensor("in_" + name, v.shape, mybir.dt.from_np(v.dtype), kind="ExternalInput").ap()
    for lay, E in ((0, E0), (1, E1)):
        d[f"xs{lay}"] = nc.dram_tensor(f"xs{lay}", (ROWS, P + E), F32, kind="Internal").ap()
        for par in range(2):
            d[f"sum{lay}{par}"] = nc.dram_tensor(f"sum{lay}{par}", (ROWS, P), F32, kind="Internal").ap()
    d["out"] = nc.dram_tensor("out", (TOK, P), F32, kind="ExternalOutput").ap()
    program(nc, d)
    r = _run(nc, [{"in_" + k: v for k, v in arrays.items()}], core_ids=[0])
    return np.asarray(r.results[0]["out"]).reshape(NB, L, P)
```
